# Optimizing a Trainium2 kernel written in Bass

```python
import numpy as np
import jax
import jax.numpy as jnp

def _softmax(x, axis=-1):
    return jax.nn.softmax(x, axis=axis)

def _gelu(x):
    return jax.nn.gelu(x, approximate=True)

def _silu(x):
    return jax.nn.silu(x)

def _sigmoid(x):
    return jax.nn.sigmoid(x)

def _layernorm(x, axis=-1, eps=1e-05):
    m = jnp.mean(x, axis=axis, keepdims=True)
    v = jnp.var(x, axis=axis, keepdims=True)
    return (x - m) / jnp.sqrt(v + eps)

def _scatter_add(tgt, idx, src, axis=0):
    return tgt.at[idx].add(src)

def _segment_sum(src, seg, n):
    return jax.ops.segment_sum(src, seg, n)
kernel_name = 'mk_recurrent_d1_jaxref_r4_a24a5a'

def setup_inputs(seed: int=0):
    np.random.seed(seed)
    _w = jnp.asarray

    def _L0_attn_setup():
        import jax, jax.numpy as jnp
        import numpy as np
        B, S, D, H = (4, 1024, 256, 16)
        DH = D // H
        key = jax.random.key(seed)
        ks = jax.random.split(key, 6)
        std = 0.02
        return {'hidden_states': jax.random.normal(ks[0], (B, S, D), jnp.float32), 'Wq': jax.random.normal(ks[1], (D, D), jnp.float32) * std, 'bq': jnp.zeros((D,), jnp.float32), 'Wqa': jax.random.normal(ks[2], (D, H), jnp.float32) * std, 'bqa': jnp.zeros((H,), jnp.float32), 'Wk': jax.random.normal(ks[3], (D, D), jnp.float32) * std, 'bk': jnp.zeros((D,), jnp.float32), 'Wka': jax.random.normal(ks[4], (D, H), jnp.float32) * std, 'bka': jnp.zeros((H,), jnp.float32), 'Wt': jax.random.normal(ks[5], (D, D), jnp.float32) * std, 'bt': jnp.zeros((D,), jnp.float32)}
    _L0_attn_in = _L0_attn_setup()

    def _L0_ffn_setup():
        import jax, jax.numpy as jnp
        import numpy as np
        B, S, H, F, E, K = (2, 256, 256, 512, 8, 2)
        key = jax.random.key(seed)
        ks = jax.random.split(key, 5)
        scale_h = 1.0 / np.sqrt(H)
        scale_f = 1.0 / np.sqrt(F)
        return {'inputs': jax.random.normal(ks[0], (B, S, H), dtype=jnp.float32), 'router_w': jax.random.normal(ks[1], (H, E), dtype=jnp.float32) * scale_h, 'w1': jax.random.normal(ks[2], (E, H, F), dtype=jnp.float32) * scale_h, 'w3': jax.random.normal(ks[3], (E, H, F), dtype=jnp.float32) * scale_h, 'w2': jax.random.normal(ks[4], (E, F, H), dtype=jnp.float32) * scale_f}
    _L0_ffn_in = _L0_ffn_setup()
    _d = {'L0_attn_hidden_states': _L0_attn_in['hidden_states'], 'L0_attn_Wq': _L0_attn_in['Wq'], 'L0_attn_bq': _L0_attn_in['bq'], 'L0_attn_Wqa': _L0_attn_in['Wqa'], 'L0_attn_bqa': _L0_attn_in['bqa'], 'L0_attn_Wk': _L0_attn_in['Wk'], 'L0_attn_bk': _L0_attn_in['bk'], 'L0_attn_Wka': _L0_attn_in['Wka'], 'L0_attn_bka': _L0_attn_in['bka'], 'L0_attn_Wt': _L0_attn_in['Wt'], 'L0_attn_bt': _L0_attn_in['bt'], 'L0_ffn_router_w': _L0_ffn_in['router_w'], 'L0_ffn_w1': _L0_ffn_in['w1'], 'L0_ffn_w3': _L0_ffn_in['w3'], 'L0_ffn_w2': _L0_ffn_in['w2']}
    _x0 = _d['L0_attn_hidden_states']
    _d['L0_attn_hidden_states'] = jax.random.normal(jax.random.fold_in(jax.random.key(seed), 1), (8, 1024, 256), dtype=_x0.dtype)
    del _x0
    return _d

def reference(L0_attn_hidden_states, L0_attn_Wq, L0_attn_bq, L0_attn_Wqa, L0_attn_bqa, L0_attn_Wk, L0_attn_bk, L0_attn_Wka, L0_attn_bka, L0_attn_Wt, L0_attn_bt, L0_ffn_router_w, L0_ffn_w1, L0_ffn_w3, L0_ffn_w2):

    def _L0_attn_ref(hidden_states, Wq, bq, Wqa, bqa, Wk, bk, Wka, bka, Wt, bt):
        import jax, jax.numpy as jnp
        import numpy as np
        B, S, D, H = (4, 1024, 256, 16)
        DH = D // H
        b, s, dm = hidden_states.shape
        h = bqa.shape[0]
        dh = dm // h
        scale = 1.0 / np.sqrt(dh)
        mixed_q = hidden_states @ Wq + bq
        mixed_k = hidden_states @ Wk + bk
        q_score = (mixed_q @ Wqa + bqa) * scale
        q_w = jax.nn.softmax(q_score, axis=1)
        pooled_q = jnp.einsum('bsh,bshd->bhd', q_w, mixed_q.reshape(b, s, h, dh))
        pooled_q = pooled_q.reshape(b, 1, dm)
        mixed_qk = mixed_k * pooled_q
        k_score = (mixed_qk @ Wka + bka) * scale
        k_w = jax.nn.softmax(k_score, axis=1)
        pooled_k = jnp.einsum('bsh,bshd->bhd', k_w, mixed_qk.reshape(b, s, h, dh))
        wv = pooled_k[:, None, :, :] * mixed_q.reshape(b, s, h, dh)
        wv = wv.reshape(b, s, dm)
        return wv @ Wt + bt + mixed_q

    def _L0_ffn_ref(inputs, router_w, w1, w3, w2):
        import jax, jax.numpy as jnp
        import numpy as np
        B, S, H, F, E, K = (2, 256, 256, 512, 8, 2)
        b, s, h = inputs.shape
        x = inputs.reshape(-1, h)
        logits = x @ router_w
        top_vals, top_idx = jax.lax.top_k(logits, K)
        importance = jax.nn.softmax(top_vals.astype(jnp.float32), axis=-1).astype(x.dtype)
        one_hot = top_idx[..., None] == jnp.arange(E)[None, None, :]
        combine = jnp.sum(jnp.where(one_hot, importance[..., None], 0.0), axis=1)
        gate = jax.nn.silu(jnp.einsum('th,ehf->etf', x, w1))
        up = jnp.einsum('th,ehf->etf', x, w3)
        expert_out = jnp.einsum('etf,efh->eth', gate * up, w2)
        out = jnp.einsum('te,eth->th', combine, expert_out)
        return out.reshape(b, s, h)
    x = L0_attn_hidden_states
    xn = _layernorm(x, axis=-1)
    s = _L0_attn_ref(xn, L0_attn_Wq, L0_attn_bq, L0_attn_Wqa, L0_attn_bqa, L0_attn_Wk, L0_attn_bk, L0_attn_Wka, L0_attn_bka, L0_attn_Wt, L0_attn_bt)
    g = _silu(_L0_ffn_ref(xn, L0_ffn_router_w, L0_ffn_w1, L0_ffn_w3, L0_ffn_w2))
    x = x + s * g
    return x

_drawn_inputs = setup_inputs


def setup_inputs(seed=0):
    import zlib

    import numpy as np

    out = dict(_drawn_inputs(seed))
    spreads = {'L0_attn_bq': (0.0, 0.362),
     'L0_attn_bqa': (0.0, 0.8),
     'L0_attn_bk': (0.0, 0.8),
     'L0_attn_bka': (0.0, 0.8),
     'L0_attn_bt': (0.0, 0.357)}
    factors = {'L0_attn_Wqa': 64.0, 'L0_attn_Wk': 24.831, 'L0_attn_Wka': 8.0, 'L0_attn_Wt': 8.0}
    for name, (base, spread) in spreads.items():
        noise = np.random.default_rng([zlib.crc32(name.encode()), seed]).standard_normal(out[name].shape)
        drawn = base * np.exp(spread * noise) if base else spread * noise
        out[name] = jnp.asarray(drawn.astype(out[name].dtype))
    for name, factor in factors.items():
        out[name] = (out[name] * factor).astype(out[name].dtype)
    return out
```

```python
import concourse.bass as bass
from concourse import mybir
from contextlib import ExitStack


def recurrent_attention_moe(
    nc: bass.Bass,
    x_in: bass.AP,
    Wq_in: bass.AP,
    bq_in: bass.AP,
    Wqa_in: bass.AP,
    bqa_in: bass.AP,
    Wk_in: bass.AP,
    bk_in: bass.AP,
    Wka_in: bass.AP,
    bka_in: bass.AP,
    Wt_in: bass.AP,
    bt_in: bass.AP,
    router_in: bass.AP,
    w1_in: bass.AP,
    w3_in: bass.AP,
    w2_in: bass.AP,
    out: bass.AP,
):
    fp32 = mybir.dt.float32
    fp16 = mybir.dt.float16
    i32 = mybir.dt.int32
    u32 = mybir.dt.uint32
    ALU = mybir.AluOpType
    ACT = mybir.ActivationFunctionType
    X = mybir.AxisListType.X
    ds = bass.ds

    P = 128
    B, S, D = x_in.shape
    H = bqa_in.shape[0]
    DH = D // H
    E, _, F = w1_in.shape
    T = B * S
    NT = T // P
    KC = D // P
    FC = F // P
    BT = 4
    NB = NT // BT
    GB = 4
    NG = B // GB
    BPG = NB // NG
    TPB = S // P
    HP = P // GB
    TS = 256
    SUB = TS // P
    NS = 2 * T // TS + E - 1
    NA = NS * SUB
    EPS = 1e-5
    SCALE = float(DH) ** -0.5
    XSC = 1024.0
    XSC_LOG = 10
    CH = KC * F
    assert CH == FC * D and NS % 2 == 1
    NCH = 3 * E
    LOADS = 3 + 1 + 2 * KC + 2 + 2 + 2 * GB
    FAR = -3.0e38
    RAW = 6400
    CREDIT = 2

    x_t = x_in.rearrange("b s d -> (b s) d").rearrange("(n p) d -> p n d", p=P)
    out_t = out.rearrange("b s d -> (b s) d").rearrange("(n p) d -> p n d", p=P)
    xs_dram = nc.dram_tensor("xs_dram", (T, 2 * D), fp16).ap()
    y_dram = nc.dram_tensor("y_dram", (NS * TS, D), fp32).ap()
    xs_t = xs_dram.rearrange("(n p) d -> p n d", p=P)
    y_t = y_dram.rearrange("(n p) d -> p n d", p=P)

    ctx = ExitStack()
    with ctx:
        def sb(name, shape, dt):
            return ctx.enter_context(nc.sbuf_tensor(name, shape, dt))

        def sem(name):
            return ctx.enter_context(nc.semaphore(name))

        WR = sb("weights", [P, (NCH + 1) * 2 * CH], fp16)
        XT = sb("xnT", [P, NT * KC * P], fp32)
        RA = sb("work", [P, RAW], fp32)
        Wq = sb("Wq", [P, KC, D], fp32)
        Wk = sb("Wk", [P, KC, D], fp32)
        Wt = sb("Wt", [P, KC, D], fp32)
        WqT = sb("WqT", [P, KC, D], fp32)
        WkT = sb("WkT", [P, KC, D], fp32)
        identf = sb("identf", [P, P], fp32)
        identh = sb("identh", [P, P], fp16)
        before = sb("before", [P, P], fp16)
        onesh = sb("onesh", [P, P], fp16)
        ones1 = sb("ones1", [1, P], fp32)
        headmask = sb("headmask", [P, KC, HP], fp32)
        Wqa = sb("Wqa", [P, KC, HP], fp32)
        Wka = sb("Wka", [P, KC, HP], fp32)
        rw = sb("rw", [P, KC, E], fp32)
        bcol = sb("bcol", [P, 2, KC], fp32)
        brow = sb("brow", [1, 2, D], fp32)
        sbias = sb("sbias", [P, 2], fp32)
        pooled = sb("pooled", [P, 2, KC, B], fp32)
        slotidx = sb("slotidx", [P, 2, NT], u32)
        imp = sb("imp", [P, 2, NT], fp32)
        tokidx = sb("tokidx", [P, NA], u32)
        woff = sb("woff", [P, NS], i32)
        sc = sb("sc", [P, 8], fp32)
        gcol = sb("gcol", [P, 2, 2], u32)
        small = sb("small", [P, 64], fp32)
        small_i = sb("small_i", [P, 16], i32)
        zeroh = sb("zeroh", [P, NA * 2], fp16)
        iotaA = sb("iotaA", [P, NA], fp16)
        iotaB = sb("iotaB", [P, P], fp16)
        iotaT = sb("iotaT", [P, NS], fp32)

        def view(region, at, shape, dt=fp32, per=4):
            n = 1
            for s in shape:
                n *= s
            size = {fp16: 2}.get(dt, 4)
            v = region[:, at:at + n * size // 4]
            if dt != fp32:
                v = v.bitcast(dt)
            if len(shape) == 1:
                return v
            names = "abcd"[:len(shape)]
            kw = {c: s for c, s in zip(names[1:], shape[1:])}
            return v.rearrange("p (" + " ".join(names) + ") -> p " + " ".join(names), **kw)

        def weight_view(chunk):
            return WR[:, (chunk + 1) * 2 * CH:(chunk + 2) * 2 * CH].bitcast(fp32)

        XN_SLOTS = BPG * BT * D // CH
        HEAD_SLOT = NCH + 1 - XN_SLOTS - 3
        EARLY = HEAD_SLOT - 1
        head = WR[:, HEAD_SLOT * 2 * CH:].bitcast(fp32)
        XN = head[:, 0:XN_SLOTS * CH].rearrange("p (n d) -> p n d", d=D)
        PR = head[:, XN_SLOTS * CH:(XN_SLOTS + 1) * CH]
        PT = head[:, (XN_SLOTS + 1) * CH:(XN_SLOTS + 2) * CH].rearrange("p (j c) -> p j c", c=P)
        misc = head[:, (XN_SLOTS + 2) * CH:(XN_SLOTS + 3) * CH]
        assert S == CH and TPB * P == CH and 4 * D == CH

        BW = BT * D
        XB = [view(RA, q * BW, [BT, D]) for q in range(2)]
        XS = [view(RA, 2 * BW + q * BW, [BT, 2, D], fp16) for q in range(2)]
        XTB = [view(RA, 4 * BW + q * BW, [BT, KC, P]) for q in range(2)]
        stats = [view(RA, 6 * BW + 40 * q, [BT, 6]) for q in range(2)]
        meanvar = [view(RA, 6 * BW + 40 * q + 24, [BT, 2]) for q in range(2)]
        wmax = view(RA, 6 * BW + 80, [3, E])
        pxn = view(misc, 0, [D])
        pxT = view(misc, D, [KC, P])
        WA = view(misc, 2 * D, [KC, GB, HP])
        A = view(misc, 3 * D, [KC, P])
        EJ = E * NT
        r_ = [view(RA, n * EJ, [E, NT]) for n in range(8)]
        rf = [view(RA, n * EJ, [EJ]) for n in range(8)]
        rc = [view(RA, 8 * EJ + n * NT, [NT]) for n in range(2 * E)]
        rci = [view(RA, 8 * EJ + n * NT, [NT], i32) for n in range(2 * E)]
        Mh = view(RA, 10 * EJ, [EJ], fp16)
        iotaE = view(RA, 10 * EJ + EJ // 2, [E, NT])
        notfirst = view(RA, 11 * EJ + EJ // 2, [EJ])
        oneA = [[view(RA, (2 * q + c) * NA, [2, NA], fp16) for c in range(2)] for q in range(2)]
        oneB = [[view(RA, 4 * NA + (2 * q + c) * 64, [P], fp16) for c in range(2)] for q in range(2)]
        assert 4 * NA + 256 <= 8 * EJ
        GX = [[view(RA, (2 * q + s) * D, [2, KC, P], fp16) for s in range(SUB)] for q in range(2)]
        GXf = [[view(RA, (2 * q + s) * D, [2 * D], fp16) for s in range(SUB)] for q in range(2)]
        XG = [view(RA, 4 * D + q * 2 * TS, [2, KC, TS], fp16) for q in range(2)]
        o = 4 * D + 4 * TS
        SG = view(RA, o, [FC, TS])
        HH = [view(RA, o + (1 + q) * FC * TS, [2, FC, TS], fp16) for q in range(2)]
        oy = o + 3 * FC * TS
        YB = [view(RA, oy + q * SUB * D, [SUB, D]) for q in range(2)]
        assert oy + 2 * SUB * D <= RAW
        YG = [[view(RA, (2 * q + c) * D, [D]) for c in range(2)] for q in range(2)]
        XR = [view(RA, 4 * D + q * D, [D]) for q in range(2)]
        XC = [view(RA, 6 * D + q * D, [KC, P]) for q in range(2)]
        OB = [view(RA, 8 * D + q * D, [D]) for q in range(2)]
        FF = [view(RA, 10 * D + q * D, [D]) for q in range(2)]
        SF = [view(RA, 12 * D + q * D, [D]) for q in range(2)]
        WTP = view(RA, 14 * D, [KC, D])
        WE = view(RA, 16 * D, [KC, D])
        BE = view(RA, 18 * D, [D])
        assert 19 * D <= RAW

        PS = ctx.enter_context(nc.psum_tensor("PS", [P, 8, 512], fp32))
        psT = [PS[:, 2 * q:2 * q + 2, :].rearrange("p b (u t) -> p (b u) t", t=P) for q in range(2)]
        psTf = [PS[:, 2 * q:2 * q + 2, :].rearrange("p b n -> p (b n)") for q in range(2)]
        psS = PS[:, 4:6, :]
        psX = PS[:, 6, :]
        psL = PS[:, 7, :].rearrange("p (n e) -> p n e", e=E)
        psRank = PS[:, 0, :]
        psCnt = PS[:, 1, :]
        psInv = PS[:, 2, 0:2 * NA]
        assert 2 * NA <= 512
        psGU = [PS[:, f, :].rearrange("p (m t) -> p m t", m=2) for f in range(FC)]
        psXG = PS[:, 4:6, :].bitcast(fp16).rearrange("p b (c t) -> p b c t", t=TS)
        psY = PS[:, 6:8, :].rearrange("p b (s d) -> p b s d", d=D)
        psAtt = [PS[:, q, 0:D] for q in range(2)]
        psEff = PS[:, 2, :].rearrange("p (c n) -> p c n", c=KC)
        psBe = PS[0:1, 3, 0:D]

        s_cl = sem("constants_loaded")
        s_cm = sem("constants_made")
        s_pc = sem("pool_chain")
        s_dc = sem("vector_chain")
        s_ac = sem("scalar_chain")
        s_turn = sem("pool_turn")
        s_vturn = sem("vector_turn")
        s_x = [sem(f"x_loaded{q}") for q in range(2)]
        s_var = sem("variance_ready")
        s_std = sem("std_ready")
        s_xn = sem("xn_ready")
        s_hi = sem("xn_hi_ready")
        s_lo = sem("xn_lo_ready")
        s_xsst = sem("xn_halves_stored")
        s_xsfree = sem("xn_halves_free")
        s_tr = sem("xn_transposed")
        s_xtb = sem("xnT_block_ready")
        s_rt = sem("router_done")
        s_keep = sem("xn_kept")
        s_keept = sem("xnT_kept")
        s_wT = sem("weight_transposed")
        s_wTc = sem("weight_transpose_copied")
        s_wa = sem("score_weights_scaled")
        s_A = sem("score_fold_done")
        s_Ac = sem("score_fold_copied")
        s_sc = sem("scores_done")
        s_mx = sem("score_max_ready")
        s_ex = sem("probs_ready")
        s_pt = sem("probs_transposed")
        s_ptc = sem("probs_transpose_copied")
        s_px = sem("weighted_xn_done")
        s_pxn = sem("weighted_xn_scaled")
        s_pxt = sem("weighted_xn_transposed")
        s_pxtc = sem("weighted_xn_transpose_copied")
        s_pv = sem("pooled_done")
        s_pooled = sem("pooled_ready")
        s_wl = sem("weights_loaded")
        s_amax = sem("weight_max_ready")
        s_gmax = sem("weight_max_everywhere")
        s_scale = sem("scales_ready")
        s_whi = sem("weight_hi_ready")
        s_wlo = sem("weight_lo_ready")
        s_choice = sem("choices_ready")
        s_rank = sem("ranks_done")
        s_iota = sem("iotas_ready")
        s_one = sem("one_hots_ready")
        s_inv = sem("inverse_step_done")
        s_invall = sem("inverse_done")
        s_idx = sem("indices_ready")
        s_col = sem("index_column_ready")
        s_g = [sem(f"gathered{q}") for q in range(2)]
        s_xgt = sem("gather_transposed")
        s_xg = sem("gather_transpose_copied")
        s_gu = sem("gate_up_done")
        s_sg = sem("silu_ready")
        s_h = sem("hidden_ready")
        s_hh = sem("hidden_hi_ready")
        s_hl = sem("hidden_lo_ready")
        s_y = sem("expert_out_done")
        s_yb = sem("expert_out_copied")
        s_yst = sem("expert_out_stored")
        s_yfree = sem("expert_out_free")
        s_wtp = sem("out_weights_scaled")
        s_eff = sem("out_weights_folded")
        s_we = sem("out_weights_ready")
        s_tc = sem("tail_column_ready")
        s_tg = [sem(f"tail_gathered{q}") for q in range(2)]
        s_tx = [sem(f"tail_x_loaded{q}") for q in range(2)]
        s_xc = sem("tail_xnT_ready")
        s_s = sem("attention_out_done")
        s_f = sem("ffn_out_ready")
        s_sf = sem("gate_ready")
        s_o = sem("out_ready")
        s_ost = sem("out_stored")
        s_ofree = sem("out_free")

        block = ctx.enter_context(nc.Block())

        class Chain:

            def __init__(self, eng, s):
                self.eng, self.s, self.n, self.off = eng, s, 0, None

            def __call__(self, ins):
                ins.then_inc(self.s, 1)
                self.n += 1
                self.eng.wait_ge(self.s, self.n if self.off is None else self.off + self.n)

            def enter(self, turn, steps):
                self.off, self.steps, self.at = turn * steps, steps, self.n

            def leave(self, turns):
                assert self.n - self.at == self.steps, (self.n - self.at, self.steps)
                self.n, self.off = self.at + self.steps * turns, None

        @block.sync
        def _(sp):
            for dst, src in ((Wq, Wq_in), (Wk, Wk_in), (Wt, Wt_in)):
                sp.dma_start(dst[:, :, :], src.rearrange("(c p) n -> p c n", p=P)).then_inc(s_cl, 16)
            sp.dma_start(rw[:, :, :], router_in.rearrange("(c p) n -> p c n", p=P)).then_inc(s_cl, 16)
            for m, src in enumerate((bq_in, bk_in)):
                for c in range(KC):
                    sp.dma_start(bcol[:, m, c:c + 1], src[c * P:(c + 1) * P].rearrange("(p a) -> p a", a=1)
                                 ).then_inc(s_cl, 16)
            for m, src in enumerate((bq_in, bt_in)):
                sp.dma_start(brow[0:1, m, :], src.rearrange("(a n) -> a n", a=1)).then_inc(s_cl, 16)
            sp.wait_ge(s_cm, 1)
            for dst, src in ((Wqa, Wqa_in), (Wka, Wka_in)):
                sp.dma_start(dst[:, :, 0:H], src.rearrange("(c p) n -> p c n", p=P)).then_inc(s_cl, 16)
            for m, src in enumerate((bqa_in, bka_in)):
                for b in range(GB):
                    sp.dma_start(sbias[HP * b:HP * b + H, m:m + 1],
                                 src.rearrange("(n a) -> n a", a=1)).then_inc(s_cl, 16)

            def load_block(n, q, turn, first):
                if not first:
                    sp.wait_ge(s_lo, n - 1)
                    sp.wait_ge(s_tr, n - 1)
                    sp.wait_ge(s_keep, n - 1)
                sp.dma_start(XB[q], x_t[:, ds(n * BT, BT), :] if not isinstance(n, int)
                             else x_t[:, n * BT:(n + 1) * BT, :]).then_inc(s_x[q], 16)

            load_block(0, 0, 0, True)
            load_block(1, 1, 0, True)
            with sp.Fori(1, NB // 2) as i:
                for q in range(2):
                    load_block(i * 2 + q, q, i, False)
            sp.wait_ge(s_pooled, 2 * NG)
            for c in range(EARLY, NCH):
                e, m = c // 3, c % 3
                src = (w1_in, w3_in, w2_in)[m][e].rearrange("(c p) n -> p c n", p=P)
                dst = weight_view(c).rearrange("p (c n) -> p c n", c=src.shape[1])
                sp.dma_start(dst, src).then_inc(s_wl, 16)

            ybufs = view(RA, oy, [2, SUB, D])
            with sp.Fori(0, NS) as t:
                sp.wait_ge(s_yb, t + (1 + CREDIT))
                sp.dma_start(y_t[:, ds(t * SUB, SUB), :], ybufs[:, ds(t % 2, 1), :, :]).then_inc(s_yst, 16)
                sp.wait_ge(s_yst, t * 16 + 16)
                sp.sem_inc(s_yfree, 1)

            with sp.Fori(0, NT // 2) as i:
                for q in range(2):
                    j = i * 2 + q
                    sp.wait_ge(s_o, j + (1 + CREDIT))
                    sp.dma_start(out_t[:, ds(j, 1), :], OB[q]).then_inc(s_ost, 16)
                    sp.wait_ge(s_ost, j * 16 + 16)
                    sp.sem_inc(s_ofree, 1)

        @block.gpsimd
        def _(pool):
            ch = Chain(pool, s_pc)
            g = nc.gpsimd
            g.memset(Wqa[:, :, :], 0.0)
            g.memset(Wka[:, :, :], 0.0)
            g.memset(sbias[:, :], 0.0).then_inc(s_cm, 1)
            g.memset(identf[:, :], 0.0)
            g.memset(onesh[:, :], 1.0)
            g.memset(zeroh[:, :], 0.0)
            g.memset(ones1[:, :], 1.0)
            ch(g.memset(headmask[:, :, :], 1.0))
            ch(g.affine_select(out=identf[:, :], in_=identf[:, :], compare_op=ALU.not_equal, fill=1.0,
                               base=0, pattern=[[-1, P]], channel_multiplier=1))
            ch(g.tensor_copy(identh[:, :], identf[:, :]))
            ch(g.affine_select(out=before[:, :], in_=onesh[:, :], compare_op=ALU.is_gt, fill=0.0,
                               base=0, pattern=[[1, P]], channel_multiplier=-1))
            ch(g.affine_select(out=headmask[:, :, :], in_=headmask[:, :, :], compare_op=ALU.is_ge, fill=0.0,
                               base=0, pattern=[[P, KC], [-DH, HP]], channel_multiplier=1))
            g.affine_select(out=headmask[:, :, :], in_=headmask[:, :, :], compare_op=ALU.is_ge, fill=0.0,
                            base=DH - 1, pattern=[[-P, KC], [DH, HP]], channel_multiplier=-1
                            ).then_inc(s_cm, 1)
            pool.sem_inc(s_xsfree, CREDIT)
            for s in (s_xgt, s_yb, s_yfree, s_f, s_o, s_ofree, s_inv):
                pool.sem_inc(s, CREDIT)

            for grp in range(NG):
                if grp:
                    pool.wait_ge(s_pooled, 2 * grp)
                with pool.Fori(0, BPG // 2) as i:
                    for q in range(2):
                        m = i * 2 + q
                        n = m + grp * BPG
                        pool.wait_ge(s_xn, n + 1)
                        pool.sem_inc(s_turn, 1)
                        g.tensor_copy(XN[:, ds(m * BT, BT), :], XB[q]).then_inc(s_keep, 1)
                        pool.wait_ge(s_xtb, n + 1)
                        pool.sem_inc(s_turn, 1)
                        g.tensor_copy(XT[:, ds(n * BW, BW)],
                                      XTB[q].rearrange("p u c t -> p (u c t)")).then_inc(s_keept, 1)
                        pool.wait_ge(s_lo, n + 1)
                        pool.sem_inc(s_turn, 1)
                        pool.dma_start(xs_t[:, ds(n * BT, BT), :],
                                       XS[q].rearrange("p u c d -> p u (c d)")).then_inc(s_xsst, 16)
                        pool.wait_ge(s_xsst, n * 16 + 16)
                        pool.wait_ge(s_keep, n + 1)
                        pool.wait_ge(s_keept, n + 1)
                        pool.sem_inc(s_xsfree, 1)

            pool.wait_ge(s_amax, 1)
            g.partition_all_reduce(small[:, 2:4], small[:, 0:2], P, bass.bass_isa.ReduceOp.absmax
                                   ).then_inc(s_gmax, 1)

            pool.wait_ge(s_rt, NB)
            pool.wait_ge(s_scale, 1)
            g.iota(r_[2].bitcast(i32), pattern=[[1, E], [0, NT]], base=0, channel_multiplier=0)
            g.iota(rci[15], pattern=[[1, NT]], base=0, channel_multiplier=0)
            g.iota(small_i[:, 8:9], pattern=[[0, 1]], base=0, channel_multiplier=1)
            g.iota(r_[0].rearrange("p e j -> p (e j)")[:, 0:NA].bitcast(i32), pattern=[[1, NA]], base=0,
                   channel_multiplier=0)
            ch(g.memset(notfirst, 1.0))
            g.tensor_copy(iotaE, r_[2].bitcast(i32))
            g.tensor_copy(rc[14], rci[15])
            g.tensor_copy(small[:, 8:9], small_i[:, 8:9])
            first = r_[0].rearrange("p e j -> p (e j)")[:, 0:NA].bitcast(i32)
            g.tensor_copy(iotaA[:, :], first)
            g.tensor_copy(iotaB[:, :], first[:, 0:P])
            g.tensor_copy(iotaT[:, :], first[:, 0:NS])
            g.affine_select(out=notfirst.rearrange("p (e j) -> p e j", e=E),
                            in_=notfirst.rearrange("p (e j) -> p e j", e=E),
                            compare_op=ALU.not_equal, fill=0.0, base=0,
                            pattern=[[0, E], [1, NT]], channel_multiplier=0).then_inc(s_iota, 1)

            pool.wait_ge(s_idx, 1)

            def gather(t, q):
                pool.wait_ge(s_xgt, t + 1)
                pool.sem_inc(s_turn, 1)
                for s in range(SUB):
                    col = t * SUB + s
                    src = tokidx[:, ds(col, 1)] if not isinstance(col, int) else tokidx[:, col:col + 1]
                    g.tensor_copy(gcol[:, q, s:s + 1], src).then_inc(s_col, 1)
                    pool.wait_ge(s_col, col + 1)
                    pool.sem_inc(s_turn, 1)
                    pool.indirect_dma_start(
                        out=GXf[q][s], out_offset=None, in_=xs_dram,
                        in_offset=bass.IndirectOffsetOnAxis(ap=gcol[:, q, s:s + 1], axis=0)
                    ).then_inc(s_g[q], 16)

            with pool.Fori(0, NS // 2) as i:
                gather(i * 2, 0)
                gather(i * 2 + 1, 1)
            gather(NS - 1, 0)

            pool.wait_ge(s_yst, NS * 16)
            with pool.Fori(0, NT // 2) as i:
                for q in range(2):
                    j = i * 2 + q
                    pool.wait_ge(s_f, j + 1)
                    pool.sem_inc(s_turn, 1)
                    for c in range(2):
                        g.tensor_copy(gcol[:, q, c:c + 1], slotidx[:, c, ds(j, 1)]).then_inc(s_tc, 1)
                        pool.wait_ge(s_tc, j * 2 + (c + 1))
                        pool.sem_inc(s_turn, 1)
                        pool.indirect_dma_start(
                            out=YG[q][c], out_offset=None, in_=y_dram,
                            in_offset=bass.IndirectOffsetOnAxis(ap=gcol[:, q, c:c + 1], axis=0)
                        ).then_inc(s_tg[q], 16)

        @block.scalar
        def _(act):
            a = nc.scalar
            ch = Chain(act, s_ac)
            for c in range(EARLY):
                e, m = c // 3, c % 3
                src = (w1_in, w3_in, w2_in)[m][e].rearrange("(c p) n -> p c n", p=P)
                dst = weight_view(c).rearrange("p (c n) -> p c n", c=src.shape[1])
                act.dma_start(dst, src).then_inc(s_wl, 16)
            for m, dst in enumerate((WqT, WkT)):
                act.wait_ge(s_wT, m + 1)
                a.copy(dst[:, :, :].rearrange("p c n -> p (c n)"), psTf[m][:, 0:KC * D]).then_inc(s_wTc, 1)

            def attention(n):
                act.wait_ge(s_A, n + 1)
                a.copy(A.rearrange("p c n -> p (c n)"), psX[:, 0:KC * P]).then_inc(s_Ac, 1)
                act.wait_ge(s_mx, n + 1)
                a.activation(PR, psS.rearrange("p b n -> p (b n)"), ACT.Exp,
                             bias=small[:, 4:5], scale=SCALE, accum_out=small[:, 5:6]).then_inc(s_ex, 1)
                act.wait_ge(s_pt, n + 1)
                a.copy(PT, psT[0]).then_inc(s_ptc, 1)
                act.wait_ge(s_pxt, n + 1)
                a.copy(pxT.rearrange("p c n -> p (c n)"), psX[:, 256:256 + KC * P]).then_inc(s_pxtc, 1)

            for grp in range(NG):
                act.preload_act_table(ACT.Sqrt)
                with act.Fori(0, BPG // 2) as i:
                    for q in range(2):
                        n = i * 2 + q + grp * BPG
                        act.wait_ge(s_var, n + 1)
                        a.activation(small[:, 24 + 8 * q:24 + 8 * q + BT], small[:, 16 + 8 * q:16 + 8 * q + BT],
                                     ACT.Sqrt).then_inc(s_std, 1)
                        act.wait_ge(s_xn, n + 1)
                        act.wait_ge(s_xsfree, n + 1)
                        a.activation(XS[q][:, :, 0, :], XB[q], ACT.Copy, scale=XSC).then_inc(s_hi, 1)
                        act.wait_ge(s_tr, n + 1)
                        a.copy(XTB[q].rearrange("p u c t -> p (u c) t"), psT[q]).then_inc(s_xtb, 1)
                act.preload_act_table(ACT.Exp)
                for m in range(2):
                    attention(2 * grp + m)

            act.wait_ge(s_scale, 1)
            for c in range(NCH):
                k = 1 if c % 3 == 2 else 0
                if c:
                    act.wait_ge(s_wlo, c)
                a.activation(WR[:, c * 2 * CH:c * 2 * CH + CH], weight_view(c), ACT.Copy,
                             scale=sc[:, k:k + 1]).then_inc(s_whi, 1)
            act.wait_ge(s_choice, 1)
            a.activation(rc[4], rc[3], ACT.Exp).then_inc(s_choice, 1)

            act.wait_ge(s_idx, 1)
            act.preload_act_table(ACT.Silu)

            def copy_gather(t, q):
                act.wait_ge(s_xgt, t + (1 + CREDIT))
                a.copy(XG[q].rearrange("p c k t -> p (c k t)"), psXG[:, q, :, :].rearrange("p c t -> p (c t)")
                       ).then_inc(s_xg, 1)

            def silu_hi(t, q):
                for h in range(2):
                    act.wait_ge(s_gu, t * 2 + (h + 1))
                    if not (isinstance(t, int) and t == 0):
                        act.wait_ge(s_hl, t * 2 + (h - 1))
                    a.activation(SG[:, 2 * h:2 * h + 2, :], PS[:, 2 * h:2 * h + 2, 0:TS], ACT.Silu,
                                 scale=sc[:, 2:3]).then_inc(s_sg, 1)
                for h in range(2):
                    act.wait_ge(s_h, t * 2 + (h + 1))
                    a.copy(HH[q][:, 0, 2 * h:2 * h + 2, :], SG[:, 2 * h:2 * h + 2, :]).then_inc(s_hh, 1)

            def copy_out(t, q):
                act.wait_ge(s_y, t + 1)
                act.wait_ge(s_yfree, t + 1)
                a.activation(YB[q].rearrange("p s d -> p (s d)"), psY[:, q, :, :].rearrange("p s d -> p (s d)"),
                             ACT.Copy, scale=sc[:, 7:8]).then_inc(s_yb, 1)

            copy_gather(0, 0)
            copy_gather(1, 1)
            silu_hi(0, 0)
            with act.Fori(0, (NS - 3) // 2) as i:
                for q in range(2):
                    t = i * 2 + 1 + q
                    copy_gather(t + 1, q)
                    silu_hi(t, 1 - q)
                    copy_out(t - 1, q)
            t = NS - 2
            copy_gather(t + 1, 0)
            silu_hi(t, 1)
            copy_out(t - 1, 0)
            silu_hi(t + 1, 0)
            copy_out(t, 1)
            copy_out(t + 1, 0)

            act.wait_ge(s_yst, NS * 16)

            def tail(j, q):
                act.wait_ge(s_o, j + 1)
                act.dma_start(XR[q], x_t[:, ds(j, 1), :]).then_inc(s_tx[q], 16)
                a.copy(XC[q].rearrange("p c t -> p (c t)"), XT[:, ds(j * D, D)]).then_inc(s_xc, 1)
                act.wait_ge(s_f, j + (1 + CREDIT))
                a.activation(SF[q], FF[q], ACT.Silu).then_inc(s_sf, 1)

            with act.Fori(0, NT // 2) as i:
                for q in range(2):
                    tail(i * 2 + q, q)

        @block.vector
        def _(dve):
            v = nc.vector
            ch = Chain(dve, s_dc)
            dve.wait_ge(s_cl, 16 * LOADS)
            dve.wait_ge(s_cm, 2)
            v.tensor_tensor(brow[0:1, 0, :], brow[0:1, 0, :], brow[0:1, 1, :], ALU.add)
            wqa4 = Wqa[:, :, :].rearrange("p c (a h) -> p c a h", a=1).broadcast_to([P, KC, GB, HP])
            wka4 = Wka[:, :, :].rearrange("p c (a h) -> p c a h", a=1).broadcast_to([P, KC, GB, HP])

            def attention(n):
                grp, k = n // 2, n % 2
                if not k:
                    v.tensor_copy(WA, wqa4).then_inc(s_wa, 1)
                else:
                    v.tensor_tensor(WA, wka4, pooled[:, 0, :, grp * GB:(grp + 1) * GB].rearrange("p c (b a) -> p c b a", a=1)
                                    .broadcast_to([P, KC, GB, HP]), ALU.mult).then_inc(s_wa, 1)
                dve.wait_ge(s_Ac, n + 1)
                ch(v.tensor_tensor(small[:, 6:7], psX[:, 500:501], sbias[:, k:k + 1], ALU.add))
                dve.wait_ge(s_sc, n + 1)
                ch(v.reduce_max(small[:, 7:8], psS.rearrange("p b n -> p (b n)"), X))
                ch(v.tensor_tensor(small[:, 7:8], small[:, 7:8], small[:, 6:7], ALU.add))
                ch(v.tensor_tensor(small[:, 6:7], small[:, 6:7], small[:, 7:8], ALU.subtract))
                v.tensor_scalar(small[:, 4:5], small[:, 6:7], SCALE, None, ALU.mult).then_inc(s_mx, 1)
                dve.wait_ge(s_ex, n + 1)
                ch(v.reciprocal(small[:, 5:6], small[:, 5:6]))
                dve.wait_ge(s_px, n + 1)
                v.tensor_scalar(pxn, psX[:, 0:D], small[:, 5:6], None, ALU.mult).then_inc(s_pxn, 1)
                dve.wait_ge(s_pv, n + 1)
                pv = psTf[1][:, 0:KC * P].rearrange("p (c b h) -> p c b h", c=KC, b=GB)
                own = A.rearrange("p c (b h) -> p c b h", b=GB)
                for c in range(KC):
                    mask = headmask[:, c, :].rearrange("p (a h) -> p a h", a=1).broadcast_to([P, GB, HP])
                    last = v.tensor_tensor(own[:, c], pv[:, c], mask, ALU.mult)
                ch(last)
                dst = pooled[:, k, :, grp * GB:(grp + 1) * GB]
                ch(v.tensor_reduce(dst, own, X, ALU.add))
                for c in range(KC):
                    last = v.tensor_scalar(dst[:, c, :], dst[:, c, :], bcol[:, k, c:c + 1], None, ALU.add)
                if not k:
                    last.then_inc(s_pooled, 1)
                    dve.wait_ge(s_pooled, n + 1)
                else:
                    ch(last)
                    v.tensor_tensor(dst, dst, pooled[:, 0, :, grp * GB:(grp + 1) * GB], ALU.mult).then_inc(s_pooled, 1)

            for grp in range(NG):
                with dve.Fori(0, BPG // 2) as i:
                    ch.enter(i, 2 * 6 - 0)
                    for q in range(2):
                        n = i * 2 + q + grp * BPG
                        var = small[:, 16 + 8 * q:16 + 8 * q + BT]
                        std = small[:, 24 + 8 * q:24 + 8 * q + BT]
                        tmp = small[:, 20 + 8 * q:20 + 8 * q + BT]
                        mv = meanvar[q]
                        dve.wait_ge(s_x[q], i * 16 + (16 + grp * 16 * BPG // 2))
                        for u in range(BT):
                            last = v.bn_stats(stats[q][:, u, :], XB[q][:, u, :])
                        ch(last)
                        dve.sem_inc(s_vturn, 1)
                        for u in range(BT):
                            last = v.bn_aggr(mv[:, u, :], stats[q][:, u, :])
                        ch(last)
                        v.tensor_scalar(var, mv[:, :, 1], EPS, None, ALU.add).then_inc(s_var, 1)
                        dve.wait_ge(s_std, n + 1)
                        ch(v.reciprocal(std, std))
                        ch(v.scalar_tensor_tensor(tmp, std, -0.5, std, ALU.mult, ALU.mult))
                        ch(v.tensor_tensor(tmp, tmp, var, ALU.mult))
                        ch(v.scalar_tensor_tensor(std, tmp, 1.5, std, ALU.add, ALU.mult))
                        for u in range(BT):
                            last = v.tensor_scalar(XB[q][:, u, :], XB[q][:, u, :], mv[:, u, 0:1], std[:, u:u + 1],
                                                   ALU.subtract, ALU.mult)
                        last.then_inc(s_xn, 1)
                        dve.wait_ge(s_hi, n + 1)
                        v.scalar_tensor_tensor(XS[q][:, :, 1, :], XB[q], XSC, XS[q][:, :, 0, :],
                                               ALU.mult, ALU.subtract).then_inc(s_lo, 1)
                ch.leave(BPG // 2)
                for m in range(2):
                    attention(2 * grp + m)

            dve.wait_ge(s_wl, 16 * NCH)
            for c in range(NCH):
                last = v.tensor_reduce(wmax[:, c % 3, c // 3:c // 3 + 1], weight_view(c), X, ALU.max,
                                       apply_absolute_value=True)
            ch(last)
            v.reduce_max(small[:, 0:1], wmax[:, 0:2, :].rearrange("p m e -> p (m e)"), X)
            v.reduce_max(small[:, 1:2], wmax[:, 2, :], X).then_inc(s_amax, 1)
            dve.wait_ge(s_gmax, 1)
            fe = small[:, 40:48]
            ch(v.tensor_scalar(small_i[:, 0:2], small[:, 2:4].bitcast(i32), 23, None, ALU.logical_shift_right))
            ch(v.tensor_copy(small[:, 10:12], small_i[:, 0:2]))
            v.tensor_scalar(fe[:, 0:2], small[:, 10:12], -1.0, 268.0, ALU.mult, ALU.add)
            ch(v.tensor_scalar(fe[:, 4:5], small[:, 10:11], -2.0, 378.0, ALU.mult, ALU.add))
            v.tensor_scalar(fe[:, 0:2], fe[:, 0:2], 200.0, 1.0, ALU.min, ALU.max)
            ch(v.tensor_scalar(fe[:, 4:5], fe[:, 4:5], 200.0, 1.0, ALU.min, ALU.max))
            v.tensor_scalar(fe[:, 2:3], fe[:, 0:1], -1.0, 254.0 - XSC_LOG, ALU.mult, ALU.add)
            v.tensor_scalar(fe[:, 3:4], fe[:, 1:2], -1.0, 254.0, ALU.mult, ALU.add)
            ch(v.tensor_scalar(fe[:, 5:6], fe[:, 4:5], -1.0, 254.0, ALU.mult, ALU.add))
            ch(v.tensor_copy(small_i[:, 0:6], fe[:, 0:6]))
            ch(v.tensor_scalar(sc[:, 0:6].bitcast(i32), small_i[:, 0:6], 23, None, ALU.logical_shift_left))
            v.tensor_tensor(sc[:, 6:7], sc[:, 2:3], sc[:, 4:5], ALU.mult)
            v.tensor_tensor(sc[:, 7:8], sc[:, 3:4], sc[:, 5:6], ALU.mult).then_inc(s_scale, 1)
            dve.wait_ge(s_scale, 1)
            for c in range(NCH):
                k = 1 if c % 3 == 2 else 0
                dve.wait_ge(s_whi, c + 1)
                v.scalar_tensor_tensor(WR[:, c * 2 * CH + CH:(c + 1) * 2 * CH], weight_view(c), sc[:, k:k + 1],
                                       WR[:, c * 2 * CH:c * 2 * CH + CH], ALU.mult, ALU.subtract
                                       ).then_inc(s_wlo, 1)

            L, eq, cand, oh1, oh2, slot, cum, cnt = r_[0:8]

            def over_e(ap):
                return ap.rearrange("p e j -> p j e")

            def each_e(ap):
                return ap.rearrange("p (a j) -> p a j", a=1).broadcast_to([P, E, NT])

            dve.wait_ge(s_iota, 1)
            dve.wait_ge(s_rt, NB)
            ch(v.tensor_copy(L, psL.rearrange("p j e -> p e j")))

            def choose(top, oh):
                ch(v.reduce_max(top, over_e(L), X))
                ch(v.tensor_tensor(eq, L, each_e(top), ALU.is_equal))
                ch(v.scalar_tensor_tensor(cand, eq, -float(E), iotaE, ALU.mult, ALU.add))
                ch(v.tensor_reduce(rc[2], over_e(cand), X, ALU.min))
                ch(v.tensor_scalar(rc[2], rc[2], float(E), None, ALU.add))
                ch(v.tensor_tensor(oh, iotaE, each_e(rc[2]), ALU.is_equal))

            choose(rc[0], oh1)
            ch(v.scalar_tensor_tensor(L, oh1, FAR, L, ALU.mult, ALU.add))
            choose(rc[1], oh2)
            v.tensor_tensor(rc[3], rc[1], rc[0], ALU.subtract).then_inc(s_choice, 1)
            v.tensor_tensor(Mh.rearrange("p (e j) -> p e j", e=E), oh1, oh2, ALU.add).then_inc(s_rank, 1)
            dve.wait_ge(s_choice, 2)
            ch(v.tensor_scalar(rc[5], rc[4], 1.0, None, ALU.add))
            ch(v.reciprocal(imp[:, 0, :], rc[5]))
            v.tensor_tensor(imp[:, 1, :], imp[:, 0, :], rc[4], ALU.mult)
            dve.wait_ge(s_rank, 2)
            ch(v.tensor_copy(cnt, psCnt.rearrange("p (e j) -> p e j", e=E)))
            ch(v.tensor_tensor_scan(rf[6], notfirst, rf[7], 0.0, ALU.mult, ALU.add))
            n_t = small[:, 48:56]
            ends = small[:, 56:64]
            ch(v.tensor_scalar(small_i[:, 0:E], cum[:, :, NT - 1], float(TS - 1), None, ALU.add))
            ch(v.tensor_scalar(small_i[:, 0:E], small_i[:, 0:E], TS.bit_length() - 1, None,
                               ALU.logical_shift_right))
            ch(v.tensor_copy(n_t, small_i[:, 0:E]))
            ch(v.memset(small[:, 32:40], 1.0))
            ch(v.tensor_tensor_scan(ends, small[:, 32:40], n_t, 0.0, ALU.mult, ALU.add))
            ch(v.tensor_tensor(n_t, ends, n_t, ALU.subtract))
            ch(v.tensor_scalar(n_t, n_t, float(TS), None, ALU.mult))
            ch(v.tensor_tensor(cum, cum, cnt, ALU.subtract))
            ch(v.tensor_tensor(slot, cum, psRank.rearrange("p (e j) -> p e j", e=E), ALU.add))
            ch(v.tensor_tensor(slot, slot, n_t.rearrange("p (e a) -> p e a", a=1).broadcast_to([P, E, NT]),
                               ALU.add))
            for c, oh in enumerate((oh1, oh2)):
                ch(v.tensor_tensor(eq, oh, slot, ALU.mult))
                ch(v.tensor_reduce(rc[6 + c], over_e(eq), X, ALU.add))
                ch(v.tensor_copy(slotidx[:, c, :], rc[6 + c]))
                si = slotidx[:, c, :].bitcast(i32)
                v.tensor_scalar(rci[12], si, 7, None, ALU.logical_shift_right)
                ch(v.tensor_scalar(rci[13], si, P - 1, None, ALU.bitwise_and))
                v.tensor_copy(rc[8 + c], rci[12])
                ch(v.tensor_copy(rc[10 + c], rci[13]))
            te = rc[5:7]
            tb = [view(RA, n * EJ, [NS]) for n in range(2)]
            ch(v.tensor_scalar(tb[0], iotaT[:, :], ends[:, 0:1], None, ALU.is_ge))
            for e in range(1, E):
                ch(v.scalar_tensor_tensor(tb[e % 2], iotaT[:, :], ends[:, e:e + 1], tb[1 - e % 2],
                                          ALU.is_ge, ALU.add))
            ch(v.tensor_scalar(tb[0], tb[1], float(E - 1), float(3 * 2 * CH), ALU.min, ALU.mult))
            ch(v.tensor_copy(woff[:, :], tb[0]))

            with dve.Fori(0, NT // 2) as i:
                for q in range(2):
                    j = i * 2 + q
                    dve.wait_ge(s_inv, j + 1)
                    for c in range(2):
                        ga, pl = rc[8 + c][:, ds(j, 1)], rc[10 + c][:, ds(j, 1)]
                        v.tensor_scalar(oneA[q][c][:, 0, :], iotaA[:, :], ga, small[:, 8:9],
                                        ALU.is_equal, ALU.mult)
                        v.tensor_scalar(oneA[q][c][:, 1, :], iotaA[:, :], ga, rc[14][:, ds(j, 1)],
                                        ALU.is_equal, ALU.mult)
                        last = v.tensor_scalar(oneB[q][c], iotaB[:, :], pl, None, ALU.is_equal)
                    last.then_inc(s_one, 1)
            dve.wait_ge(s_invall, 1)
            ch(v.tensor_copy(small[:, 0:1], small[:, 8:9]))
            tile_no = view(RA, 0, [NA])
            ch(v.tensor_scalar(tile_no, psInv[:, NA:2 * NA], float(P), None, ALU.mult))
            v.tensor_tensor(tokidx[:, :], tile_no, psInv[:, 0:NA], ALU.add).then_inc(s_idx, 1)

            def hidden(t, q):
                for h in range(2):
                    dve.wait_ge(s_sg, t * 2 + (h + 1))
                    v.scalar_tensor_tensor(SG[:, 2 * h:2 * h + 2, :], PS[:, 2 * h:2 * h + 2, TS:2 * TS],
                                           sc[:, 6:7], SG[:, 2 * h:2 * h + 2, :], ALU.mult, ALU.mult
                                           ).then_inc(s_h, 1)
                for h in range(2):
                    dve.wait_ge(s_hh, t * 2 + (h + 1))
                    v.tensor_tensor(HH[q][:, 1, 2 * h:2 * h + 2, :], SG[:, 2 * h:2 * h + 2, :],
                                    HH[q][:, 0, 2 * h:2 * h + 2, :], ALU.subtract).then_inc(s_hl, 1)

            with dve.Fori(0, NS // 2) as i:
                hidden(i * 2, 0)
                hidden(i * 2 + 1, 1)
            hidden(NS - 1, 0)

            dve.wait_ge(s_yst, NS * 16)
            at = ch.n
            with dve.Fori(0, B) as b:
                for c in range(KC):
                    last = v.tensor_scalar(WTP[:, c, :], Wt[:, c, :], pooled[:, 1, c, ds(b, 1)], None, ALU.mult)
                last.then_inc(s_wtp, 1)
                dve.wait_ge(s_eff, b + 1)
                v.tensor_tensor(WE, psEff, Wq[:, :, :], ALU.add)
                v.tensor_tensor(BE[0:1, :], psBe, brow[0:1, 0, :], ALU.add).then_inc(s_we, 1)
                with dve.Fori(0, TPB // 2) as i:
                    for q in range(2):
                        jj = i * 2 + q
                        j = b * TPB + jj
                        ch.n, ch.off = at, b * (2 * TPB) + i * 4 + 2 * q
                        dve.wait_ge(s_tg[q], b * (16 * TPB) + i * 32 + 32)
                        ch(v.tensor_scalar(FF[q], YG[q][0], imp[:, 0, ds(j, 1)], None, ALU.mult))
                        v.scalar_tensor_tensor(FF[q], YG[q][1], imp[:, 1, ds(j, 1)], FF[q],
                                               ALU.mult, ALU.add).then_inc(s_f, 1)
                        dve.wait_ge(s_sf, j + 1)
                        dve.wait_ge(s_s, j + 1)
                        ch(v.tensor_tensor(SF[q], psAtt[q], SF[q], ALU.mult))
                        dve.wait_ge(s_tx[q], b * (8 * TPB) + i * 16 + 16)
                        dve.wait_ge(s_ofree, j + 1)
                        v.tensor_tensor(OB[q], SF[q], XR[q], ALU.add).then_inc(s_o, 1)

        @block.tensor
        def _(pe):
            t_ = nc.tensor
            pe.wait_ge(s_cl, 16 * LOADS)
            pe.wait_ge(s_cm, 2)
            for m, W in enumerate((Wq, Wk)):
                for hc in range(KC):
                    for kc in range(KC):
                        last = t_.transpose(psT[m][:, hc * KC + kc, :], W[:, kc, hc * P:(hc + 1) * P], identf[:, :])
                last.then_inc(s_wT, 1)
            pe.wait_ge(s_wTc, 2)
            XT4 = XT[:, :].rearrange("p (n c t) -> p n c t", c=KC, t=P)

            def attention(n):
                grp, k = n // 2, n % 2
                W, WT = ((Wq, WqT), (Wk, WkT))[k]
                WAf = WA.rearrange("p c b h -> p c (b h)")
                pe.wait_ge(s_wa, n + 1)
                for dc in range(KC):
                    for hc in range(KC):
                        t_.matmul(psX[:, dc * P:(dc + 1) * P], WT[:, hc, dc * P:(dc + 1) * P], WAf[:, hc, :],
                                  start=hc == 0, stop=hc == KC - 1)
                for hc in range(KC):
                    last = t_.matmul(psX[:, 500:501], WAf[:, hc, :], bcol[:, k, hc:hc + 1],
                                     start=hc == 0, stop=hc == KC - 1)
                last.then_inc(s_A, 1)
                pe.wait_ge(s_Ac, n + 1)
                pe.wait_ge(s_keept, BPG * (grp + 1))
                for hf in range(2):
                    for b in range(GB):
                        n0 = (grp * GB + b) * TPB + hf * BT
                        for kc in range(KC):
                            last = t_.matmul(psS[HP * b:HP * (b + 1), hf, :], A[:, kc, HP * b:HP * (b + 1)],
                                             XT4[:, n0:n0 + BT, kc, :], start=kc == 0, stop=kc == KC - 1)
                last.then_inc(s_sc, 1)
                pe.wait_ge(s_ex, n + 1)
                for j in range(TPB):
                    last = t_.transpose(psT[0][:, j, :], PR[:, j * P:(j + 1) * P], identf[:, :])
                last.then_inc(s_pt, 1)
                pe.wait_ge(s_ptc, n + 1)
                for b in range(GB):
                    for j in range(TPB):
                        last = t_.matmul(psX[HP * b:HP * (b + 1), 0:D], PT[:, j, HP * b:HP * (b + 1)],
                                         XN[:, b * TPB + j, :], start=j == 0, stop=j == TPB - 1)
                last.then_inc(s_px, 1)
                pe.wait_ge(s_pxn, n + 1)
                for kc in range(KC):
                    last = t_.transpose(psX[:, D + kc * P:D + (kc + 1) * P], pxn[:, kc * P:(kc + 1) * P],
                                        identf[:, :])
                last.then_inc(s_pxt, 1)
                pe.wait_ge(s_pxtc, n + 1)
                for hc in range(KC):
                    for kc in range(KC):
                        last = t_.matmul(psTf[1][:, hc * P:(hc + 1) * P], W[:, kc, hc * P:(hc + 1) * P],
                                         pxT[:, kc, :], start=kc == 0, stop=kc == KC - 1)
                last.then_inc(s_pv, 1)

            for grp in range(NG):
                if grp:
                    pe.wait_ge(s_pooled, 2 * grp)
                with pe.Fori(0, BPG // 2) as i:
                    for q in range(2):
                        n = i * 2 + q + grp * BPG
                        pe.wait_ge(s_xn, n + 1)
                        for u in range(BT):
                            for kc in range(KC):
                                last = t_.transpose(psT[q][:, u * KC + kc, :], XB[q][:, u, kc * P:(kc + 1) * P],
                                                    identf[:, :])
                        last.then_inc(s_tr, 1)
                        pe.wait_ge(s_xtb, n + 1)
                        for u in range(BT):
                            for kc in range(KC):
                                last = t_.matmul(psL[:, ds(n * BT + u, 1), :], XTB[q][:, u, kc, :], rw[:, kc, :],
                                                 start=kc == 0, stop=kc == KC - 1)
                        last.then_inc(s_rt, 1)
                for m in range(2):
                    attention(2 * grp + m)

            pe.wait_ge(s_rank, 1)
            t_.matmul(psRank, before[:, :], Mh, start=True, stop=True)
            t_.matmul(psCnt, onesh[:, :], Mh, start=True, stop=True).then_inc(s_rank, 1)
            t_.matmul(psInv, zeroh[:, 0:P], zeroh[:, :], start=True, stop=False)
            with pe.Fori(0, NT // 2) as i:
                for q in range(2):
                    pe.wait_ge(s_one, i * 2 + (q + 1))
                    for c in range(2):
                        last = t_.matmul(psInv, oneB[q][c], oneA[q][c].rearrange("p m a -> p (m a)"),
                                         start=False, stop=False)
                    last.then_inc(s_inv, 1)
            t_.matmul(psInv, zeroh[:, 0:P], zeroh[:, :], start=False, stop=True).then_inc(s_invall, 1)

            pe.wait_ge(s_idx, 1)
            pe.wait_ge(s_wlo, NCH)
            WMAX = (E - 1) * 3 * 2 * CH

            def offset(t):
                src = woff[0:1, t:t + 1] if isinstance(t, int) else woff[0:1, ds(t, 1)]
                return pe.value_load(src, min_val=0, max_val=WMAX)

            def transposes(t, q, nth):
                pe.wait_ge(s_g[q], nth * (16 * SUB) + 16 * SUB)
                for s in range(SUB):
                    for c in range(2 * KC):
                        last = t_.transpose(psXG[:, q, c, s * P:(s + 1) * P], GX[q][s][:, c // KC, c % KC, :],
                                            identh[:, :])
                last.then_inc(s_xgt, 1)

            def gate_up(t, q):
                w = offset(t)
                pe.wait_ge(s_xg, t + 1)
                for h in range(2):
                    if not (isinstance(t, int) and t == 0):
                        pe.wait_ge(s_h, t * 2 + (h - 1))
                    for f in range(2 * h, 2 * h + 2):
                        for m in range(2):
                            n = 0
                            for kc in range(KC):
                                for wl, xl in ((0, 0), (0, 1), (1, 0)):
                                    at = m * 2 * CH + wl * CH + kc * F + f * P
                                    last = t_.matmul(psGU[f][:, m, :], WR[:, ds(w + at, P)], XG[q][:, xl, kc, :],
                                                     start=n == 0, stop=n == 3 * KC - 1)
                                    n += 1
                    last.then_inc(s_gu, 1)

            def down(t, q):
                w = offset(t)
                pe.wait_ge(s_hl, t * 2 + 2)
                pe.wait_ge(s_yb, t + 1)
                for s in range(SUB):
                    n = 0
                    for f in range(FC):
                        for hl, wl in ((0, 0), (0, 1), (1, 0)):
                            at = 2 * 2 * CH + wl * CH + f * D
                            last = t_.matmul(psY[:, q, s, :], HH[q][:, hl, f, s * P:(s + 1) * P],
                                             WR[:, ds(w + at, D)], start=n == 0, stop=n == 3 * FC - 1)
                            n += 1
                last.then_inc(s_y, 1)

            transposes(0, 0, 0)
            transposes(1, 1, 0)
            gate_up(0, 0)
            with pe.Fori(0, (NS - 3) // 2) as i:
                for q in range(2):
                    t = i * 2 + 1 + q
                    transposes(t + 1, q, i + 1)
                    gate_up(t, 1 - q)
                    down(t - 1, q)
            t = NS - 2
            transposes(t + 1, 0, (NS - 1) // 2)
            gate_up(t, 1)
            down(t - 1, 0)
            gate_up(t + 1, 0)
            down(t, 1)
            down(t + 1, 0)

            with pe.Fori(0, B) as b:
                pe.wait_ge(s_wtp, b + 1)
                for dc in range(KC):
                    for hc in range(KC):
                        t_.matmul(psEff[:, dc, :], WqT[:, hc, dc * P:(dc + 1) * P], WTP[:, hc, :],
                                  start=hc == 0, stop=hc == KC - 1)
                for hc in range(KC):
                    last = t_.matmul(psBe, bcol[:, 0, hc:hc + 1], WTP[:, hc, :], start=hc == 0, stop=hc == KC - 1)
                last.then_inc(s_eff, 1)
                with pe.Fori(0, TPB // 2) as i:
                    for q in range(2):
                        pe.wait_ge(s_we, b + 1)
                        pe.wait_ge(s_xc, b * TPB + i * 2 + (q + 1))
                        for kc in range(KC):
                            t_.matmul(psAtt[q], XC[q][:, kc, :], WE[:, kc, :], start=kc == 0, stop=False)
                        t_.matmul(psAtt[q], ones1[0:1, :], BE[0:1, :], start=False, stop=True).then_inc(s_s, 1)


_INS = ['L0_attn_hidden_states', 'L0_attn_Wq', 'L0_attn_bq', 'L0_attn_Wqa', 'L0_attn_bqa', 'L0_attn_Wk', 'L0_attn_bk',
        'L0_attn_Wka', 'L0_attn_bka', 'L0_attn_Wt', 'L0_attn_bt', 'L0_ffn_router_w', 'L0_ffn_w1', 'L0_ffn_w3',
        'L0_ffn_w2']


def kernel(**inputs):
    import numpy as _np
    import concourse.bacc as _bacc
    from concourse import mybir as _mybir
    from concourse.bass_utils import run_bass_kernel_spmd as _run

    nc = _bacc.Bacc("TRN2", target_bir_lowering=False, num_devices=1)
    arrays, args = {}, []
    for name in _INS:
        a = _np.ascontiguousarray(inputs[name])
        arrays[f"in_{name}_dram"] = a
        args.append(nc.dram_tensor(f"in_{name}_dram", a.shape, _mybir.dt.from_np(a.dtype), kind="ExternalInput").ap())
    shape = inputs[_INS[0]].shape
    args.append(nc.dram_tensor("out_0_dram", shape, _mybir.dt.float32, kind="ExternalOutput").ap())
    recurrent_attention_moe(nc, *args)
    r = _run(nc, [arrays], core_ids=[0])
    return r.results[0]["out_0_dram"]
```

```python
import concourse.bass as bass
from concourse import mybir
from contextlib import ExitStack


def recurrent_attention_moe(
    nc: bass.Bass,
    x_in: bass.AP,
    Wq_in: bass.AP,
    bq_in: bass.AP,
    Wqa_in: bass.AP,
    bqa_in: bass.AP,
    Wk_in: bass.AP,
    bk_in: bass.AP,
    Wka_in: bass.AP,
    bka_in: bass.AP,
    Wt_in: bass.AP,
    bt_in: bass.AP,
    router_in: bass.AP,
    w1_in: bass.AP,
    w3_in: bass.AP,
    w2_in: bass.AP,
    out: bass.AP,
):
    fp32 = mybir.dt.float32
    fp16 = mybir.dt.float16
    bf16 = mybir.dt.bfloat16
    i32 = mybir.dt.int32
    u32 = mybir.dt.uint32
    ALU = mybir.AluOpType
    ACT = mybir.ActivationFunctionType
    X = mybir.AxisListType.X
    ds = bass.ds

    P = 128
    B, S, D = x_in.shape
    H = bqa_in.shape[0]
    DH = D // H
    E, _, F = w1_in.shape
    T = B * S
    NT = T // P
    KC = D // P
    FC = F // P
    BT = 4
    NB = NT // BT
    GB = 4
    NG = B // GB
    BPG = NB // NG
    TPB = S // P
    HP = P // GB
    TS = 256
    SUB = TS // P
    NS = 2 * T // TS + E - 1
    RG = T + TS
    NR = 2 * NG
    BPR = NB // NR
    NTR = NT // NR
    EPS = 1e-5
    SCALE = float(DH) ** -0.5
    XSC = 1024.0
    XSC_LOG = 10
    CH = KC * F
    assert CH == FC * D and NS % 2 == 1 and E == BPG
    NCH = 3 * E
    LOADS = 2 + 1 + 2 * KC + 2 + 2 * GB
    FAR = -3.0e38
    RAW = 6208
    CREDIT = 2
    TQ = 4
    TY = 8
    assert TY == TPB == 2 * TQ
    SHARES = ((2, 3), (4, 4), (1, 3), (4, 3))
    SPLITS, at = [], 0
    for shares in SHARES:
        SPLITS.append([range(at, at + shares[0]), range(at + shares[0], at + sum(shares))])
        at += sum(shares)
    assert at == NCH

    x_t = x_in.rearrange("b s d -> (b s) d").rearrange("(n p) d -> p n d", p=P)
    out_t = out.rearrange("b s d -> (b s) d").rearrange("(n p) d -> p n d", p=P)
    xs_dram = nc.dram_tensor("xs_dram", (T, 2 * D), fp16).ap()
    sorted_dram = nc.dram_tensor("sorted_dram", (E * RG, 2 * D), fp16).ap()
    y_dram = nc.dram_tensor("y_dram", (NS * TS, D), fp32).ap()
    be_dram = nc.dram_tensor("be_dram", (B, D), fp32).ap()
    y_t = y_dram.rearrange("(n p) d -> p n d", p=P)
    xt_dram = nc.dram_tensor("xt_dram", (T, D), fp32).ap()
    xt_t = xt_dram.rearrange("(n p) d -> p n d", p=P)
    xs_t = xs_dram.rearrange("(n p) d -> p n d", p=P)

    ctx = ExitStack()
    with ctx:
        def sb(name, shape, dt):
            return ctx.enter_context(nc.sbuf_tensor(name, shape, dt))

        def sem(name):
            return ctx.enter_context(nc.semaphore(name))

        WR = sb("weights", [P, (NCH + 1) * 2 * CH], fp16)
        XX = sb("xn_both_ways", [P, 2 * BPG * BT * D], fp32)
        RA = sb("work", [P, RAW], fp32)
        AT = sb("attention_work", [P, 6 * D], fp32)
        Wq = sb("Wq", [P, KC, D], fp32)
        Wk = sb("Wk", [P, KC, D], fp32)
        WqT = sb("WqT", [P, KC, D], fp32)
        WkT = sb("WkT", [P, KC, D], fp32)
        identf = sb("identf", [P, P], fp32)
        identh = sb("identh", [P, P], fp16)
        before = sb("before", [P, P], bf16)
        zerosh = sb("zerosh", [P, D], fp16)
        onesb = sb("onesb", [P, P], bf16)
        headmask = sb("headmask", [P, KC, HP], fp32)
        Wqa = sb("Wqa", [P, KC, HP], fp32)
        Wka = sb("Wka", [P, KC, HP], fp32)
        rw = sb("rw", [P, KC, E], fp32)
        bcol = sb("bcol", [P, 2, KC], fp32)
        sbias = sb("sbias", [P, 2], fp32)
        pooled = sb("pooled", [P, 2, KC, B], fp32)
        sc = sb("sc", [P, 8], fp32)
        gcol = sb("gcol", [P, 2 * BT, 2], u32)
        small = sb("small", [P, 64], fp32)
        small_i = sb("small_i", [P, 16], i32)
        wmax = sb("wmax", [P, 3, E], fp32)
        rowidx = sb("rowidx", [P, NT, 2], u32)
        imp = sb("imp", [P, 2, NT], fp32)
        woff = sb("woff", [P, NS], i32)
        rowoff = sb("rowoff", [P, NS], i32)
        zoff = sb("zoff", [P, E + 1], i32)
        iotaT = sb("iotaT", [P, NS], fp32)
        iotaE = sb("iotaE", [P, E], fp32)
        notfirst = sb("notfirst", [P, NTR], fp32)

        def view(region, at, shape, dt=fp32):
            n = 1
            for s in shape:
                n *= s
            size = {fp16: 2, bf16: 2}.get(dt, 4)
            v = region[:, at:at + n * size // 4]
            if dt != fp32:
                v = v.bitcast(dt)
            if len(shape) == 1:
                return v
            names = "abcd"[:len(shape)]
            kw = {c: s for c, s in zip(names[1:], shape[1:])}
            return v.rearrange("p (" + " ".join(names) + ") -> p " + " ".join(names), **kw)

        def weight_view(chunk):
            return WR[:, (chunk + 1) * 2 * CH:(chunk + 2) * 2 * CH].bitcast(fp32)

        XN = view(XX, 0, [BPG * BT, D])
        XNf = view(XX, 0, [BPG * BT * D])
        XT = view(XX, BPG * BT * D, [BPG * BT * KC * P])
        itemp = view(XX, BPG * BT * D, [NS], i32)
        XTt = view(XX, BPG * BT * D, [BPG * BT, D])
        XT4 = view(XX, BPG * BT * D, [BPG * BT, KC, P])
        PR = view(AT, 0, [S])
        PT = view(AT, 0, [TPB, P])
        WA = view(AT, S, [KC, GB, HP])
        pxn = view(AT, S, [D])
        A = view(AT, S + D, [KC, P])
        pxT = view(AT, S + D, [KC, P])
        SQ = [view(AT, q * CH // 2, [CH], bf16) for q in range(2)]
        assert S == CH == 4 * D

        BW = BT * D
        XS = [view(RA, q * BW, [BT, 2, D], fp16) for q in range(2)]
        XTB = [view(RA, 2 * BW + q * BW, [BT, KC, P]) for q in range(2)]
        EJ = E * NTR
        IN_BLOCKS = NR - 2
        at_routing = [AT if part == IN_BLOCKS else RA[:, 2 * BW:4 * BW] for part in range(NR)]
        route = [([view(reg, n * EJ, [E, NTR]) for n in range(7)],
                  [view(reg, n * EJ, [EJ]) for n in range(7)],
                  [view(reg, 7 * EJ + n * NTR, [NTR]) for n in range(4)],
                  [view(reg, 7 * EJ + (4 + n) * NTR, [NTR], i32) for n in range(2)],
                  view(reg, 8 * EJ, [EJ], bf16)) for reg in at_routing]
        tb = [view(RA, 2 * BW + 9 * EJ + n * NS, [NS]) for n in range(3)]
        assert 6 * NTR <= EJ and 9 * EJ + 3 * NS <= 2 * BW and 9 * EJ <= 6 * D and 2 * EJ <= 512
        o = 4 * BW
        SC = [view(RA, o + q * BW, [BT, 2 * D], fp16) for q in range(2)]
        stats = [view(RA, o + 2 * BW + 32 * q, [BT, 6]) for q in range(2)]
        meanvar = [view(RA, o + 2 * BW + 32 * q + 24, [BT, 2]) for q in range(2)]
        assert o + 2 * BW + 64 <= RAW
        GX = [[view(XX, (2 * q + s) * D, [2, KC, P], fp16) for s in range(SUB)] for q in range(2)]
        GXf = [view(XX, 2 * q * D, [SUB, 2 * D], fp16) for q in range(2)]
        XG = [view(XX, 4 * D + q * 2 * TS, [2, KC, TS], fp16) for q in range(2)]
        o = 4 * D + 4 * TS
        assert SUB == 2
        SG = view(XX, o, [FC, TS])
        HH = [view(XX, o + (1 + q) * FC * TS, [2, FC, TS], fp16) for q in range(2)]
        oy = o + 3 * FC * TS
        YB = [view(XX, oy + q * SUB * D, [SUB, D]) for q in range(2)]
        ot = oy + 2 * SUB * D
        YG = [[view(XX, (2 * q + c) * D, [D]) for c in range(2)] for q in range(TY)]
        assert 2 * TY * D <= ot
        XR = [view(XX, ot + q * D, [D]) for q in range(TQ)]
        OB = [view(XX, ot + (4 + q) * D, [D]) for q in range(TQ)]
        SF = [view(XX, ot + (8 + q) * D, [D]) for q in range(TQ)]
        XC = [view(XX, ot + (12 + q) * D, [KC, P]) for q in range(TQ)]
        of = ot + 16 * D
        assert of >= BPG * BT * D
        BE = view(XX, of, [B, D])
        Wt = view(XX, of + B * D, [KC, D])
        WTP = [view(XX, of + (B + 2 + 2 * q) * D, [KC, D]) for q in range(2)]
        brow = view(XX, of + (B + 6) * D, [2, D])
        bqk = view(XX, of + (B + 8) * D, [KC, B])
        be8 = view(XX, of + (B + 9) * D, [D])
        assert of + (B + 10) * D <= 2 * BPG * BT * D and KC * B <= D
        WE = view(RA, 0, [B, KC, D])
        assert B * KC * D <= 4 * BW
        FF = [view(RA, 4 * BW + q * D, [D]) for q in range(TQ)]
        assert TQ * D <= 2 * BW

        PS = ctx.enter_context(nc.psum_tensor("PS", [P, 8, 512], fp32))
        psT = [PS[:, 2 * q:2 * q + 2, :].rearrange("p b (u t) -> p (b u) t", t=P) for q in range(2)]
        psTf = [PS[:, 2 * q:2 * q + 2, :].rearrange("p b n -> p (b n)") for q in range(2)]
        psS = PS[:, 4:6, :]
        psX = PS[:, 7, :]
        logits_at = 7 * 512 - (NR - 1) * NTR * E
        assert logits_at >= 6 * 512
        psL = PS[:, :, :].rearrange("p b n -> p (b n)")[:, logits_at:logits_at + NT * E].rearrange(
            "p (n e) -> p n e", e=E)
        bank = [5 if part == IN_BLOCKS else 2 for part in range(NR)]
        psRank = [PS[:, n, 0:EJ] for n in bank]
        psCnt = [PS[:, n, EJ:2 * EJ] for n in bank]
        psGU = [PS[:, f, :].rearrange("p (m t) -> p m t", m=2) for f in range(FC)]
        psXG = PS[:, 4:6, :].bitcast(fp16).rearrange("p b (c t) -> p b c t", t=TS)
        psY = PS[:, 6:8, :].rearrange("p b (s d) -> p b s d", d=D)
        psNorm = [PS[:, 4 + q, :] for q in range(2)]
        psAtt = [PS[:, q, 0:D] for q in range(TQ)]
        psEff = [PS[:, q, :].rearrange("p (c n) -> p c n", c=KC) for q in range(2)]
        psBe = PS[0:B, 2, 0:D]

        s_cl = sem("constants_loaded")
        s_cm = sem("constants_made")
        s_pc = sem("pool_chain")
        s_dc = sem("vector_chain")
        s_ac = sem("scalar_chain")
        s_turn = sem("pool_turn")
        s_vturn = sem("vector_turn")
        s_x = [sem(f"x_loaded{q}") for q in range(2)]
        s_var = sem("variance_ready")
        s_std = sem("std_ready")
        s_xn = sem("xn_ready")
        s_hi = sem("xn_hi_ready")
        s_lo = sem("xn_lo_ready")
        s_xsst = [sem(f"xn_halves_stored{q}") for q in range(2)]
        s_xsfree = sem("xn_halves_free")
        s_tr = sem("xn_transposed")
        s_xtb = sem("xnT_block_ready")
        s_rt = sem("router_done")
        s_wT = sem("weight_transposed")
        s_wTc = sem("weight_transpose_copied")
        s_wa = sem("score_weights_scaled")
        s_A = sem("score_fold_done")
        s_Ac = sem("score_fold_copied")
        s_sc = sem("scores_done")
        s_mx = sem("score_max_ready")
        s_ex = sem("probs_ready")
        s_pt = sem("probs_transposed")
        s_ptc = sem("probs_transpose_copied")
        s_px = sem("weighted_xn_done")
        s_pxn = sem("weighted_xn_scaled")
        s_pxt = sem("weighted_xn_transposed")
        s_pxtc = sem("weighted_xn_transpose_copied")
        s_pv = sem("pooled_done")
        s_pooled = sem("pooled_ready")
        s_w = [sem(f"weights_loaded{q}") for q in range(2)]
        s_sq = sem("weight_squares_ready")
        s_nm = sem("weight_norms_done")
        s_nx = sem("weight_norm_max_ready")
        s_scale = sem("scales_ready")
        s_whi = sem("weight_hi_ready")
        s_wlo = sem("weight_lo_ready")
        s_choice = sem("choices_ready")
        s_rank = sem("ranks_done")
        s_slots = sem("slots_ready")
        s_tables = sem("tile_tables_ready")
        s_scl = [sem(f"halves_loaded{q}") for q in range(2)]
        s_sct = [sem(f"halves_scattered{q}") for q in range(2)]
        s_zero = sem("zeros_stored")
        s_col = sem("index_column_ready")
        s_g = [sem(f"gathered{q}") for q in range(2)]
        s_xgt = sem("gather_transposed")
        s_xg = sem("gather_transpose_copied")
        s_gu = sem("gate_up_done")
        s_sg = sem("silu_ready")
        s_h = sem("hidden_ready")
        s_hh = sem("hidden_hi_ready")
        s_hl = sem("hidden_lo_ready")
        s_y = sem("expert_out_done")
        s_yb = sem("expert_out_copied")
        s_yst = sem("expert_out_stored")
        s_yfree = sem("expert_out_free")
        s_wtp = sem("out_weights_scaled")
        s_eff = sem("out_weights_folded")
        s_we = sem("out_weights_ready")
        s_tc = sem("tail_column_ready")
        s_tl = sem("out_weights_loaded")
        s_bq = sem("bias_products_ready")
        s_be = sem("bias_sums_done")
        s_be8 = sem("biases_ready")
        s_best = sem("biases_stored")
        s_beld = sem("biases_spread")
        s_fa = sem("first_expert_weighted")
        s_tg = [sem(f"tail_gathered{q}") for q in range(TY)]
        s_tx = [sem(f"tail_x_loaded{q}") for q in range(TQ)]
        s_xtst = sem("xnT_stored")
        s_s = sem("attention_out_done")
        s_f = sem("ffn_out_ready")
        s_sf = sem("gate_ready")
        s_o = sem("out_ready")
        s_ost = [sem(f"out_stored{q}") for q in range(TQ)]
        s_ofree = sem("out_free")

        block = ctx.enter_context(nc.Block())

        class Chain:

            def __init__(self, eng, s):
                self.eng, self.s, self.n, self.off = eng, s, 0, None

            def __call__(self, ins):
                ins.then_inc(self.s, 1)
                self.n += 1
                self.eng.wait_ge(self.s, self.n if self.off is None else self.off + self.n)

            def enter(self, turn, steps):
                self.off, self.steps, self.at = turn * steps, steps, self.n

            def leave(self, turns):
                assert self.n - self.at == self.steps, (self.n - self.at, self.steps)
                self.n, self.off = self.at + self.steps * turns, None

        @block.sync
        def _(sp):
            def load_constants():
                for dst, src in ((Wq, Wq_in), (Wk, Wk_in)):
                    sp.dma_start(dst[:, :, :], src.rearrange("(c p) n -> p c n", p=P)).then_inc(s_cl, 16)
                sp.dma_start(rw[:, :, :], router_in.rearrange("(c p) n -> p c n", p=P)).then_inc(s_cl, 16)
                for m, src in enumerate((bq_in, bk_in)):
                    for c in range(KC):
                        sp.dma_start(bcol[:, m, c:c + 1], src[c * P:(c + 1) * P].rearrange("(p a) -> p a", a=1)
                                     ).then_inc(s_cl, 16)
                sp.wait_ge(s_cm, 1)
                for dst, src in ((Wqa, Wqa_in), (Wka, Wka_in)):
                    sp.dma_start(dst[:, :, 0:H], src.rearrange("(c p) n -> p c n", p=P)).then_inc(s_cl, 16)
                for m, src in enumerate((bqa_in, bka_in)):
                    for b in range(GB):
                        sp.dma_start(sbias[HP * b:HP * b + H, m:m + 1],
                                     src.rearrange("(n a) -> n a", a=1)).then_inc(s_cl, 16)

            def rows(ap, n, tiles=BT):
                return ap[:, n * tiles:(n + 1) * tiles, :] if isinstance(n, int) else ap[:, ds(n * tiles, tiles), :]

            def load_block(m, grp, q):
                sp.dma_start(rows(XN, m), rows(x_t, m + grp * BPG)).then_inc(s_x[q], 16)

            def store_block(i, grp, q, more):
                m = i * 2 + q
                sp.wait_ge(s_lo, m + (grp * BPG + 1))
                sp.dma_start(rows(xs_t, m + grp * BPG), XS[q].rearrange("p u c d -> p u (c d)")
                             ).then_inc(s_xsst[q], 16)
                if more:
                    load_block(m + 3, grp, 1 - q)
                sp.wait_ge(s_xsst[q], i * 16 + (grp * (BPG // 2) * 16 + 16))
                sp.sem_inc(s_xsfree, 1)

            def store_blocks(grp):
                sp.wait_ge(s_x[0], grp * (BPG // 2) * 16 + 16)
                load_block(2, grp, 0)
                with sp.Fori(0, BPG // 2 - 2) as i:
                    for q in range(2):
                        store_block(i, grp, q, True)
                store_block(BPG // 2 - 2, grp, 0, True)
                store_block(BPG // 2 - 2, grp, 1, False)
                for q in range(2):
                    store_block(BPG // 2 - 1, grp, q, False)

            def load_halves(i, q, first=False):
                if not first:
                    sp.wait_ge(s_sct[q], i * (2 * BT * 16))
                sp.dma_start(SC[q], rows(xs_t, i * 2 + q)).then_inc(s_scl[q], 16)

            load_block(0, 0, 0)
            load_block(1, 0, 1)
            load_constants()
            def store_transposes(grp):
                sp.wait_ge(s_xtb, BPG * (grp + 1))
                with sp.Fori(0, BPG // 2) as i:
                    sp.dma_start(xt_t[:, ds(i * (2 * BT) + grp * BPG * BT, 2 * BT), :], XTt[:, ds(i * (2 * BT), 2 * BT), :]
                                 ).then_inc(s_xtst, 16)

            store_blocks(0)
            for q in range(2):
                load_halves(0, q, True)
            store_transposes(0)
            with sp.Fori(0, BPG // 2 - 2) as i:
                for q in range(2):
                    load_halves(i + 1, q)
            sp.wait_ge(s_px, 2)
            load_block(0, 1, 0)
            load_block(1, 1, 1)
            sp.wait_ge(s_x[0], BPG // 2 * 16 + 16)
            load_block(2, 1, 0)
            for i in range(BPG // 2):
                for q in range(2):
                    store_block(i, 1, q, i * 2 + q + 3 < BPG)
                    if i == 0:
                        load_halves(BPG // 2 - 1, q)
                if i == BPG // 2 - 2:
                    for q in range(2):
                        load_halves(BPG // 2, q)
            store_transposes(1)
            with sp.Fori(0, BPR // 2) as i:
                for q in range(2):
                    load_halves(i + (BPG // 2 + 1), q)
            for i in range(BPG // 2 + 1 + BPR // 2, NB // 2):
                for q in range(2):
                    load_halves(i, q)

            sp.wait_ge(s_sc, 2 * NG)
            sp.wait_ge(s_xtst, NB // 2 * 16)
            sp.dma_start(Wt, Wt_in.rearrange("(c p) n -> p c n", p=P)).then_inc(s_tl, 16)
            for m, src in enumerate((bq_in, bt_in)):
                sp.dma_start(brow[0:B, m, :], src.rearrange("(a n) -> a n", a=1).broadcast_to([B, D])
                             ).then_inc(s_tl, 16)
            sp.wait_ge(s_tables, 1)
            zeros = zerosh[:, :].rearrange("p (s d) -> p s d", s=1).broadcast_to([P, SUB * 2, D])
            for e in range(E + 1):
                if e == E:
                    sp.wait_ge(s_zero, 16 * E)
                row = sp.value_load(zoff[0:1, e:e + 1], min_val=0, max_val=E * RG - TS)
                sp.dma_start(sorted_dram[ds(row, TS), :].rearrange("(p s) (c d) -> p (s c) d", p=P, d=D), zeros
                             ).then_inc(s_zero, 16)
            sp.wait_ge(s_px, 2 * NG)
            sp.wait_ge(s_zero, 16 * (E + 1))
            for q in range(2):
                sp.wait_ge(s_sct[q], NB // 2 * (2 * BT * 16))

            def row_of(t):
                src = rowoff[0:1, t:t + 1] if isinstance(t, int) else rowoff[0:1, ds(t, 1)]
                return sp.value_load(src, min_val=0, max_val=E * RG - TS)

            def load_tile(t, q, first=False):
                row = row_of(t)
                if not first:
                    sp.wait_ge(s_xgt, t - 1)
                sp.dma_start(GXf[q], sorted_dram[ds(row, TS), :].rearrange("(s p) d -> p s d", p=P)
                             ).then_inc(s_g[q], 16)

            def store_tile(t, q):
                sp.wait_ge(s_yb, t + (1 + CREDIT))
                sp.dma_start(rows(y_t, t, SUB), YB[q]).then_inc(s_yst, 16)
                sp.wait_ge(s_yst, t * 16 + 16)
                sp.sem_inc(s_yfree, 1)

            load_tile(0, 0, True)
            load_tile(1, 1, True)
            load_tile(2, 0)
            sp.wait_ge(s_be8, 1)
            sp.dma_start(be_dram[:, :], be8[0:B, :]).then_inc(s_best, 16)
            sp.wait_ge(s_best, 16)
            sp.dma_start(BE, be_dram.rearrange("(a b) n -> a b n", a=1).broadcast_to([P, B, D])).then_inc(s_beld, 16)
            with sp.Fori(0, (NS - 3) // 2) as i:
                for q in range(2):
                    load_tile(i * 2 + (3 + q), 1 - q)
                    store_tile(i * 2 + q, q)
            for t in range(NS - 3, NS):
                store_tile(t, t % 2)

            def load_tail(j, q):
                at = slice(j, j + 1) if isinstance(j, int) else ds(j, 1)
                sp.dma_start(XR[q], x_t[:, at, :]).then_inc(s_tx[q], 16)
                sp.dma_start(XC[q], xt_t[:, at, :].rearrange("p a (c t) -> p (a c) t", c=KC)).then_inc(s_tx[q], 16)

            def store_tail(i, q):
                j = i * TQ + q
                sp.wait_ge(s_o, j + (1 + TQ))
                at = slice(j, j + 1) if isinstance(j, int) else ds(j, 1)
                sp.dma_start(out_t[:, at, :], OB[q]).then_inc(s_ost[q], 16)

            def step(i, q, last=False):
                store_tail(i, q)
                if not last:
                    load_tail(i * TQ + (TQ + q), q)
                if not (isinstance(i, int) and i == 0 and q == 0):
                    sp.wait_ge(s_ost[q - 1], (i if q else i - 1) * 16 + 16)
                    sp.sem_inc(s_ofree, 1)

            for q in range(TQ):
                load_tail(q, q)
            step(0, 0)
            with sp.Fori(0, NT // TQ - 2) as i:
                for q in range(1, TQ):
                    step(i, q)
                step(i + 1, 0)
            for q in range(1, TQ):
                step(NT // TQ - 2, q)
            for q in range(TQ):
                step(NT // TQ - 1, q, last=True)
            sp.wait_ge(s_ost[TQ - 1], NT // TQ * 16)

        @block.gpsimd
        def _(pool):
            ch = Chain(pool, s_pc)
            g = nc.gpsimd
            g.memset(Wqa[:, :, :], 0.0)
            g.memset(Wka[:, :, :], 0.0)
            g.memset(sbias[:, :], 0.0).then_inc(s_cm, 1)
            g.memset(identf[:, :], 0.0)
            g.memset(onesb[:, :], 1.0)
            g.memset(zerosh[:, :], 0.0)
            g.memset(notfirst[:, :], 1.0)
            g.iota(itemp, pattern=[[1, NS]], base=0, channel_multiplier=0)
            ch(g.memset(headmask[:, :, :], 1.0))
            ch(g.affine_select(out=identf[:, :], in_=identf[:, :], compare_op=ALU.not_equal, fill=1.0,
                               base=0, pattern=[[-1, P]], channel_multiplier=1))
            g.tensor_copy(iotaE[:, :], itemp[:, 0:E])
            g.tensor_copy(iotaT[:, :], itemp)
            ch(g.tensor_copy(identh[:, :], identf[:, :]))
            g.affine_select(out=notfirst[:, :], in_=notfirst[:, :], compare_op=ALU.not_equal, fill=0.0, base=0,
                            pattern=[[1, NTR]], channel_multiplier=0)
            ch(g.affine_select(out=before[:, :], in_=onesb[:, :], compare_op=ALU.is_gt, fill=0.0,
                               base=0, pattern=[[1, P]], channel_multiplier=-1))
            ch(g.affine_select(out=headmask[:, :, :], in_=headmask[:, :, :], compare_op=ALU.is_ge, fill=0.0,
                               base=0, pattern=[[P, KC], [-DH, HP]], channel_multiplier=1))
            g.affine_select(out=headmask[:, :, :], in_=headmask[:, :, :], compare_op=ALU.is_ge, fill=0.0,
                            base=DH - 1, pattern=[[-P, KC], [DH, HP]], channel_multiplier=-1
                            ).then_inc(s_cm, 1)
            pool.sem_inc(s_xsfree, CREDIT)
            for s in (s_nm, s_nx, s_yb, s_yfree):
                pool.sem_inc(s, CREDIT)
            for s in (s_ofree, s_o):
                pool.sem_inc(s, TQ)
            pool.sem_inc(s_f, TY)

            def scatter(i, q):
                k = i * 2 + q
                pool.wait_ge(s_scl[q], i * 16 + 16)
                pool.sem_inc(s_turn, 1)
                cols = gcol[:, q * BT:(q + 1) * BT, :]
                g.tensor_copy(cols, rowidx[:, ds(k * BT, BT), :]).then_inc(s_col, 1)
                pool.wait_ge(s_col, k + 1)
                pool.sem_inc(s_turn, 1)
                for u in range(BT):
                    for c in range(2):
                        pool.indirect_dma_start(
                            out=sorted_dram, in_=SC[q][:, u, :], in_offset=None,
                            out_offset=bass.IndirectOffsetOnAxis(ap=gcol[:, q * BT + u, c:c + 1], axis=0)
                        ).then_inc(s_sct[q], 16)

            for part in range(NR):
                pool.wait_ge(s_slots, part + 1)
                with pool.Fori(0, BPR // 2) as i:
                    for q in range(2):
                        scatter(i + part * (BPR // 2), q)

            pool.wait_ge(s_slots, NR + 1)
            pool.wait_ge(s_yst, NS * 16)
            with pool.Fori(0, NT // TY) as i:
                for h in range(2):
                    pool.wait_ge(s_f, i * TY + (h * TQ + 4))
                    pool.sem_inc(s_turn, 1)
                    g.tensor_copy(gcol[:, h * TQ:(h + 1) * TQ, :], rowidx[:, ds(i * TY + h * TQ, TQ), :]).then_inc(s_tc, 1)
                    pool.wait_ge(s_tc, i * 2 + (h + 1))
                    pool.sem_inc(s_turn, 1)
                    for u in range(TQ):
                        q = h * TQ + u
                        pool.wait_ge(s_f, i * TY + (q + 1))
                        pool.sem_inc(s_turn, 1)
                        for c in range(2):
                            pool.indirect_dma_start(
                                out=YG[q][c], out_offset=None, in_=y_dram,
                                in_offset=bass.IndirectOffsetOnAxis(ap=gcol[:, q, c:c + 1], axis=0)
                            ).then_inc(s_tg[q], 16)

        @block.scalar
        def _(act):
            a = nc.scalar
            ch = Chain(act, s_ac)
            def load_expert(e, q):
                for m, src in enumerate((w1_in, w3_in, w2_in)):
                    of = src[e:e + 1] if isinstance(e, int) else src[ds(e, 1)]
                    of = of.rearrange("a (c p) n -> p (a c) n", p=P)
                    slot = e * 3 + (m + 1)
                    dst = (WR[:, slot * 2 * CH:(slot + 1) * 2 * CH] if isinstance(e, int) else
                           WR[:, ds(slot * (2 * CH), 2 * CH)]).bitcast(fp32)
                    act.dma_start(dst.rearrange("p (c n) -> p c n", c=of.shape[1]), of).then_inc(s_w[q], 16)

            load_expert(0, 0)
            load_expert(1, 1)
            for m, dst in enumerate((WqT, WkT)):
                act.wait_ge(s_wT, m + 1)
                a.copy(dst[:, :, :].rearrange("p c n -> p (c n)"), psTf[m][:, 0:KC * D]).then_inc(s_wTc, 1)

            def hi(c):
                k = 1 if c % 3 == 2 else 0
                if c:
                    act.wait_ge(s_wlo, 2 * c - 1)
                for h in range(2):
                    at = c * 2 * CH + h * CH // 2
                    a.activation(WR[:, at:at + CH // 2], weight_view(c)[:, h * CH // 2:(h + 1) * CH // 2],
                                 ACT.Copy, scale=sc[:, k:k + 1]).then_inc(s_whi, 1)

            def attention(n, split, after_probs=lambda: None):
                act.wait_ge(s_A, n + 1)
                a.copy(A.rearrange("p c n -> p (c n)"), psX[:, 0:KC * P]).then_inc(s_Ac, 1)
                for c in split[0]:
                    hi(c)
                act.wait_ge(s_mx, n + 1)
                a.activation(PR, psS.rearrange("p b n -> p (b n)"), ACT.Exp,
                             bias=small[:, 4:5], scale=SCALE, accum_out=small[:, 5:6]).then_inc(s_ex, 1)
                after_probs()
                act.wait_ge(s_pt, n + 1)
                a.copy(PT, psT[0]).then_inc(s_ptc, 1)
                for c in split[1]:
                    hi(c)
                act.wait_ge(s_pxt, n + 1)
                a.copy(pxT.rearrange("p c n -> p (c n)"), psX[:, 256:256 + KC * P]).then_inc(s_pxtc, 1)

            def root(n, q):
                act.wait_ge(s_var, n + 1)
                a.activation(small[:, 24 + 8 * q:24 + 8 * q + BT], small[:, 16 + 8 * q:16 + 8 * q + BT],
                             ACT.Sqrt).then_inc(s_std, 1)

            def keep(m, grp, q):
                act.wait_ge(s_tr, m + (grp * BPG + 1))
                if grp and isinstance(m, int) and m == 0:
                    act.wait_ge(s_xtst, grp * (BPG // 2) * 16)
                dst = XT[:, m * BW:(m + 1) * BW] if isinstance(m, int) else XT[:, ds(m * BW, BW)]
                a.activation(dst, psTf[q], ACT.Copy, scale=1.0 / XSC)
                a.activation(XTB[q].rearrange("p u c t -> p (u c t)"), psTf[q], ACT.Copy, scale=1.0 / XSC
                             ).then_inc(s_xtb, 1)

            def block_steps(i, grp, q, prefetch=False, first=False, more=True):
                m = i * 2 + q
                n = m + grp * BPG

                def square(w):
                    if grp:
                        return
                    if w == 0:
                        act.wait_ge(s_w[q], i * (16 * 3) + 16 * 3)
                    act.wait_ge(s_nm, m * 3 + (w + 1))
                    slot = m * 3 + (w + 1)
                    raw = (WR[:, slot * 2 * CH:(slot + 1) * 2 * CH] if isinstance(m, int) else
                           WR[:, ds(slot * (2 * CH), 2 * CH)]).bitcast(fp32)
                    a.activation(SQ[(3 * q + w) % 2], raw, ACT.Square).then_inc(s_sq, 1)

                act.wait_ge(s_xn, n + 1)
                act.wait_ge(s_xsfree, n + 1)
                src = XN[:, m * BT:(m + 1) * BT, :] if isinstance(m, int) else XN[:, ds(m * BT, BT), :]
                a.activation(XS[q][:, :, 0, :], src, ACT.Copy, scale=XSC).then_inc(s_hi, 1)
                square(0)
                if more:
                    root(n + 1, 1 - q)
                square(1)
                if not first:
                    keep(m - 1, grp, 1 - q)
                square(2)
                if prefetch:
                    load_expert(m + 2, q)

            def blocks(grp):
                for q in range(2):
                    block_steps(0, grp, q, prefetch=not grp, first=not q)
                with act.Fori(0, BPG // 2 - 2) as i:
                    for q in range(2):
                        block_steps(i + 1, grp, q, prefetch=not grp)
                for q in range(2):
                    block_steps(BPG // 2 - 1, grp, q, more=not q)
                keep(BPG - 1, grp, 1)

            def choice_weights():
                act.wait_ge(s_choice, NR)
                a.activation(imp[:, 1, :], imp[:, 1, :], ACT.Exp).then_inc(s_choice, 1)

            act.preload_act_table(ACT.Sqrt)
            root(0, 0)
            blocks(0)
            act.preload_act_table(ACT.Exp)
            act.wait_ge(s_scale, 1)
            attention(0, SPLITS[0])
            attention(1, SPLITS[1])
            act.preload_act_table(ACT.Sqrt)
            root(BPG, 0)
            blocks(1)
            act.preload_act_table(ACT.Exp)
            attention(2, SPLITS[2])
            attention(3, SPLITS[3], choice_weights)

            act.preload_act_table(ACT.Silu)

            def copy_gather(t, q):
                act.wait_ge(s_xgt, t + 1)
                a.copy(XG[q].rearrange("p c k t -> p (c k t)"), psXG[:, q, :, :].rearrange("p c t -> p (c t)")
                       ).then_inc(s_xg, 1)

            def silu_hi(t, q):
                for h in range(2):
                    act.wait_ge(s_gu, t * 2 + (h + 1))
                    if not (isinstance(t, int) and t == 0):
                        act.wait_ge(s_hl, t * 2 + (h - 1))
                    a.activation(SG[:, 2 * h:2 * h + 2, :], PS[:, 2 * h:2 * h + 2, 0:TS], ACT.Silu,
                                 scale=sc[:, 2:3]).then_inc(s_sg, 1)
                for h in range(2):
                    act.wait_ge(s_h, t * 2 + (h + 1))
                    a.copy(HH[q][:, 0, 2 * h:2 * h + 2, :], SG[:, 2 * h:2 * h + 2, :]).then_inc(s_hh, 1)

            def copy_out(t, q):
                act.wait_ge(s_y, t + 1)
                act.wait_ge(s_yfree, t + 1)
                a.activation(YB[q].rearrange("p s d -> p (s d)"), psY[:, q, :, :].rearrange("p s d -> p (s d)"),
                             ACT.Copy, scale=sc[:, 7:8]).then_inc(s_yb, 1)

            copy_gather(0, 0)
            copy_gather(1, 1)
            silu_hi(0, 0)
            with act.Fori(0, (NS - 3) // 2) as i:
                for q in range(2):
                    t = i * 2 + 1 + q
                    copy_gather(t + 1, q)
                    silu_hi(t, 1 - q)
                    copy_out(t - 1, q)
            t = NS - 2
            copy_gather(t + 1, 0)
            silu_hi(t, 1)
            copy_out(t - 1, 0)
            silu_hi(t + 1, 0)
            copy_out(t, 1)
            copy_out(t + 1, 0)

            def first_expert(i, q):
                j = i * TY + q
                act.wait_ge(s_tg[q], i * 32 + 32)
                w = imp[:, 0, j:j + 1] if isinstance(j, int) else imp[:, 0, ds(j, 1)]
                a.activation(FF[q % TQ], YG[q][0], ACT.Copy, scale=w).then_inc(s_fa, 1)

            def gate(i, q):
                act.wait_ge(s_f, i * TY + (q + 1 + TY))
                a.activation(SF[q % TQ], FF[q % TQ], ACT.Silu).then_inc(s_sf, 1)

            def steps(i, more=True):
                for q in range(TY):
                    if more or q < TY - 1:
                        first_expert(i + (q + 1) // TY, (q + 1) % TY)
                    gate(i, q)

            first_expert(0, 0)
            with act.Fori(0, NT // TY - 1) as i:
                steps(i)
            steps(NT // TY - 1, more=False)

        @block.vector
        def _(dve):
            v = nc.vector
            ch = Chain(dve, s_dc)
            wqa4 = Wqa[:, :, :].rearrange("p c (a h) -> p c a h", a=1).broadcast_to([P, KC, GB, HP])
            wka4 = Wka[:, :, :].rearrange("p c (a h) -> p c a h", a=1).broadcast_to([P, KC, GB, HP])

            def lo(c):
                k = 1 if c % 3 == 2 else 0
                for h in range(2):
                    dve.wait_ge(s_whi, 2 * c + 1 + h)
                    if c and not h:
                        dve.wait_ge(s_wlo, 2 * c)
                    at = c * 2 * CH + h * CH // 2
                    v.scalar_tensor_tensor(WR[:, at + CH:at + CH + CH // 2],
                                           weight_view(c)[:, h * CH // 2:(h + 1) * CH // 2], sc[:, k:k + 1],
                                           WR[:, at:at + CH // 2], ALU.mult, ALU.subtract).then_inc(s_wlo, 1)

            def attention(n, during_scores, during_sums):
                grp, k = n // 2, n % 2
                if not k:
                    v.tensor_copy(WA, wqa4).then_inc(s_wa, 1)
                else:
                    v.tensor_tensor(WA, wka4, pooled[:, 0, :, grp * GB:(grp + 1) * GB].rearrange("p c (b a) -> p c b a", a=1)
                                    .broadcast_to([P, KC, GB, HP]), ALU.mult).then_inc(s_wa, 1)
                dve.wait_ge(s_Ac, n + 1)
                ch(v.tensor_tensor(small[:, 6:7], psX[:, 500:501], sbias[:, k:k + 1], ALU.add))
                during_scores()
                dve.wait_ge(s_sc, n + 1)
                ch(v.reduce_max(small[:, 7:8], psS.rearrange("p b n -> p (b n)"), X))
                ch(v.tensor_tensor(small[:, 7:8], small[:, 7:8], small[:, 6:7], ALU.add))
                ch(v.tensor_tensor(small[:, 6:7], small[:, 6:7], small[:, 7:8], ALU.subtract))
                v.tensor_scalar(small[:, 4:5], small[:, 6:7], SCALE, None, ALU.mult).then_inc(s_mx, 1)
                dve.wait_ge(s_ex, n + 1)
                ch(v.reciprocal(small[:, 5:6], small[:, 5:6]))
                during_sums()
                dve.wait_ge(s_px, n + 1)
                v.tensor_scalar(pxn, psX[:, 0:D], small[:, 5:6], None, ALU.mult).then_inc(s_pxn, 1)
                dve.wait_ge(s_pv, n + 1)
                pv = psTf[1][:, 0:KC * P].rearrange("p (c b h) -> p c b h", c=KC, b=GB)
                own = A.rearrange("p c (b h) -> p c b h", b=GB)
                for c in range(KC):
                    mask = headmask[:, c, :].rearrange("p (a h) -> p a h", a=1).broadcast_to([P, GB, HP])
                    last = v.tensor_tensor(own[:, c], pv[:, c], mask, ALU.mult)
                ch(last)
                dst = pooled[:, k, :, grp * GB:(grp + 1) * GB]
                ch(v.tensor_reduce(dst, own, X, ALU.add))
                for c in range(KC):
                    last = v.tensor_scalar(dst[:, c, :], dst[:, c, :], bcol[:, k, c:c + 1], None, ALU.add)
                if not k:
                    last.then_inc(s_pooled, 1)
                    dve.wait_ge(s_pooled, n + 1)
                else:
                    ch(last)
                    v.tensor_tensor(dst, dst, pooled[:, 0, :, grp * GB:(grp + 1) * GB], ALU.mult).then_inc(s_pooled, 1)

            def rows(m):
                return [XNf[:, (m * BT + u) * D:(m * BT + u + 1) * D] if isinstance(m, int) else
                        XNf[:, ds(m * BW + u * D, D)] for u in range(BT)]

            def statistics(m, grp, q, nth):
                dve.wait_ge(s_x[q], nth * 16 + (grp * (BPG // 2) * 16 + 16))
                dve.sem_inc(s_vturn, 1)
                for u, row in enumerate(rows(m)):
                    last = v.bn_stats(stats[q][:, u, :], row)
                ch(last)
                dve.sem_inc(s_vturn, 1)
                for u in range(BT):
                    last = v.bn_aggr(meanvar[q][:, u, :], stats[q][:, u, :])
                ch(last)
                v.tensor_scalar(small[:, 16 + 8 * q:16 + 8 * q + BT], meanvar[q][:, :, 1], EPS, None,
                                ALU.add).then_inc(s_var, 1)

            def norm(m, q, w):
                dve.wait_ge(s_nm, m * 3 + (w + 1 + CREDIT))
                dst = wmax[:, w, m:m + 1] if isinstance(m, int) else wmax[:, w, ds(m, 1)]
                v.reduce_max(dst, psNorm[(3 * q + w) % 2][:, 0:F if w < 2 else D], X).then_inc(s_nx, 1)

            def block_steps(i, grp, q, more=True, first=False):
                m = i * 2 + q
                n = m + grp * BPG
                var = small[:, 16 + 8 * q:16 + 8 * q + BT]
                std = small[:, 24 + 8 * q:24 + 8 * q + BT]
                tmp = small[:, 20 + 8 * q:20 + 8 * q + BT]
                dve.wait_ge(s_std, n + 1)
                ch(v.reciprocal(std, std))
                ch(v.scalar_tensor_tensor(tmp, std, -0.5, std, ALU.mult, ALU.mult))
                ch(v.tensor_tensor(tmp, tmp, var, ALU.mult))
                ch(v.scalar_tensor_tensor(std, tmp, 1.5, std, ALU.add, ALU.mult))
                for u, row in enumerate(rows(m)):
                    last = v.tensor_scalar(row, row, meanvar[q][:, u, 0:1], std[:, u:u + 1],
                                           ALU.subtract, ALU.mult)
                last.then_inc(s_xn, 1)
                if more:
                    statistics(m + 1, grp, 1 - q, i + q)
                if not grp and not first:
                    norm(m - 1, 1 - q, 1)
                    norm(m - 1, 1 - q, 2)
                dve.wait_ge(s_hi, n + 1)
                src = XN[:, m * BT:(m + 1) * BT, :] if isinstance(m, int) else XN[:, ds(m * BT, BT), :]
                v.scalar_tensor_tensor(XS[q][:, :, 1, :], src, XSC, XS[q][:, :, 0, :],
                                       ALU.mult, ALU.subtract).then_inc(s_lo, 1)
                if not grp:
                    norm(m, q, 0)

            def blocks(grp, *between):
                statistics(0, grp, 0, 0)
                for q in range(2):
                    block_steps(0, grp, q, first=not q)
                with dve.Fori(0, BPG // 2 - 2) as i:
                    ch.enter(i, 2 * 6)
                    for q in range(2):
                        block_steps(i + 1, grp, q)
                ch.leave(BPG // 2 - 2)
                for q in range(2):
                    if between:
                        between[q]()
                    block_steps(BPG // 2 - 1, grp, q, more=not q)
                if not grp:
                    norm(BPG - 1, 1, 1)
                    norm(BPG - 1, 1, 2)

            blocks(0)

            dve.wait_ge(s_nx, 3 * E + CREDIT)
            v.reduce_max(small[:, 2:3], wmax[:, 0:2, :].rearrange("p m e -> p (m e)"), X)
            ch(v.reduce_max(small[:, 3:4], wmax[:, 2, :], X))
            fe = small[:, 40:48]
            ch(v.tensor_scalar(small_i[:, 0:2], small[:, 2:4].bitcast(i32), 23, None, ALU.logical_shift_right))
            ch(v.tensor_copy(small[:, 10:12], small_i[:, 0:2]))
            v.tensor_scalar(small_i[:, 0:2], small[:, 10:12], -1.0, 409.0, ALU.mult, ALU.add)
            ch(v.tensor_scalar(fe[:, 4:5], small[:, 10:11], -1.0, 259.0, ALU.mult, ALU.add))
            ch(v.tensor_scalar(small_i[:, 0:2], small_i[:, 0:2], 1, None, ALU.logical_shift_right))
            ch(v.tensor_scalar(fe[:, 0:2], small_i[:, 0:2], 200.0, 1.0, ALU.min, ALU.max))
            ch(v.tensor_scalar(fe[:, 4:5], fe[:, 4:5], 200.0, 1.0, ALU.min, ALU.max))
            v.tensor_scalar(fe[:, 2:3], fe[:, 0:1], -1.0, 254.0 - XSC_LOG, ALU.mult, ALU.add)
            v.tensor_scalar(fe[:, 3:4], fe[:, 1:2], -1.0, 254.0, ALU.mult, ALU.add)
            ch(v.tensor_scalar(fe[:, 5:6], fe[:, 4:5], -1.0, 254.0, ALU.mult, ALU.add))
            ch(v.tensor_copy(small_i[:, 0:6], fe[:, 0:6]))
            ch(v.tensor_scalar(sc[:, 0:6].bitcast(i32), small_i[:, 0:6], 23, None, ALU.logical_shift_left))
            v.tensor_tensor(sc[:, 6:7], sc[:, 2:3], sc[:, 4:5], ALU.mult)
            v.tensor_tensor(sc[:, 7:8], sc[:, 3:4], sc[:, 5:6], ALU.mult).then_inc(s_scale, 1)
            dve.wait_ge(s_scale, 1)

            def split(chunks):
                for c in chunks:
                    lo(c)

            taken = small[:, 48:56]
            n_t = small[:, 56:64]
            experts = iotaE[:, :].rearrange("p (e a) -> p e a", a=1).broadcast_to([P, E, NTR])
            resets = notfirst[:, :].rearrange("p (a j) -> p a j", a=1).broadcast_to([P, E, NTR])

            def over_e(ap):
                return ap.rearrange("p e j -> p j e")

            def each_e(ap):
                return ap.rearrange("p (a j) -> p a j", a=1).broadcast_to([P, E, NTR])

            def logits(part):
                dve.wait_ge(s_rt, BPG * (part // 2 + 1) if part != IN_BLOCKS else BPR * (part + 1))
                ch(v.tensor_copy(route[part][0][0], psL[:, part * NTR:(part + 1) * NTR, :].rearrange("p j e -> p e j")))

            def choices(part):
                (L, eq, cand, oh1, oh2, cum, cnt), rf, rc, rci, chosen = route[part]
                own = slice(part * NTR, (part + 1) * NTR)

                def choose(top, oh):
                    ch(v.reduce_max(top, over_e(L), X))
                    ch(v.tensor_tensor(eq, L, each_e(top), ALU.is_equal))
                    ch(v.scalar_tensor_tensor(cand, eq, -float(E), experts, ALU.mult, ALU.add))
                    ch(v.tensor_reduce(rc[2], over_e(cand), X, ALU.min))
                    ch(v.tensor_scalar(rc[2], rc[2], float(E), None, ALU.add))
                    ch(v.tensor_tensor(oh, experts, each_e(rc[2]), ALU.is_equal))

                choose(rc[0], oh1)
                ch(v.scalar_tensor_tensor(L, oh1, FAR, L, ALU.mult, ALU.add))
                choose(rc[1], oh2)
                v.tensor_tensor(imp[:, 1, own], rc[1], rc[0], ALU.subtract).then_inc(s_choice, 1)
                v.tensor_tensor(chosen.rearrange("p (e j) -> p e j", e=E), oh1, oh2, ALU.add).then_inc(s_rank, 1)

            def slots(part):
                (L, eq, slot, oh1, oh2, cum, cnt), rf, rc, rci, chosen = route[part]
                own = slice(part * NTR, (part + 1) * NTR)
                dve.wait_ge(s_rank, 2 * part + 2)
                v.tensor_copy(L, resets)
                ch(v.tensor_copy(cnt, psCnt[part].rearrange("p (e j) -> p e j", e=E)))
                ch(v.tensor_tensor_scan(rf[5], rf[0], rf[6], 0.0, ALU.mult, ALU.add))
                ch(v.tensor_copy(n_t, cum[:, :, NTR - 1]))
                ch(v.tensor_tensor(cum, cum, cnt, ALU.subtract))
                ch(v.tensor_tensor(slot, cum, psRank[part].rearrange("p (e j) -> p e j", e=E), ALU.add))
                if not part:
                    ch(v.tensor_scalar(taken, iotaE[:, :], float(RG), None, ALU.mult))
                ch(v.tensor_tensor(slot, slot, taken.rearrange("p (e a) -> p e a", a=1).broadcast_to([P, E, NTR]),
                                   ALU.add))
                for c, oh in enumerate((oh1, oh2)):
                    ch(v.tensor_tensor(eq, oh, slot, ALU.mult))
                    ch(v.tensor_reduce(rc[c], over_e(eq), X, ALU.add))
                    ch(v.tensor_copy(rci[c], rc[c]))
                    last = v.tensor_copy(rowidx[:, own, c], rci[c].bitcast(u32))
                last.then_inc(s_slots, 1)
                ch(v.tensor_tensor(taken, taken, n_t, ALU.add))

            def choice_weights():
                dve.wait_ge(s_choice, NR + 1)
                ch(v.tensor_scalar(imp[:, 0, :], imp[:, 1, :], 1.0, None, ALU.add))
                ch(v.reciprocal(imp[:, 0, :], imp[:, 0, :]))
                ch(v.tensor_tensor(imp[:, 1, :], imp[:, 0, :], imp[:, 1, :], ALU.mult))

            def tables():
                ends = small[:, 32:40]
                shift, steps = small[:, 16:24], small[:, 24:24 + E - 1]
                ones = small[:, 40:48]
                ch(v.scalar_tensor_tensor(n_t, iotaE[:, :], -float(RG), taken, ALU.mult, ALU.add))
                ch(v.tensor_scalar(small_i[:, 0:E], n_t, float(TS - 1), None, ALU.add))
                ch(v.tensor_scalar(small_i[:, 0:E], small_i[:, 0:E], TS.bit_length() - 1, None,
                                   ALU.logical_shift_right))
                ch(v.tensor_copy(n_t, small_i[:, 0:E]))
                ch(v.memset(ones, 1.0))
                ch(v.tensor_tensor_scan(ends, ones, n_t, 0.0, ALU.mult, ALU.add))
                ch(v.tensor_tensor(shift, ends, n_t, ALU.subtract))
                ch(v.tensor_scalar(shift, shift, float(TS), None, ALU.mult))
                ch(v.scalar_tensor_tensor(shift, iotaE[:, :], -float(RG), shift, ALU.mult, ALU.add))
                v.tensor_tensor(steps, shift[:, 1:E], shift[:, 0:E - 1], ALU.subtract)
                v.tensor_copy(zoff[:, 0:E], taken)
                v.tensor_scalar(zoff[:, E:E + 1], n_t[:, E - 1:E], float(TS), float((E - 1) * RG), ALU.mult, ALU.add)
                ch(v.tensor_scalar(tb[2], iotaT[:, :], ends[:, E - 1:E], float(TS), ALU.min, ALU.mult))
                ch(v.tensor_scalar(n_t, n_t, -float(TS), float(RG), ALU.mult, ALU.add))
                ch(v.tensor_scalar(tb[0], iotaT[:, :], ends[:, 0:1], None, ALU.is_ge))
                ch(v.scalar_tensor_tensor(tb[2], tb[0], n_t[:, 0:1], tb[2], ALU.mult, ALU.add))
                for e in range(1, E - 1):
                    ch(v.tensor_scalar(tb[1], iotaT[:, :], ends[:, e:e + 1], None, ALU.is_ge))
                    v.tensor_tensor(tb[0], tb[0], tb[1], ALU.add)
                    ch(v.scalar_tensor_tensor(tb[2], tb[1], n_t[:, e:e + 1], tb[2], ALU.mult, ALU.add))
                v.tensor_scalar(woff[:, :], tb[0], float(3 * 2 * CH), None, ALU.mult)
                v.tensor_copy(rowoff[:, :], tb[2]).then_inc(s_tables, 1)

            dve.wait_ge(s_cl, 16 * LOADS)
            dve.wait_ge(s_cm, 2)
            attention(0, lambda: (logits(0), choices(0), split(SPLITS[0][0])), lambda: (slots(0), split(SPLITS[0][1])))
            attention(1, lambda: (logits(1), choices(1), split(SPLITS[1][0])), lambda: (slots(1), split(SPLITS[1][1])))
            blocks(1, lambda: (logits(IN_BLOCKS), choices(IN_BLOCKS)), lambda: slots(IN_BLOCKS))
            logits(NR - 1)
            attention(2, lambda: (choices(NR - 1), split(SPLITS[2][0])),
                      lambda: (slots(NR - 1), split(SPLITS[2][1])))
            attention(3, lambda: split(SPLITS[3][0]), lambda: (tables(), choice_weights(), split(SPLITS[3][1])))

            dve.wait_ge(s_tl, 16 * 3)
            dve.wait_ge(s_pooled, 2 * NG)
            for c in range(KC):
                last = v.tensor_scalar(bqk[:, c, :], pooled[:, 1, c, :], bcol[:, 0, c:c + 1], None, ALU.mult)
            last.then_inc(s_bq, 1)
            ch(v.tensor_tensor(brow[0:B, 0, :], brow[0:B, 0, :], brow[0:B, 1, :], ALU.add))
            for b in range(B + 1):
                if b < B:
                    for c in range(KC):
                        last = v.tensor_scalar(WTP[b % 2][:, c, :], Wt[:, c, :], pooled[:, 1, c, b:b + 1], None,
                                               ALU.mult)
                    last.then_inc(s_wtp, 1)
                if b:
                    dve.wait_ge(s_eff, b)
                    v.tensor_tensor(WE[:, b - 1], psEff[(b - 1) % 2], Wq[:, :, :], ALU.add).then_inc(s_we, 1)
            dve.wait_ge(s_be, 1)
            v.tensor_tensor(be8[0:B, :], psBe, brow[0:B, 0, :], ALU.add).then_inc(s_be8, 1)

            shift, steps = small[:, 16:24], small[:, 24:24 + E - 1]
            of_y, past, beyond = (view(AT, n * 2 * NT, [2 * NT]) for n in range(3))
            both = rowidx[:, :, :].rearrange("p j c -> p (j c)")
            ch(v.tensor_copy(past, both.bitcast(i32)))
            ch(v.tensor_scalar(of_y, past, shift[:, 0:1], None, ALU.add))
            for e in range(1, E):
                ch(v.tensor_scalar(beyond, past, float(e * RG), steps[:, e - 1:e], ALU.is_ge, ALU.mult))
                ch(v.tensor_tensor(of_y, of_y, beyond, ALU.add))
            ch(v.tensor_copy(past.bitcast(i32), of_y))
            for q in range(2):
                dve.wait_ge(s_sct[q], NB // 2 * (2 * BT * 16))
            v.tensor_copy(both, past.bitcast(u32)).then_inc(s_slots, 1)

            def hidden(t, q):
                for h in range(2):
                    dve.wait_ge(s_sg, t * 2 + (h + 1))
                    v.scalar_tensor_tensor(SG[:, 2 * h:2 * h + 2, :], PS[:, 2 * h:2 * h + 2, TS:2 * TS],
                                           sc[:, 6:7], SG[:, 2 * h:2 * h + 2, :], ALU.mult, ALU.mult
                                           ).then_inc(s_h, 1)
                for h in range(2):
                    dve.wait_ge(s_hh, t * 2 + (h + 1))
                    v.tensor_tensor(HH[q][:, 1, 2 * h:2 * h + 2, :], SG[:, 2 * h:2 * h + 2, :],
                                    HH[q][:, 0, 2 * h:2 * h + 2, :], ALU.subtract).then_inc(s_hl, 1)

            with dve.Fori(0, NS // 2) as i:
                hidden(i * 2, 0)
                hidden(i * 2 + 1, 1)
            hidden(NS - 1, 0)

            def batch(b, more=True):
                def ffn(u):
                    j = b * TPB + u
                    q = u % TQ
                    w = imp[:, 1, j:j + 1] if isinstance(j, int) else imp[:, 1, ds(j, 1)]
                    dve.wait_ge(s_fa, j + 1)
                    v.scalar_tensor_tensor(FF[q], YG[u % TY][1], w, FF[q], ALU.mult, ALU.add).then_inc(s_f, 1)

                def result(u):
                    j = b * TPB + u
                    q = u % TQ
                    dve.wait_ge(s_s, j + 1)
                    dve.wait_ge(s_ofree, j + 1)
                    bias = BE[:, b, :] if isinstance(b, int) else BE[:, ds(b, 1), :].rearrange("p a n -> p (a n)")
                    ch(v.tensor_tensor(OB[q], psAtt[q], bias, ALU.add))
                    dve.wait_ge(s_sf, j + 1)
                    ch(v.tensor_tensor(OB[q], OB[q], SF[q], ALU.mult))
                    dve.wait_ge(s_tx[q], b * (32 * TPB // TQ) + (32 * (u // TQ) + 32))
                    v.tensor_tensor(OB[q], OB[q], XR[q], ALU.add).then_inc(s_o, 1)

                if isinstance(b, int) and b == 0:
                    return ffn(0)
                for u in range(TPB):
                    if more or u < TPB - 1:
                        ffn(u + 1)
                    result(u)

            dve.wait_ge(s_beld, 16)
            batch(0)
            with dve.Fori(0, B - 1) as b:
                ch.enter(b, 2 * TPB)
                batch(b)
            ch.leave(B - 1)
            batch(B - 1, more=False)

        @block.tensor
        def _(pe):
            t_ = nc.tensor
            pe.wait_ge(s_cl, 16 * LOADS)
            pe.wait_ge(s_cm, 2)
            for m, W in enumerate((Wq, Wk)):
                for hc in range(KC):
                    for kc in range(KC):
                        last = t_.transpose(psT[m][:, hc * KC + kc, :], W[:, kc, hc * P:(hc + 1) * P], identf[:, :])
                last.then_inc(s_wT, 1)
            pe.wait_ge(s_wTc, 2)

            def attention(n, after_scores=lambda: None):
                grp, k = n // 2, n % 2
                W, WT = ((Wq, WqT), (Wk, WkT))[k]
                WAf = WA.rearrange("p c b h -> p c (b h)")
                pe.wait_ge(s_wa, n + 1)
                for dc in range(KC):
                    for hc in range(KC):
                        t_.matmul(psX[:, dc * P:(dc + 1) * P], WT[:, hc, dc * P:(dc + 1) * P], WAf[:, hc, :],
                                  start=hc == 0, stop=hc == KC - 1)
                for hc in range(KC):
                    last = t_.matmul(psX[:, 500:501], WAf[:, hc, :], bcol[:, k, hc:hc + 1],
                                     start=hc == 0, stop=hc == KC - 1)
                last.then_inc(s_A, 1)
                pe.wait_ge(s_Ac, n + 1)
                pe.wait_ge(s_xtb, BPG * (grp + 1))
                for hf in range(2):
                    for kc in range(KC):
                        for b in range(GB):
                            n0 = b * TPB + hf * BT
                            last = t_.matmul(psS[HP * b:HP * (b + 1), hf, :], A[:, kc, HP * b:HP * (b + 1)],
                                             XT4[:, n0:n0 + BT, kc, :], start=kc == 0, stop=kc == KC - 1)
                last.then_inc(s_sc, 1)
                after_scores()
                pe.wait_ge(s_ex, n + 1)
                for j in range(TPB):
                    last = t_.transpose(psT[0][:, j, :], PR[:, j * P:(j + 1) * P], identf[:, :])
                last.then_inc(s_pt, 1)
                pe.wait_ge(s_ptc, n + 1)
                for j in range(TPB):
                    for b in range(GB):
                        last = t_.matmul(psX[HP * b:HP * (b + 1), 0:D], PT[:, j, HP * b:HP * (b + 1)],
                                         XN[:, b * TPB + j, :], start=j == 0, stop=j == TPB - 1)
                last.then_inc(s_px, 1)
                pe.wait_ge(s_pxn, n + 1)
                for kc in range(KC):
                    last = t_.transpose(psX[:, D + kc * P:D + (kc + 1) * P], pxn[:, kc * P:(kc + 1) * P],
                                        identf[:, :])
                last.then_inc(s_pxt, 1)
                pe.wait_ge(s_pxtc, n + 1)
                for hc in range(KC):
                    for kc in range(KC):
                        last = t_.matmul(psTf[1][:, hc * P:(hc + 1) * P], W[:, kc, hc * P:(hc + 1) * P],
                                         pxT[:, kc, :], start=kc == 0, stop=kc == KC - 1)
                last.then_inc(s_pv, 1)

            def transpose(n, q):
                pe.wait_ge(s_lo, n + 1)
                for u in range(BT):
                    for kc in range(KC):
                        for hl in range(2):
                            last = t_.matmul(psT[q][:, u * KC + kc, :], XS[q][:, u, hl, kc * P:(kc + 1) * P],
                                             identh[:, :], start=hl == 0, stop=hl == 1)
                last.then_inc(s_tr, 1)

            def norms(m, q, ws):
                for w in ws:
                    r = (3 * q + w) % 2
                    width, parts = (F, KC) if w < 2 else (D, FC)
                    pe.wait_ge(s_sq, m * 3 + (w + 1))
                    pe.wait_ge(s_nx, m * 3 + (w + 1))
                    for c in range(parts):
                        last = t_.matmul(psNorm[r][:, 0:width], onesb[:, :], SQ[r][:, c * width:(c + 1) * width],
                                         start=c == 0, stop=c == parts - 1)
                    last.then_inc(s_nm, 1)

            def router(n, q):
                pe.wait_ge(s_xtb, n + 1)
                for u in range(BT):
                    j = n * BT + u
                    dst = psL[:, j, :] if isinstance(j, int) else psL[:, ds(j, 1), :]
                    for kc in range(KC):
                        last = t_.matmul(dst, XTB[q][:, u, kc, :], rw[:, kc, :], start=kc == 0, stop=kc == KC - 1)
                last.then_inc(s_rt, 1)

            def ranks(part):
                chosen = route[part][4]
                pe.wait_ge(s_rank, 2 * part + 1)
                t_.matmul(psRank[part], before[:, :], chosen, start=True, stop=True)
                t_.matmul(psCnt[part], onesb[:, :], chosen, start=True, stop=True).then_inc(s_rank, 1)

            def blocks(grp):
                def step(i, q, first=False):
                    n = i * 2 + (q + grp * BPG)
                    if not grp:
                        norms(n, q, (0,))
                    transpose(n, q)
                    if not grp:
                        norms(n, q, (1,))
                    if not first:
                        router(n - 1, 1 - q)
                    if not grp:
                        norms(n, q, (2,))

                step(0, 0, True)
                step(0, 1)
                with pe.Fori(0, BPG // 2 - 2) as i:
                    for q in range(2):
                        step(i + 1, q)
                if grp == NG - 1:
                    ranks(IN_BLOCKS)
                step(BPG // 2 - 1, 0)
                step(BPG // 2 - 1, 1)
                router((grp + 1) * BPG - 1, 1)


            blocks(0)
            attention(0, lambda: ranks(0))
            pe.wait_ge(s_pooled, 1)
            attention(1, lambda: ranks(1))
            pe.wait_ge(s_pooled, 2)
            blocks(1)
            attention(2, lambda: ranks(NR - 1))
            pe.wait_ge(s_pooled, 3)
            attention(3)

            pe.wait_ge(s_pooled, 4)
            pe.wait_ge(s_bq, 1)
            for b in range(B):
                pe.wait_ge(s_wtp, b + 1)
                if b >= 2:
                    pe.wait_ge(s_we, b - 1)
                for dc in range(KC):
                    for hc in range(KC):
                        last = t_.matmul(psEff[b % 2][:, dc, :], WqT[:, hc, dc * P:(dc + 1) * P], WTP[b % 2][:, hc, :],
                                         start=hc == 0, stop=hc == KC - 1)
                last.then_inc(s_eff, 1)
            for hc in range(KC):
                last = t_.matmul(psBe, bqk[:, hc, :], Wt[:, hc, :], start=hc == 0, stop=hc == KC - 1)
            last.then_inc(s_be, 1)

            pe.wait_ge(s_tables, 1)
            pe.wait_ge(s_we, B)
            pe.wait_ge(s_be8, 1)
            pe.wait_ge(s_wlo, 2 * NCH)
            WMAX = (E - 1) * 3 * 2 * CH

            def offset(t):
                src = woff[0:1, t:t + 1] if isinstance(t, int) else woff[0:1, ds(t, 1)]
                return pe.value_load(src, min_val=0, max_val=WMAX)

            def transposes(t, q, nth):
                pe.wait_ge(s_g[q], nth * 16 + 16)
                for s in range(SUB):
                    for c in range(2 * KC):
                        last = t_.transpose(psXG[:, q, c, s * P:(s + 1) * P], GX[q][s][:, c // KC, c % KC, :],
                                            identh[:, :])
                last.then_inc(s_xgt, 1)

            def gate_up(t, q):
                w = offset(t)
                pe.wait_ge(s_xg, t + 1)
                for h in range(2):
                    if not (isinstance(t, int) and t == 0):
                        pe.wait_ge(s_h, t * 2 + (h - 1))
                    for f in range(2 * h, 2 * h + 2):
                        for m in range(2):
                            n = 0
                            for kc in range(KC):
                                for wl, xl in ((0, 0), (0, 1), (1, 0)):
                                    at = m * 2 * CH + wl * CH + kc * F + f * P
                                    last = t_.matmul(psGU[f][:, m, :], WR[:, ds(w + at, P)], XG[q][:, xl, kc, :],
                                                     start=n == 0, stop=n == 3 * KC - 1)
                                    n += 1
                    last.then_inc(s_gu, 1)

            def down(t, q):
                w = offset(t)
                pe.wait_ge(s_hl, t * 2 + 2)
                pe.wait_ge(s_yb, t + 1)
                for s in range(SUB):
                    n = 0
                    for f in range(FC):
                        for hl, wl in ((0, 0), (0, 1), (1, 0)):
                            at = 2 * 2 * CH + wl * CH + f * D
                            last = t_.matmul(psY[:, q, s, :], HH[q][:, hl, f, s * P:(s + 1) * P],
                                             WR[:, ds(w + at, D)], start=n == 0, stop=n == 3 * FC - 1)
                            n += 1
                last.then_inc(s_y, 1)

            transposes(0, 0, 0)
            transposes(1, 1, 0)
            gate_up(0, 0)
            with pe.Fori(0, (NS - 3) // 2) as i:
                for q in range(2):
                    t = i * 2 + 1 + q
                    transposes(t + 1, q, i + 1)
                    gate_up(t, 1 - q)
                    down(t - 1, q)
            t = NS - 2
            transposes(t + 1, 0, (NS - 1) // 2)
            gate_up(t, 1)
            down(t - 1, 0)
            gate_up(t + 1, 0)
            down(t, 1)
            down(t + 1, 0)

            with pe.Fori(0, B) as b:
                for u in range(TPB):
                    q = u % TQ
                    pe.wait_ge(s_tx[q], b * (32 * TPB // TQ) + (32 * (u // TQ) + 32))
                    pe.wait_ge(s_o, b * TPB + (u + 1))
                    for kc in range(KC):
                        last = t_.matmul(psAtt[q], XC[q][:, kc, :], WE[:, ds(b, 1), kc, :],
                                         start=kc == 0, stop=kc == KC - 1)
                    last.then_inc(s_s, 1)


_INS = ['L0_attn_hidden_states', 'L0_attn_Wq', 'L0_attn_bq', 'L0_attn_Wqa', 'L0_attn_bqa', 'L0_attn_Wk', 'L0_attn_bk',
        'L0_attn_Wka', 'L0_attn_bka', 'L0_attn_Wt', 'L0_attn_bt', 'L0_ffn_router_w', 'L0_ffn_w1', 'L0_ffn_w3',
        'L0_ffn_w2']


def kernel(**inputs):
    import numpy as _np
    import concourse.bacc as _bacc
    from concourse import mybir as _mybir
    from concourse.bass_utils import run_bass_kernel_spmd as _run

    nc = _bacc.Bacc("TRN2", target_bir_lowering=False, num_devices=1)
    arrays, args = {}, []
    for name in _INS:
        a = _np.ascontiguousarray(inputs[name])
        arrays[f"in_{name}_dram"] = a
        args.append(nc.dram_tensor(f"in_{name}_dram", a.shape, _mybir.dt.from_np(a.dtype), kind="ExternalInput").ap())
    shape = inputs[_INS[0]].shape
    args.append(nc.dram_tensor("out_0_dram", shape, _mybir.dt.float32, kind="ExternalOutput").ap())
    recurrent_attention_moe(nc, *args)
    r = _run(nc, [arrays], core_ids=[0])
    return r.results[0]["out_0_dram"]
```

```python
import concourse.bass as bass
from concourse import mybir
from contextlib import ExitStack


def recurrent_attention_moe(
    nc: bass.Bass,
    x_in: bass.AP,
    Wq_in: bass.AP,
    bq_in: bass.AP,
    Wqa_in: bass.AP,
    bqa_in: bass.AP,
    Wk_in: bass.AP,
    bk_in: bass.AP,
    Wka_in: bass.AP,
    bka_in: bass.AP,
    Wt_in: bass.AP,
    bt_in: bass.AP,
    router_in: bass.AP,
    w1_in: bass.AP,
    w3_in: bass.AP,
    w2_in: bass.AP,
    out: bass.AP,
):
    fp32 = mybir.dt.float32
    fp16 = mybir.dt.float16
    bf16 = mybir.dt.bfloat16
    i32 = mybir.dt.int32
    u32 = mybir.dt.uint32
    ALU = mybir.AluOpType
    ACT = mybir.ActivationFunctionType
    X = mybir.AxisListType.X
    ds = bass.ds

    P = 128
    B, S, D = x_in.shape
    H = bqa_in.shape[0]
    DH = D // H
    E, _, F = w1_in.shape
    T = B * S
    NT = T // P
    KC = D // P
    FC = F // P
    BT = 4
    NB = NT // BT
    GB = 4
    NG = B // GB
    BPG = NB // NG
    TPB = S // P
    HP = P // GB
    TS = 256
    SUB = TS // P
    NS = 2 * T // TS + E - 1
    RG = T + TS
    NR = 2 * NG
    BPR = NB // NR
    NTR = NT // NR
    EPS = 1e-5
    SCALE = float(DH) ** -0.5
    XSC = 1024.0
    XSC_LOG = 10
    CH = KC * F
    assert CH == FC * D and NS % 2 == 1 and E == BPG
    NCH = 3 * E
    LOADS = 2 + 1 + 2 * KC + 2 + 2 * GB
    FAR = -3.0e38
    RAW = 6224
    CREDIT = 2
    TQ = 4
    assert TPB == 2 * TQ
    ROW = 2 * D + 4
    SHARES = ((1, 3), (4, 4), (2, 3), (4, 3))
    SPLITS, at = [], 0
    for shares in SHARES:
        SPLITS.append([range(at, at + shares[0]), range(at + shares[0], at + sum(shares))])
        at += sum(shares)
    assert at == NCH

    x_t = x_in.rearrange("b s d -> (b s) d").rearrange("(n p) d -> p n d", p=P)
    out_t = out.rearrange("b s d -> (b s) d").rearrange("(n p) d -> p n d", p=P)
    xs_dram = nc.dram_tensor("xs_dram", (T, 2 * D), fp16).ap()
    sorted_dram = nc.dram_tensor("sorted_dram", (E * RG, ROW), fp16).ap()
    y_dram = nc.dram_tensor("y_dram", (2 * T + TS, D), fp32).ap()
    be_dram = nc.dram_tensor("be_dram", (B, D), fp32).ap()
    y_t = y_dram.rearrange("(n p) d -> p n d", p=P)
    assert NT + 2 * NT + SUB <= 2048
    xt_dram = nc.dram_tensor("xt_dram", (T, D), fp32).ap()
    xt_t = xt_dram.rearrange("(n p) d -> p n d", p=P)
    xs_t = xs_dram.rearrange("(n p) d -> p n d", p=P)

    ctx = ExitStack()
    with ctx:
        def sb(name, shape, dt):
            return ctx.enter_context(nc.sbuf_tensor(name, shape, dt))

        def sem(name):
            return ctx.enter_context(nc.semaphore(name))

        WR = sb("weights", [P, (NCH + 1) * 2 * CH], fp16)
        XX = sb("xn_both_ways", [P, 2 * BPG * BT * D], fp32)
        RA = sb("work", [P, RAW], fp32)
        AT = sb("attention_work", [P, 6 * D], fp32)
        Wq = sb("Wq", [P, KC, D], fp32)
        Wk = sb("Wk", [P, KC, D], fp32)
        WqT = sb("WqT", [P, KC, D], fp32)
        WkT = sb("WkT", [P, KC, D], fp32)
        identf = sb("identf", [P, P], fp32)
        identh = sb("identh", [P, P], fp16)
        before = sb("before", [P, P], bf16)
        meta = sb("meta", [P, NT, 4], fp16)
        onesb = sb("onesb", [P, P], bf16)
        headmask = sb("headmask", [P, KC, HP], fp32)
        Wqa = sb("Wqa", [P, KC, HP], fp32)
        Wka = sb("Wka", [P, KC, HP], fp32)
        rw = sb("rw", [P, KC, E], fp32)
        bcol = sb("bcol", [P, 2, KC], fp32)
        sbias = sb("sbias", [P, 2], fp32)
        pooled = sb("pooled", [P, 2, KC, B], fp32)
        sc = sb("sc", [P, 8], fp32)
        gcol = sb("gcol", [P, 2 * BT, 2], u32)
        small = sb("small", [P, 64], fp32)
        small_i = sb("small_i", [P, 16], i32)
        wmax = sb("wmax", [P, 3, E], fp32)
        rowidx = sb("rowidx", [P, NT, 2], u32)
        imp = sb("imp", [P, 2, NT], fp32)
        woff = sb("woff", [P, NS], i32)
        rowoff = sb("rowoff", [P, NS], i32)
        zoff = sb("zoff", [P, E + 1], i32)
        iotaT = sb("iotaT", [P, NS], fp32)
        idxf = sb("idxf", [P, 2, SUB], fp32)
        iotaE = sb("iotaE", [P, E], fp32)
        notfirst = sb("notfirst", [P, NTR], fp32)

        def view(region, at, shape, dt=fp32):
            n = 1
            for s in shape:
                n *= s
            size = {fp16: 2, bf16: 2}.get(dt, 4)
            v = region[:, at:at + n * size // 4]
            if dt != fp32:
                v = v.bitcast(dt)
            if len(shape) == 1:
                return v
            names = "abcd"[:len(shape)]
            kw = {c: s for c, s in zip(names[1:], shape[1:])}
            return v.rearrange("p (" + " ".join(names) + ") -> p " + " ".join(names), **kw)

        def weight_view(chunk):
            return WR[:, (chunk + 1) * 2 * CH:(chunk + 2) * 2 * CH].bitcast(fp32)

        XN = view(XX, 0, [BPG * BT, D])
        XNf = view(XX, 0, [BPG * BT * D])
        XT = view(XX, BPG * BT * D, [BPG * BT * KC * P])
        itemp = view(XX, BPG * BT * D, [NS], i32)
        jtemp = view(XX, BPG * BT * D + P, [NT, 1], i32)
        XTt = view(XX, BPG * BT * D, [BPG * BT, D])
        XT4 = view(XX, BPG * BT * D, [BPG * BT, KC, P])
        PR = view(AT, 0, [S])
        PT = view(AT, 0, [TPB, P])
        WA = view(AT, S, [KC, GB, HP])
        pxn = view(AT, S, [D])
        A = view(AT, S + D, [KC, P])
        pxT = view(AT, S + D, [KC, P])
        SQ = [view(AT, q * CH // 2, [CH], bf16) for q in range(2)]
        assert S == CH == 4 * D

        BW = BT * D
        XS = [view(RA, q * BW, [BT, 2, D], fp16) for q in range(2)]
        XTB = [view(RA, 2 * BW + q * BW, [BT, KC, P]) for q in range(2)]
        EJ = E * NTR
        IN_BLOCKS = NR - 2
        at_routing = [AT if part == IN_BLOCKS else RA[:, 2 * BW:4 * BW] for part in range(NR)]
        route = [([view(reg, n * EJ, [E, NTR]) for n in range(7)],
                  [view(reg, n * EJ, [EJ]) for n in range(7)],
                  [view(reg, 7 * EJ + n * NTR, [NTR]) for n in range(4)],
                  [view(reg, 7 * EJ + (4 + n) * NTR, [NTR], i32) for n in range(2)],
                  view(reg, 8 * EJ, [EJ], bf16)) for reg in at_routing]
        tb = [view(RA, 2 * BW + 9 * EJ + n * NS, [NS]) for n in range(3)]
        assert 6 * NTR <= EJ and 9 * EJ + 3 * NS <= 2 * BW - SUB * ROW // 2 and 9 * EJ <= 6 * D and 2 * EJ <= 512
        past = view(RA, 0, [NS, E - 1])
        zrow = view(RA, 4 * BW - SUB * ROW // 2, [SUB, ROW], fp16)
        o = 4 * BW
        SCW = BT * ROW // 2
        SC = [view(RA, o + q * SCW, [BT, ROW], fp16) for q in range(2)]
        stats = [view(RA, o + 2 * SCW + 32 * q, [BT, 6]) for q in range(2)]
        meanvar = [view(RA, o + 2 * SCW + 32 * q + 24, [BT, 2]) for q in range(2)]
        assert o + 2 * SCW + 64 <= RAW
        assert SUB == 2
        GXf = [view(XX, q * ROW, [SUB, ROW], fp16) for q in range(2)]
        GX = [[GXf[q][:, s, 0:2 * D].rearrange("p (c k n) -> p c k n", c=2, k=KC) for s in range(SUB)]
              for q in range(2)]
        XG = [view(XX, 2 * ROW + q * 2 * TS, [2, KC, TS], fp16) for q in range(2)]
        o = 2 * ROW + 4 * TS
        SG = view(XX, o, [FC, TS])
        HH = [view(XX, o + (1 + q) * FC * TS, [2, FC, TS], fp16) for q in range(2)]
        oy = o + 3 * FC * TS
        YB = [view(XX, oy + q * SUB * D, [SUB, D]) for q in range(2)]
        ot = oy + 2 * SUB * D
        TH = range(TQ)
        YG = [view(XX, h * 4 * D, [2, 2, D]) for h in TH]
        OB = [view(XX, (4 * TQ + h * 2) * D, [2, D]) for h in TH]
        XR = [view(XX, ot + h * 2 * D, [2, D]) for h in TH]
        XC = [view(XX, ot + (2 * TQ + h * 2) * D, [2, KC, P]) for h in TH]
        assert 6 * TQ * D <= ot and 4 * TQ * D <= 16 * D
        of = ot + 16 * D
        assert of >= BPG * BT * D
        BE = view(XX, of, [B, D])
        Wt = view(XX, of + B * D, [KC, D])
        WTP = [view(XX, of + (B + 2 + 2 * q) * D, [KC, D]) for q in range(2)]
        brow = view(XX, of + (B + 6) * D, [2, D])
        bqk = view(XX, of + (B + 8) * D, [KC, B])
        be8 = view(XX, of + (B + 9) * D, [D])
        assert of + (B + 10) * D <= 2 * BPG * BT * D and KC * B <= D
        WE = view(RA, 0, [B, KC, D])
        assert B * KC * D <= 4 * BW
        FF = [view(RA, 4 * BW + q * D, [D]) for q in range(TQ)]
        SF = [view(RA, 4 * BW + (TQ + q) * D, [D]) for q in range(TQ)]
        assert 2 * TQ * D <= 2 * SCW

        PS = ctx.enter_context(nc.psum_tensor("PS", [P, 8, 512], fp32))
        psT = [PS[:, 2 * q:2 * q + 2, :].rearrange("p b (u t) -> p (b u) t", t=P) for q in range(2)]
        psTf = [PS[:, 2 * q:2 * q + 2, :].rearrange("p b n -> p (b n)") for q in range(2)]
        psS = PS[:, 4:6, :]
        psW = PS[:, 7, :]
        psX = PS[:, 7, :]
        logits_at = 7 * 512 - (NR - 1) * NTR * E
        assert logits_at >= 6 * 512
        psL = PS[:, :, :].rearrange("p b n -> p (b n)")[:, logits_at:logits_at + NT * E].rearrange(
            "p (n e) -> p n e", e=E)
        bank = [5 if part == IN_BLOCKS else 2 for part in range(NR)]
        psRank = [PS[:, n, 0:EJ] for n in bank]
        psCnt = [PS[:, n, EJ:2 * EJ] for n in bank]
        psGU = [PS[:, f, :].rearrange("p (m t) -> p m t", m=2) for f in range(FC)]
        psXG = PS[:, 4:6, :].bitcast(fp16).rearrange("p b (c t) -> p b c t", t=TS)
        psY = PS[:, 6:8, :].rearrange("p b (s d) -> p b s d", d=D)
        psNorm = [PS[:, 4 + q, :] for q in range(2)]
        psAtt = [PS[:, q, 0:D] for q in range(TQ)]
        psEff = [PS[:, q, :].rearrange("p (c n) -> p c n", c=KC) for q in range(2)]
        psBe = PS[0:B, 2, 0:D]

        s_cl = sem("constants_loaded")
        s_cm = sem("constants_made")
        s_pc = sem("pool_chain")
        s_dc = sem("vector_chain")
        s_ac = sem("scalar_chain")
        s_turn = sem("pool_turn")
        s_vturn = sem("vector_turn")
        s_x = [sem(f"x_loaded{q}") for q in range(2)]
        s_var = sem("variance_ready")
        s_std = sem("std_ready")
        s_xn = sem("xn_ready")
        s_hi = sem("xn_hi_ready")
        s_lo = sem("xn_lo_ready")
        s_xsst = [sem(f"xn_halves_stored{q}") for q in range(2)]
        s_xsfree = sem("xn_halves_free")
        s_tr = sem("xn_transposed")
        s_xtb = sem("xnT_block_ready")
        s_kept = sem("xnT_kept")
        s_rt = sem("router_done")
        s_wT = sem("weight_transposed")
        s_wTc = sem("weight_transpose_copied")
        s_wa = sem("score_weights_scaled")
        s_A = sem("score_fold_done")
        s_Ac = sem("score_fold_copied")
        s_sc = sem("scores_done")
        s_mx = sem("score_max_ready")
        s_ex = sem("probs_ready")
        s_pt = sem("probs_transposed")
        s_ptc = sem("probs_transpose_copied")
        s_px = sem("weighted_xn_done")
        s_pxn = sem("weighted_xn_scaled")
        s_pxt = sem("weighted_xn_transposed")
        s_pxtc = sem("weighted_xn_transpose_copied")
        s_pv = sem("pooled_done")
        s_pooled = sem("pooled_ready")
        s_w = [sem(f"weights_loaded{q}") for q in range(2)]
        s_sq = sem("weight_squares_ready")
        s_nm = sem("weight_norms_done")
        s_nx = sem("weight_norm_max_ready")
        s_scale = sem("scales_ready")
        s_whi = sem("weight_hi_ready")
        s_wlo = sem("weight_lo_ready")
        s_choice = sem("choices_ready")
        s_rank = sem("ranks_done")
        s_slots = sem("slots_ready")
        s_tables = sem("tile_tables_ready")
        s_scl = [sem(f"halves_loaded{q}") for q in range(2)]
        s_sct = [sem(f"halves_scattered{q}") for q in range(2)]
        s_zero = sem("zeros_stored")
        s_col = sem("index_column_ready")
        s_g = [sem(f"gathered{q}") for q in range(2)]
        s_xgt = sem("gather_transposed")
        s_xg = sem("gather_transpose_copied")
        s_gu = sem("gate_up_done")
        s_sg = sem("silu_ready")
        s_h = sem("hidden_ready")
        s_hh = sem("hidden_hi_ready")
        s_hl = sem("hidden_lo_ready")
        s_y = sem("expert_out_done")
        s_yb = sem("expert_out_copied")
        s_yst = sem("expert_out_stored")
        s_yfree = sem("expert_out_free")
        s_wtp = sem("out_weights_scaled")
        s_eff = sem("out_weights_folded")
        s_we = sem("out_weights_ready")
        s_idx = sem("result_rows_ready")
        s_yc = sem("result_columns_ready")
        s_tl = sem("out_weights_loaded")
        s_bq = sem("bias_products_ready")
        s_be = sem("bias_sums_done")
        s_be8 = sem("biases_ready")
        s_best = sem("biases_stored")
        s_beld = sem("biases_spread")
        s_fa = sem("first_expert_weighted")
        s_tx = [sem(f"tail_x_loaded{q}") for q in range(TQ)]
        s_xtst = sem("xnT_stored")
        s_s = sem("attention_out_done")
        s_f = sem("ffn_out_ready")
        s_sf = sem("gate_ready")
        s_o = sem("out_ready")
        s_ost = [sem(f"out_stored{q}") for q in range(TQ)]
        s_ofree = sem("out_free")

        block = ctx.enter_context(nc.Block())

        class Chain:

            def __init__(self, eng, s):
                self.eng, self.s, self.n, self.off = eng, s, 0, None

            def __call__(self, ins):
                ins.then_inc(self.s, 1)
                self.n += 1
                self.eng.wait_ge(self.s, self.n if self.off is None else self.off + self.n)

            def enter(self, turn, steps):
                self.off, self.steps, self.at = turn * steps, steps, self.n

            def leave(self, turns):
                assert self.n - self.at == self.steps, (self.n - self.at, self.steps)
                self.n, self.off = self.at + self.steps * turns, None

        @block.sync
        def _(sp):
            def load_constants():
                for dst, src in ((Wq, Wq_in), (Wk, Wk_in)):
                    sp.dma_start(dst[:, :, :], src.rearrange("(c p) n -> p c n", p=P)).then_inc(s_cl, 16)
                sp.dma_start(rw[:, :, :], router_in.rearrange("(c p) n -> p c n", p=P)).then_inc(s_cl, 16)
                for m, src in enumerate((bq_in, bk_in)):
                    for c in range(KC):
                        sp.dma_start(bcol[:, m, c:c + 1], src[c * P:(c + 1) * P].rearrange("(p a) -> p a", a=1)
                                     ).then_inc(s_cl, 16)
                sp.wait_ge(s_cm, 1)
                for dst, src in ((Wqa, Wqa_in), (Wka, Wka_in)):
                    sp.dma_start(dst[:, :, 0:H], src.rearrange("(c p) n -> p c n", p=P)).then_inc(s_cl, 16)
                for m, src in enumerate((bqa_in, bka_in)):
                    for b in range(GB):
                        sp.dma_start(sbias[HP * b:HP * b + H, m:m + 1],
                                     src.rearrange("(n a) -> n a", a=1)).then_inc(s_cl, 16)

            def rows(ap, n, tiles=BT):
                return ap[:, n * tiles:(n + 1) * tiles, :] if isinstance(n, int) else ap[:, ds(n * tiles, tiles), :]

            def load_block(m, grp, q):
                sp.dma_start(rows(XN, m), rows(x_t, m + grp * BPG)).then_inc(s_x[q], 16)

            def store_block(i, grp, q, more):
                m = i * 2 + q
                sp.wait_ge(s_lo, m + (grp * BPG + 1))
                sp.dma_start(rows(xs_t, m + grp * BPG), XS[q].rearrange("p u c d -> p u (c d)")
                             ).then_inc(s_xsst[q], 16)
                if more:
                    load_block(m + 3, grp, 1 - q)
                sp.wait_ge(s_xsst[q], i * 16 + (grp * (BPG // 2) * 16 + 16))
                sp.sem_inc(s_xsfree, 1)

            def store_blocks(grp):
                sp.wait_ge(s_x[0], grp * (BPG // 2) * 16 + 16)
                load_block(2, grp, 0)
                with sp.Fori(0, BPG // 2 - 2) as i:
                    for q in range(2):
                        store_block(i, grp, q, True)
                store_block(BPG // 2 - 2, grp, 0, True)
                store_block(BPG // 2 - 2, grp, 1, False)
                for q in range(2):
                    store_block(BPG // 2 - 1, grp, q, False)

            def load_halves(i, q, first=False):
                if not first:
                    sp.wait_ge(s_sct[q], i * (2 * BT * 16))
                sp.dma_start(SC[q][:, :, 0:2 * D], rows(xs_t, i * 2 + q)).then_inc(s_scl[q], 16)

            load_block(0, 0, 0)
            load_block(1, 0, 1)
            load_constants()
            def store_transposes(grp, i):
                sp.dma_start(rows(xt_t, i + grp * (BPG // 2), 2 * BT), rows(XTt, i, 2 * BT)).then_inc(s_xtst, 16)

            store_blocks(0)
            for q in range(2):
                load_halves(0, q, True)
            sp.wait_ge(s_kept, BPG)
            with sp.Fori(0, BPG // 2) as i:
                store_transposes(0, i)
            with sp.Fori(0, BPG // 2 - 2) as i:
                for q in range(2):
                    load_halves(i + 1, q)
            sp.wait_ge(s_px, 2)
            load_block(0, 1, 0)
            load_block(1, 1, 1)
            sp.wait_ge(s_x[0], BPG // 2 * 16 + 16)
            load_block(2, 1, 0)
            for i in range(BPG // 2):
                for q in range(2):
                    store_block(i, 1, q, i * 2 + q + 3 < BPG)
                    if i == 0:
                        load_halves(BPG // 2 - 1, q)
                if i == BPG // 2 - 2:
                    for q in range(2):
                        load_halves(BPG // 2, q)
            for q in range(2):
                load_halves(BPG // 2 + 1, q)
            sp.wait_ge(s_kept, NB)
            for i in range(BPG // 2):
                store_transposes(1, i)
                load_halves(BPG // 2 + 2 + i // 2, i % 2)
            sp.wait_ge(s_sc, 2 * NG)
            sp.wait_ge(s_xtst, NB // 2 * 16)
            sp.dma_start(Wt, Wt_in.rearrange("(c p) n -> p c n", p=P)).then_inc(s_tl, 16)
            for m, src in enumerate((bq_in, bt_in)):
                sp.dma_start(brow[0:B, m, :], src.rearrange("(a n) -> a n", a=1).broadcast_to([B, D])
                             ).then_inc(s_tl, 16)
            sp.wait_ge(s_tables, 1)
            for e in range(E + 1):
                if e == E:
                    sp.wait_ge(s_zero, 16 * E)
                row = sp.value_load(zoff[0:1, e:e + 1], min_val=0, max_val=E * RG - TS)
                sp.dma_start(sorted_dram[ds(row, TS), :].rearrange("(s p) d -> p s d", p=P), zrow
                             ).then_inc(s_zero, 16)
            sp.wait_ge(s_px, 2 * NG)
            sp.wait_ge(s_zero, 16 * (E + 1))
            for q in range(2):
                sp.wait_ge(s_sct[q], NB // 2 * (2 * BT * 16))

            def row_of(t):
                src = rowoff[0:1, t:t + 1] if isinstance(t, int) else rowoff[0:1, ds(t, 1)]
                return sp.value_load(src, min_val=0, max_val=E * RG - TS)

            def load_tile(t, q, first=False):
                row = row_of(t)
                if not first:
                    sp.wait_ge(s_xgt, t - 1)
                    sp.wait_ge(s_idx, t - 1)
                sp.dma_start(GXf[q], sorted_dram[ds(row, TS), :].rearrange("(s p) d -> p s d", p=P)
                             ).then_inc(s_g[q], 16)

            load_tile(0, 0, True)
            load_tile(1, 1, True)
            load_tile(2, 0)
            sp.wait_ge(s_be8, 1)
            sp.dma_start(be_dram[:, :], be8[0:B, :]).then_inc(s_best, 16)
            sp.wait_ge(s_best, 16)
            sp.dma_start(BE, be_dram.rearrange("(a b) n -> a b n", a=1).broadcast_to([P, B, D])).then_inc(s_beld, 16)
            with sp.Fori(0, (NS - 3) // 2) as i:
                for q in range(2):
                    load_tile(i * 2 + (3 + q), 1 - q)

            def load_inputs(i, h):
                p = i * TQ + h
                sp.dma_start(XR[h], rows(x_t, p, 2)).then_inc(s_tx[h], 16)
                sp.dma_start(XC[h].rearrange("p u c t -> p u (c t)"), rows(xt_t, p, 2)).then_inc(s_tx[h], 16)

            def load_results(i, h):
                p = i * TQ + h
                for c in range(2):
                    sp.dma_start(YG[h][:, c], rows(y_t, p + c * (NT // 2), 2)).then_inc(s_tx[h], 16)

            def step(i, h, last=False):
                p = i * TQ + h
                sp.wait_ge(s_o, p * 2 + (2 + TQ))
                sp.dma_start(rows(out_t, p, 2), OB[h]).then_inc(s_ost[h], 16)
                if not last:
                    load_results(i + 1, h)
                    load_inputs(i + 1, h)
                if not (isinstance(i, int) and i == 0 and h == 0):
                    sp.wait_ge(s_ost[h - 1], (i if h else i - 1) * 16 + 16)
                    sp.sem_inc(s_ofree, 2)

            for h in TH:
                load_inputs(0, h)
            sp.wait_ge(s_yst, NS * (16 * SUB))
            for h in TH:
                load_results(0, h)
            step(0, 0)
            with sp.Fori(0, B - 2) as i:
                for h in range(1, TQ):
                    step(i, h)
                step(i + 1, 0)
            for h in range(1, TQ):
                step(B - 2, h)
            for h in TH:
                step(B - 1, h, last=True)
            sp.wait_ge(s_ost[TQ - 1], B * 16)

        @block.gpsimd
        def _(pool):
            ch = Chain(pool, s_pc)
            g = nc.gpsimd
            g.memset(Wqa[:, :, :], 0.0)
            g.memset(Wka[:, :, :], 0.0)
            g.memset(sbias[:, :], 0.0).then_inc(s_cm, 1)
            g.memset(identf[:, :], 0.0)
            g.memset(onesb[:, :], 1.0)
            g.memset(notfirst[:, :], 1.0)
            ch(g.iota(jtemp, pattern=[[1, NT], [0, 1]], base=0, channel_multiplier=0))
            ch(g.tensor_copy(meta[:, :, 0:1], jtemp))
            ch(g.iota(jtemp, pattern=[[0, NT], [0, 1]], base=0, channel_multiplier=1))
            g.tensor_copy(meta[:, :, 1:2], jtemp)
            g.memset(meta[:, :, 3:4], 0.0)
            g.iota(itemp, pattern=[[1, NS]], base=0, channel_multiplier=0)
            ch(g.memset(headmask[:, :, :], 1.0))
            ch(g.affine_select(out=identf[:, :], in_=identf[:, :], compare_op=ALU.not_equal, fill=1.0,
                               base=0, pattern=[[-1, P]], channel_multiplier=1))
            g.tensor_copy(iotaE[:, :], itemp[:, 0:E])
            g.tensor_copy(iotaT[:, :], itemp)
            ch(g.tensor_copy(identh[:, :], identf[:, :]))
            g.affine_select(out=notfirst[:, :], in_=notfirst[:, :], compare_op=ALU.not_equal, fill=0.0, base=0,
                            pattern=[[1, NTR]], channel_multiplier=0)
            ch(g.affine_select(out=before[:, :], in_=onesb[:, :], compare_op=ALU.is_gt, fill=0.0,
                               base=0, pattern=[[1, P]], channel_multiplier=-1))
            ch(g.affine_select(out=headmask[:, :, :], in_=headmask[:, :, :], compare_op=ALU.is_ge, fill=0.0,
                               base=0, pattern=[[P, KC], [-DH, HP]], channel_multiplier=1))
            g.affine_select(out=headmask[:, :, :], in_=headmask[:, :, :], compare_op=ALU.is_ge, fill=0.0,
                            base=DH - 1, pattern=[[-P, KC], [DH, HP]], channel_multiplier=-1
                            ).then_inc(s_cm, 1)
            pool.sem_inc(s_xsfree, CREDIT)
            for s in (s_nm, s_nx, s_yb, s_yfree, s_yc):
                pool.sem_inc(s, CREDIT)
            pool.sem_inc(s_o, TQ)
            pool.sem_inc(s_ofree, 2 * TQ)

            def scatter(i, q):
                k = i * 2 + q
                pool.wait_ge(s_scl[q], i * 16 + 16)
                pool.sem_inc(s_turn, 1)
                cols = gcol[:, q * BT:(q + 1) * BT, :]
                g.tensor_copy(SC[q][:, :, 2 * D:ROW], meta[:, ds(k * BT, BT), :])
                g.tensor_copy(cols, rowidx[:, ds(k * BT, BT), :]).then_inc(s_col, 1)
                pool.wait_ge(s_col, k + 1)
                pool.sem_inc(s_turn, 1)
                for u in range(BT):
                    for c in range(2):
                        pool.indirect_dma_start(
                            out=sorted_dram, in_=SC[q][:, u, :], in_offset=None,
                            out_offset=bass.IndirectOffsetOnAxis(ap=gcol[:, q * BT + u, c:c + 1], axis=0)
                        ).then_inc(s_sct[q], 16)

            for part in range(NR):
                pool.wait_ge(s_slots, part + 1)
                with pool.Fori(0, BPR // 2) as i:
                    for q in range(2):
                        scatter(i + part * (BPR // 2), q)

            def scatter_results(t, q):
                pool.wait_ge(s_idx, t + 1)
                pool.wait_ge(s_yb, t + (1 + CREDIT))
                pool.sem_inc(s_turn, 1)
                g.tensor_copy(gcol[:, q, :], idxf[:, q, :]).then_inc(s_yc, 1)
                pool.wait_ge(s_yc, t + (1 + CREDIT))
                pool.sem_inc(s_turn, 1)
                for c in range(SUB):
                    pool.indirect_dma_start(
                        out=y_dram, in_=YB[q][:, c, :], in_offset=None,
                        out_offset=bass.IndirectOffsetOnAxis(ap=gcol[:, q, c:c + 1], axis=0)
                    ).then_inc(s_yst, 16)
                pool.wait_ge(s_yst, t * (16 * SUB) + 16 * SUB)
                pool.sem_inc(s_yfree, 1)

            with pool.Fori(0, NS // 2) as i:
                scatter_results(i * 2, 0)
                scatter_results(i * 2 + 1, 1)
            scatter_results(NS - 1, 0)

        @block.scalar
        def _(act):
            a = nc.scalar
            ch = Chain(act, s_ac)
            def load_expert(e, q):
                for m, src in enumerate((w1_in, w3_in, w2_in)):
                    of = src[e:e + 1] if isinstance(e, int) else src[ds(e, 1)]
                    of = of.rearrange("a (c p) n -> p (a c) n", p=P)
                    slot = e * 3 + (m + 1)
                    dst = (WR[:, slot * 2 * CH:(slot + 1) * 2 * CH] if isinstance(e, int) else
                           WR[:, ds(slot * (2 * CH), 2 * CH)]).bitcast(fp32)
                    act.dma_start(dst.rearrange("p (c n) -> p c n", c=of.shape[1]), of).then_inc(s_w[q], 16)

            load_expert(0, 0)
            load_expert(1, 1)

            def copy_projection(m):
                act.wait_ge(s_wT, m + 1)
                a.copy((WqT, WkT)[m][:, :, :].rearrange("p c n -> p (c n)"), psW).then_inc(s_wTc, 1)

            def hi(c):
                k = 1 if c % 3 == 2 else 0
                if c:
                    act.wait_ge(s_wlo, 2 * c - 1)
                for h in range(2):
                    at = c * 2 * CH + h * CH // 2
                    a.activation(WR[:, at:at + CH // 2], weight_view(c)[:, h * CH // 2:(h + 1) * CH // 2],
                                 ACT.Copy, scale=sc[:, k:k + 1]).then_inc(s_whi, 1)

            def attention(n, split, after_probs=lambda: None):
                act.wait_ge(s_A, n + 1)
                a.copy(A.rearrange("p c n -> p (c n)"), psX[:, 0:KC * P]).then_inc(s_Ac, 1)
                if n == 0 and len(split[0]):
                    act.wait_ge(s_scale, 1)
                for c in split[0]:
                    hi(c)
                act.wait_ge(s_mx, n + 1)
                a.activation(PR, psS.rearrange("p b n -> p (b n)"), ACT.Exp,
                             bias=small[:, 4:5], scale=SCALE, accum_out=small[:, 5:6]).then_inc(s_ex, 1)
                after_probs()
                act.wait_ge(s_pt, n + 1)
                a.copy(PT, psT[0]).then_inc(s_ptc, 1)
                for c in split[1]:
                    hi(c)
                act.wait_ge(s_pxt, n + 1)
                a.copy(pxT.rearrange("p c n -> p (c n)"), psX[:, 256:256 + KC * P]).then_inc(s_pxtc, 1)

            def root(n, q):
                act.wait_ge(s_var, n + 1)
                a.activation(small[:, 24 + 8 * q:24 + 8 * q + BT], small[:, 16 + 8 * q:16 + 8 * q + BT],
                             ACT.Sqrt).then_inc(s_std, 1)

            def keep(m, grp, q):
                act.wait_ge(s_tr, m + (grp * BPG + 1))
                if grp and isinstance(m, int) and m == 0:
                    act.wait_ge(s_xtst, grp * (BPG // 2) * 16)
                dst = XT[:, m * BW:(m + 1) * BW] if isinstance(m, int) else XT[:, ds(m * BW, BW)]
                a.activation(XTB[q].rearrange("p u c t -> p (u c t)"), psTf[q], ACT.Copy, scale=1.0 / XSC
                             ).then_inc(s_xtb, 1)
                a.activation(dst, psTf[q], ACT.Copy, scale=1.0 / XSC).then_inc(s_kept, 1)

            def block_steps(i, grp, q, prefetch=False, first=False, more=True):
                m = i * 2 + q
                n = m + grp * BPG

                def square(w):
                    if grp:
                        return
                    if w == 0:
                        act.wait_ge(s_w[q], i * (16 * 3) + 16 * 3)
                        if prefetch:
                            load_expert(m + 2, q)
                    act.wait_ge(s_nm, m * 3 + (w + 1))
                    slot = m * 3 + (w + 1)
                    raw = (WR[:, slot * 2 * CH:(slot + 1) * 2 * CH] if isinstance(m, int) else
                           WR[:, ds(slot * (2 * CH), 2 * CH)]).bitcast(fp32)
                    a.activation(SQ[(3 * q + w) % 2], raw, ACT.Square).then_inc(s_sq, 1)

                act.wait_ge(s_xn, n + 1)
                act.wait_ge(s_xsfree, n + 1)
                src = XN[:, m * BT:(m + 1) * BT, :] if isinstance(m, int) else XN[:, ds(m * BT, BT), :]
                a.activation(XS[q][:, :, 0, :], src, ACT.Copy, scale=XSC).then_inc(s_hi, 1)
                square(0)
                if more:
                    root(n + 1, 1 - q)
                square(1)
                if not first:
                    keep(m - 1, grp, 1 - q)
                square(2)

            def blocks(grp):
                for q in range(2):
                    block_steps(0, grp, q, prefetch=not grp, first=not q)
                if not grp:
                    copy_projection(0)
                with act.Fori(0, BPG // 2 - 2) as i:
                    for q in range(2):
                        block_steps(i + 1, grp, q, prefetch=not grp)
                if not grp:
                    copy_projection(1)
                for q in range(2):
                    block_steps(BPG // 2 - 1, grp, q, more=not q)
                keep(BPG - 1, grp, 1)

            def choice_weights():
                act.wait_ge(s_choice, NR)
                a.activation(imp[:, 1, :], imp[:, 1, :], ACT.Exp).then_inc(s_choice, 1)

            act.preload_act_table(ACT.Sqrt)
            root(0, 0)
            blocks(0)
            act.preload_act_table(ACT.Exp)
            attention(0, SPLITS[0])
            attention(1, SPLITS[1])
            act.preload_act_table(ACT.Sqrt)
            root(BPG, 0)
            blocks(1)
            act.preload_act_table(ACT.Exp)
            attention(2, SPLITS[2])
            attention(3, SPLITS[3], choice_weights)

            act.preload_act_table(ACT.Silu)

            def copy_gather(t, q):
                act.wait_ge(s_xgt, t + 1)
                a.copy(XG[q].rearrange("p c k t -> p (c k t)"), psXG[:, q, :, :].rearrange("p c t -> p (c t)")
                       ).then_inc(s_xg, 1)

            def silu_hi(t, q):
                for h in range(2):
                    act.wait_ge(s_gu, t * 2 + (h + 1))
                    if not (isinstance(t, int) and t == 0):
                        act.wait_ge(s_hl, t * 2 + (h - 1))
                    a.activation(SG[:, 2 * h:2 * h + 2, :], PS[:, 2 * h:2 * h + 2, 0:TS], ACT.Silu,
                                 scale=sc[:, 2:3]).then_inc(s_sg, 1)
                for h in range(2):
                    act.wait_ge(s_h, t * 2 + (h + 1))
                    a.copy(HH[q][:, 0, 2 * h:2 * h + 2, :], SG[:, 2 * h:2 * h + 2, :]).then_inc(s_hh, 1)

            def copy_out(t, q):
                act.wait_ge(s_y, t + 1)
                act.wait_ge(s_yfree, t + 1)
                a.activation(YB[q].rearrange("p s d -> p (s d)"), psY[:, q, :, :].rearrange("p s d -> p (s d)"),
                             ACT.Copy, scale=sc[:, 7:8]).then_inc(s_yb, 1)

            copy_gather(0, 0)
            copy_gather(1, 1)
            silu_hi(0, 0)
            with act.Fori(0, (NS - 3) // 2) as i:
                for q in range(2):
                    t = i * 2 + 1 + q
                    copy_gather(t + 1, q)
                    silu_hi(t, 1 - q)
                    copy_out(t - 1, q)
            t = NS - 2
            copy_gather(t + 1, 0)
            silu_hi(t, 1)
            copy_out(t - 1, 0)
            silu_hi(t + 1, 0)
            copy_out(t, 1)
            copy_out(t + 1, 0)

            def first_expert(i, u):
                j = i * TPB + u
                act.wait_ge(s_tx[u // 2], i * 64 + 64)
                w = imp[:, 0, j:j + 1] if isinstance(j, int) else imp[:, 0, ds(j, 1)]
                a.activation(FF[u % TQ], YG[u // 2][:, 0, u % 2, :], ACT.Copy, scale=w).then_inc(s_fa, 1)

            def gate(i, u):
                act.wait_ge(s_f, i * TPB + (u + 1))
                a.activation(SF[u % TQ], FF[u % TQ], ACT.Silu).then_inc(s_sf, 1)

            def steps(i, more=True):
                for u in range(TPB):
                    if more or u < TPB - 1:
                        first_expert(i + (u + 1) // TPB, (u + 1) % TPB)
                    gate(i, u)

            first_expert(0, 0)
            with act.Fori(0, B - 1) as i:
                steps(i)
            steps(B - 1, more=False)

        @block.vector
        def _(dve):
            v = nc.vector
            ch = Chain(dve, s_dc)
            wqa4 = Wqa[:, :, :].rearrange("p c (a h) -> p c a h", a=1).broadcast_to([P, KC, GB, HP])
            wka4 = Wka[:, :, :].rearrange("p c (a h) -> p c a h", a=1).broadcast_to([P, KC, GB, HP])

            def lo(c):
                k = 1 if c % 3 == 2 else 0
                for h in range(2):
                    dve.wait_ge(s_whi, 2 * c + 1 + h)
                    if c and not h:
                        dve.wait_ge(s_wlo, 2 * c)
                    at = c * 2 * CH + h * CH // 2
                    v.scalar_tensor_tensor(WR[:, at + CH:at + CH + CH // 2],
                                           weight_view(c)[:, h * CH // 2:(h + 1) * CH // 2], sc[:, k:k + 1],
                                           WR[:, at:at + CH // 2], ALU.mult, ALU.subtract).then_inc(s_wlo, 1)

            def attention(n, during_scores, during_sums, after_sums=lambda: None):
                grp, k = n // 2, n % 2
                if not k:
                    v.tensor_copy(WA, wqa4).then_inc(s_wa, 1)
                else:
                    v.tensor_tensor(WA, wka4, pooled[:, 0, :, grp * GB:(grp + 1) * GB].rearrange("p c (b a) -> p c b a", a=1)
                                    .broadcast_to([P, KC, GB, HP]), ALU.mult).then_inc(s_wa, 1)
                dve.wait_ge(s_Ac, n + 1)
                ch(v.tensor_tensor(small[:, 6:7], psX[:, 500:501], sbias[:, k:k + 1], ALU.add))
                during_scores()
                dve.wait_ge(s_sc, n + 1)
                ch(v.reduce_max(small[:, 7:8], psS.rearrange("p b n -> p (b n)"), X))
                ch(v.tensor_tensor(small[:, 7:8], small[:, 7:8], small[:, 6:7], ALU.add))
                ch(v.tensor_tensor(small[:, 6:7], small[:, 6:7], small[:, 7:8], ALU.subtract))
                v.tensor_scalar(small[:, 4:5], small[:, 6:7], SCALE, None, ALU.mult).then_inc(s_mx, 1)
                dve.wait_ge(s_ex, n + 1)
                ch(v.reciprocal(small[:, 5:6], small[:, 5:6]))
                during_sums()
                dve.wait_ge(s_px, n + 1)
                v.tensor_scalar(pxn, psX[:, 0:D], small[:, 5:6], None, ALU.mult).then_inc(s_pxn, 1)
                after_sums()
                dve.wait_ge(s_pv, n + 1)
                pv = psTf[1][:, 0:KC * P].rearrange("p (c b h) -> p c b h", c=KC, b=GB)
                own = A.rearrange("p c (b h) -> p c b h", b=GB)
                for c in range(KC):
                    mask = headmask[:, c, :].rearrange("p (a h) -> p a h", a=1).broadcast_to([P, GB, HP])
                    last = v.tensor_tensor(own[:, c], pv[:, c], mask, ALU.mult)
                ch(last)
                dst = pooled[:, k, :, grp * GB:(grp + 1) * GB]
                ch(v.tensor_reduce(dst, own, X, ALU.add))
                for c in range(KC):
                    last = v.tensor_scalar(dst[:, c, :], dst[:, c, :], bcol[:, k, c:c + 1], None, ALU.add)
                if not k:
                    last.then_inc(s_pooled, 1)
                    dve.wait_ge(s_pooled, n + 1)
                else:
                    ch(last)
                    v.tensor_tensor(dst, dst, pooled[:, 0, :, grp * GB:(grp + 1) * GB], ALU.mult).then_inc(s_pooled, 1)

            def rows(m):
                return [XNf[:, (m * BT + u) * D:(m * BT + u + 1) * D] if isinstance(m, int) else
                        XNf[:, ds(m * BW + u * D, D)] for u in range(BT)]

            def statistics(m, grp, q, nth):
                dve.wait_ge(s_x[q], nth * 16 + (grp * (BPG // 2) * 16 + 16))
                dve.sem_inc(s_vturn, 1)
                for u, row in enumerate(rows(m)):
                    last = v.bn_stats(stats[q][:, u, :], row)
                ch(last)
                dve.sem_inc(s_vturn, 1)
                for u in range(BT):
                    last = v.bn_aggr(meanvar[q][:, u, :], stats[q][:, u, :])
                ch(last)
                v.tensor_scalar(small[:, 16 + 8 * q:16 + 8 * q + BT], meanvar[q][:, :, 1], EPS, None,
                                ALU.add).then_inc(s_var, 1)

            def norm(m, q, w):
                dve.wait_ge(s_nm, m * 3 + (w + 1 + CREDIT))
                dst = wmax[:, w, m:m + 1] if isinstance(m, int) else wmax[:, w, ds(m, 1)]
                v.reduce_max(dst, psNorm[(3 * q + w) % 2][:, 0:F if w < 2 else D], X).then_inc(s_nx, 1)

            def block_steps(i, grp, q, more=True, first=False):
                m = i * 2 + q
                n = m + grp * BPG
                var = small[:, 16 + 8 * q:16 + 8 * q + BT]
                std = small[:, 24 + 8 * q:24 + 8 * q + BT]
                tmp = small[:, 20 + 8 * q:20 + 8 * q + BT]
                dve.wait_ge(s_std, n + 1)
                ch(v.reciprocal(std, std))
                ch(v.scalar_tensor_tensor(tmp, std, -0.5, std, ALU.mult, ALU.mult))
                ch(v.tensor_tensor(tmp, tmp, var, ALU.mult))
                ch(v.scalar_tensor_tensor(std, tmp, 1.5, std, ALU.add, ALU.mult))
                for u, row in enumerate(rows(m)):
                    last = v.tensor_scalar(row, row, meanvar[q][:, u, 0:1], std[:, u:u + 1],
                                           ALU.subtract, ALU.mult)
                last.then_inc(s_xn, 1)
                if more:
                    statistics(m + 1, grp, 1 - q, i + q)
                if not grp and not first:
                    norm(m - 1, 1 - q, 1)
                    norm(m - 1, 1 - q, 2)
                dve.wait_ge(s_hi, n + 1)
                src = XN[:, m * BT:(m + 1) * BT, :] if isinstance(m, int) else XN[:, ds(m * BT, BT), :]
                v.scalar_tensor_tensor(XS[q][:, :, 1, :], src, XSC, XS[q][:, :, 0, :],
                                       ALU.mult, ALU.subtract).then_inc(s_lo, 1)
                if not grp:
                    norm(m, q, 0)

            def blocks(grp, *between):
                statistics(0, grp, 0, 0)
                for q in range(2):
                    block_steps(0, grp, q, first=not q)
                with dve.Fori(0, BPG // 2 - 2) as i:
                    ch.enter(i, 2 * 6)
                    for q in range(2):
                        block_steps(i + 1, grp, q)
                ch.leave(BPG // 2 - 2)
                for q in range(2):
                    if between:
                        between[q]()
                    block_steps(BPG // 2 - 1, grp, q, more=not q)
                if not grp:
                    norm(BPG - 1, 1, 1)
                    norm(BPG - 1, 1, 2)

            blocks(0)

            def scales():
                dve.wait_ge(s_nx, 3 * E + CREDIT)
                v.reduce_max(small[:, 2:3], wmax[:, 0:2, :].rearrange("p m e -> p (m e)"), X)
                ch(v.reduce_max(small[:, 3:4], wmax[:, 2, :], X))
                fe = small[:, 40:48]
                ch(v.tensor_scalar(small_i[:, 0:2], small[:, 2:4].bitcast(i32), 23, None, ALU.logical_shift_right))
                ch(v.tensor_copy(small[:, 10:12], small_i[:, 0:2]))
                v.tensor_scalar(small_i[:, 0:2], small[:, 10:12], -1.0, 409.0, ALU.mult, ALU.add)
                ch(v.tensor_scalar(fe[:, 4:5], small[:, 10:11], -1.0, 259.0, ALU.mult, ALU.add))
                ch(v.tensor_scalar(small_i[:, 0:2], small_i[:, 0:2], 1, None, ALU.logical_shift_right))
                ch(v.tensor_scalar(fe[:, 0:2], small_i[:, 0:2], 200.0, 1.0, ALU.min, ALU.max))
                ch(v.tensor_scalar(fe[:, 4:5], fe[:, 4:5], 200.0, 1.0, ALU.min, ALU.max))
                v.tensor_scalar(fe[:, 2:3], fe[:, 0:1], -1.0, 254.0 - XSC_LOG, ALU.mult, ALU.add)
                v.tensor_scalar(fe[:, 3:4], fe[:, 1:2], -1.0, 254.0, ALU.mult, ALU.add)
                ch(v.tensor_scalar(fe[:, 5:6], fe[:, 4:5], -1.0, 254.0, ALU.mult, ALU.add))
                ch(v.tensor_copy(small_i[:, 0:6], fe[:, 0:6]))
                ch(v.tensor_scalar(sc[:, 0:6].bitcast(i32), small_i[:, 0:6], 23, None, ALU.logical_shift_left))
                v.tensor_tensor(sc[:, 6:7], sc[:, 2:3], sc[:, 4:5], ALU.mult)
                v.tensor_tensor(sc[:, 7:8], sc[:, 3:4], sc[:, 5:6], ALU.mult).then_inc(s_scale, 1)
                dve.wait_ge(s_scale, 1)

            def split(chunks):
                for c in chunks:
                    lo(c)

            taken = small[:, 48:56]
            n_t = small[:, 56:64]
            experts = iotaE[:, :].rearrange("p (e a) -> p e a", a=1).broadcast_to([P, E, NTR])
            resets = notfirst[:, :].rearrange("p (a j) -> p a j", a=1).broadcast_to([P, E, NTR])

            def over_e(ap):
                return ap.rearrange("p e j -> p j e")

            def each_e(ap):
                return ap.rearrange("p (a j) -> p a j", a=1).broadcast_to([P, E, NTR])

            def logits(part):
                dve.wait_ge(s_rt, BPG * (part // 2 + 1) if part != IN_BLOCKS else BPR * (part + 1))
                ch(v.tensor_copy(route[part][0][0], psL[:, part * NTR:(part + 1) * NTR, :].rearrange("p j e -> p e j")))

            def choices(part):
                (L, eq, cand, oh1, oh2, cum, cnt), rf, rc, rci, chosen = route[part]
                own = slice(part * NTR, (part + 1) * NTR)

                def choose(top, oh):
                    ch(v.reduce_max(top, over_e(L), X))
                    ch(v.tensor_tensor(eq, L, each_e(top), ALU.is_equal))
                    ch(v.scalar_tensor_tensor(cand, eq, -float(E), experts, ALU.mult, ALU.add))
                    ch(v.tensor_reduce(rc[2], over_e(cand), X, ALU.min))
                    ch(v.tensor_scalar(rc[2], rc[2], float(E), None, ALU.add))
                    ch(v.tensor_tensor(oh, experts, each_e(rc[2]), ALU.is_equal))

                choose(rc[0], oh1)
                ch(v.scalar_tensor_tensor(L, oh1, FAR, L, ALU.mult, ALU.add))
                choose(rc[1], oh2)
                v.tensor_copy(meta[:, own, 2], rc[2])
                v.tensor_tensor(imp[:, 1, own], rc[1], rc[0], ALU.subtract).then_inc(s_choice, 1)
                v.tensor_tensor(chosen.rearrange("p (e j) -> p e j", e=E), oh1, oh2, ALU.add).then_inc(s_rank, 1)

            def slots(part):
                (L, eq, slot, oh1, oh2, cum, cnt), rf, rc, rci, chosen = route[part]
                own = slice(part * NTR, (part + 1) * NTR)
                dve.wait_ge(s_rank, 2 * part + 2)
                v.tensor_copy(L, resets)
                ch(v.tensor_copy(cnt, psCnt[part].rearrange("p (e j) -> p e j", e=E)))
                ch(v.tensor_tensor_scan(rf[5], rf[0], rf[6], 0.0, ALU.mult, ALU.add))
                ch(v.tensor_copy(n_t, cum[:, :, NTR - 1]))
                ch(v.tensor_tensor(cum, cum, cnt, ALU.subtract))
                ch(v.tensor_tensor(slot, cum, psRank[part].rearrange("p (e j) -> p e j", e=E), ALU.add))
                if not part:
                    ch(v.tensor_scalar(taken, iotaE[:, :], float(RG), None, ALU.mult))
                ch(v.tensor_tensor(slot, slot, taken.rearrange("p (e a) -> p e a", a=1).broadcast_to([P, E, NTR]),
                                   ALU.add))
                for c, oh in enumerate((oh1, oh2)):
                    ch(v.tensor_tensor(eq, oh, slot, ALU.mult))
                    ch(v.tensor_reduce(rc[c], over_e(eq), X, ALU.add))
                    ch(v.tensor_copy(rci[c], rc[c]))
                    last = v.tensor_copy(rowidx[:, own, c], rci[c].bitcast(u32))
                last.then_inc(s_slots, 1)
                ch(v.tensor_tensor(taken, taken, n_t, ALU.add))

            def choice_weights():
                dve.wait_ge(s_choice, NR + 1)
                ch(v.tensor_scalar(imp[:, 0, :], imp[:, 1, :], 1.0, None, ALU.add))
                ch(v.reciprocal(imp[:, 0, :], imp[:, 0, :]))
                ch(v.tensor_tensor(imp[:, 1, :], imp[:, 0, :], imp[:, 1, :], ALU.mult))

            def tables():
                ends = small[:, 32:40]
                ones = small[:, 40:48]
                ch(v.scalar_tensor_tensor(n_t, iotaE[:, :], -float(RG), taken, ALU.mult, ALU.add))
                ch(v.tensor_scalar(small_i[:, 0:E], n_t, float(TS - 1), None, ALU.add))
                ch(v.tensor_scalar(small_i[:, 0:E], small_i[:, 0:E], TS.bit_length() - 1, None,
                                   ALU.logical_shift_right))
                ch(v.tensor_copy(n_t, small_i[:, 0:E]))
                ch(v.memset(ones, 1.0))
                ch(v.tensor_tensor_scan(ends, ones, n_t, 0.0, ALU.mult, ALU.add))
                v.tensor_copy(zoff[:, 0:E], taken)
                v.tensor_scalar(zoff[:, E:E + 1], n_t[:, E - 1:E], float(TS), float((E - 1) * RG), ALU.mult, ALU.add)
                ch(v.tensor_scalar(tb[1], iotaT[:, :], ends[:, E - 1:E], float(TS), ALU.min, ALU.mult))
                ch(v.tensor_scalar(n_t, n_t, -float(TS), float(RG), ALU.mult, ALU.add))
                tiles = iotaT[:, :].rearrange("p (t e) -> p t e", e=1).broadcast_to([P, NS, E - 1])

                def each_tile(ap):
                    return ap[:, 0:E - 1].rearrange("p (t e) -> p t e", t=1).broadcast_to([P, NS, E - 1])

                dve.wait_ge(s_xsfree, NB + CREDIT)
                ch(v.tensor_tensor(past, tiles, each_tile(ends), ALU.is_ge))
                ch(v.reduce_sum(tb[0], past, X))
                ch(v.tensor_tensor(past, past, each_tile(n_t), ALU.mult))
                ch(v.reduce_sum(tb[2], past, X))
                ch(v.tensor_tensor(tb[2], tb[2], tb[1], ALU.add))
                v.tensor_copy(iotaT[:, :], tb[0])
                v.tensor_scalar(woff[:, :], tb[0], float(3 * 2 * CH), None, ALU.mult)
                ch(v.memset(zrow, 0.0))
                for c in range(SUB):
                    v.memset(zrow[:, c, 2 * D:2 * D + 1], float(2 * NT + c))
                    v.tensor_copy(zrow[:, c, 2 * D + 1:2 * D + 2], meta[:, 0, 1:2])
                    v.memset(zrow[:, c, 2 * D + 2:2 * D + 3], -1.0)
                v.tensor_copy(rowoff[:, :], tb[2]).then_inc(s_tables, 1)

            def to_fold(b):
                if b == 4:
                    dve.wait_ge(s_pooled, 2 * NG)
                for c in range(KC):
                    last = v.tensor_scalar(WTP[b % 2][:, c, :], Wt[:, c, :], pooled[:, 1, c, b:b + 1], None, ALU.mult)
                last.then_inc(s_wtp, 1)

            def folded(b):
                if (b + 1) * KC * D > 4 * BW - SUB * ROW // 2:
                    dve.wait_ge(s_zero, 16 * (E + 1))
                dve.wait_ge(s_eff, b + 1)
                v.tensor_tensor(WE[:, b], psEff[b % 2], Wq[:, :, :], ALU.add).then_inc(s_we, 1)

            def fold_first():
                dve.wait_ge(s_tl, 16 * 3)
                to_fold(0)
                to_fold(1)

            def fold_second():
                for b in range(2):
                    folded(b)
                for b in range(2, 4):
                    to_fold(b)

            dve.wait_ge(s_cl, 16 * LOADS)
            dve.wait_ge(s_cm, 2)
            attention(0, lambda: (logits(0), choices(0), scales(), split(SPLITS[0][0])), lambda: (slots(0), split(SPLITS[0][1])))
            attention(1, lambda: (logits(1), choices(1), split(SPLITS[1][0])), lambda: (slots(1), split(SPLITS[1][1])))
            blocks(1, lambda: (logits(IN_BLOCKS), choices(IN_BLOCKS)), lambda: slots(IN_BLOCKS))
            logits(NR - 1)
            attention(2, lambda: (choices(NR - 1), split(SPLITS[2][0])),
                      lambda: (slots(NR - 1), split(SPLITS[2][1])))
            attention(3, lambda: split(SPLITS[3][0]),
                      lambda: (tables(), choice_weights(), split(SPLITS[3][1]), fold_first()), fold_second)

            for b in range(2, B):
                folded(b)
                if b + 2 < B:
                    to_fold(b + 2)
                if b == 2:
                    dve.wait_ge(s_pooled, 2 * NG)
                    for c in range(KC):
                        last = v.tensor_scalar(bqk[:, c, :], pooled[:, 1, c, :], bcol[:, 0, c:c + 1], None, ALU.mult)
                    last.then_inc(s_bq, 1)
                    ch(v.tensor_tensor(brow[0:B, 0, :], brow[0:B, 0, :], brow[0:B, 1, :], ALU.add))
            dve.wait_ge(s_be, 1)
            v.tensor_tensor(be8[0:B, :], psBe, brow[0:B, 0, :], ALU.add).then_inc(s_be8, 1)

            def hidden(t, q):
                for h in range(2):
                    dve.wait_ge(s_sg, t * 2 + (h + 1))
                    v.scalar_tensor_tensor(SG[:, 2 * h:2 * h + 2, :], PS[:, 2 * h:2 * h + 2, TS:2 * TS],
                                           sc[:, 6:7], SG[:, 2 * h:2 * h + 2, :], ALU.mult, ALU.mult
                                           ).then_inc(s_h, 1)
                for h in range(2):
                    dve.wait_ge(s_hh, t * 2 + (h + 1))
                    v.tensor_tensor(HH[q][:, 1, 2 * h:2 * h + 2, :], SG[:, 2 * h:2 * h + 2, :],
                                    HH[q][:, 0, 2 * h:2 * h + 2, :], ALU.subtract).then_inc(s_hl, 1)

            def result_rows(t, q, nth):
                of = GXf[q][:, :, 2 * D:ROW]
                expert = iotaT[:, t:t + 1] if isinstance(t, int) else iotaT[:, ds(t, 1)]
                dve.wait_ge(s_g[q], nth * 16 + 16)
                dve.wait_ge(s_yc, t + 1)
                ch(v.tensor_scalar(idxf[:, q, :], of[:, :, 2], expert, float(NT), ALU.is_equal, ALU.mult))
                ch(v.tensor_tensor(idxf[:, q, :], idxf[:, q, :], of[:, :, 0], ALU.add))
                v.scalar_tensor_tensor(idxf[:, q, :], idxf[:, q, :], float(P), of[:, :, 1], ALU.mult, ALU.add
                                       ).then_inc(s_idx, 1)

            with dve.Fori(0, NS // 2) as i:
                ch.enter(i, 2 * 2)
                for q in range(2):
                    result_rows(i * 2 + q, q, i)
                    hidden(i * 2 + q, q)
            ch.leave(NS // 2)
            result_rows(NS - 1, 0, NS // 2)
            hidden(NS - 1, 0)

            def batch(b, more=True):
                def ffn(u):
                    j = b * TPB + u
                    q = u % TQ
                    w = imp[:, 1, j:j + 1] if isinstance(j, int) else imp[:, 1, ds(j, 1)]
                    dve.wait_ge(s_fa, j + 1)
                    v.scalar_tensor_tensor(FF[q], YG[u % TPB // 2][:, 1, u % 2, :], w, FF[q], ALU.mult, ALU.add
                                           ).then_inc(s_f, 1)

                def result(u):
                    j = b * TPB + u
                    q = u % TQ
                    to = OB[u // 2][:, u % 2, :]
                    dve.wait_ge(s_s, j + 1)
                    dve.wait_ge(s_ofree, j + 1)
                    bias = BE[:, b, :] if isinstance(b, int) else BE[:, ds(b, 1), :].rearrange("p a n -> p (a n)")
                    ch(v.tensor_tensor(to, psAtt[q], bias, ALU.add))
                    dve.wait_ge(s_sf, j + 1)
                    ch(v.tensor_tensor(to, to, SF[q], ALU.mult))
                    dve.wait_ge(s_tx[u // 2], b * 64 + 64)
                    v.tensor_tensor(to, to, XR[u // 2][:, u % 2, :], ALU.add).then_inc(s_o, 1)

                if isinstance(b, int) and b == 0:
                    return ffn(0)
                for u in range(TPB):
                    if more or u < TPB - 1:
                        ffn(u + 1)
                    result(u)

            dve.wait_ge(s_beld, 16)
            batch(0)
            with dve.Fori(0, B - 1) as b:
                ch.enter(b, 2 * TPB)
                batch(b)
            ch.leave(B - 1)
            batch(B - 1, more=False)

        @block.tensor
        def _(pe):
            t_ = nc.tensor
            pe.wait_ge(s_cm, 2)

            def transpose_projection(m):
                W = (Wq, Wk)[m]
                if m:
                    pe.wait_ge(s_wTc, m)
                for hc in range(KC):
                    for kc in range(KC):
                        at = (hc * KC + kc) * P
                        last = t_.transpose(psW[:, at:at + P], W[:, kc, hc * P:(hc + 1) * P], identf[:, :])
                last.then_inc(s_wT, 1)

            def attention(n, after_scores=lambda: None, after_sums=lambda: None):
                grp, k = n // 2, n % 2
                W, WT = ((Wq, WqT), (Wk, WkT))[k]
                WAf = WA.rearrange("p c b h -> p c (b h)")
                pe.wait_ge(s_wa, n + 1)
                for dc in range(KC):
                    for hc in range(KC):
                        t_.matmul(psX[:, dc * P:(dc + 1) * P], WT[:, hc, dc * P:(dc + 1) * P], WAf[:, hc, :],
                                  start=hc == 0, stop=hc == KC - 1)
                for hc in range(KC):
                    last = t_.matmul(psX[:, 500:501], WAf[:, hc, :], bcol[:, k, hc:hc + 1],
                                     start=hc == 0, stop=hc == KC - 1)
                last.then_inc(s_A, 1)
                pe.wait_ge(s_Ac, n + 1)
                pe.wait_ge(s_kept, BPG * (grp + 1))
                for hf in range(2):
                    for kc in range(KC):
                        for b in range(GB):
                            n0 = b * TPB + hf * BT
                            last = t_.matmul(psS[HP * b:HP * (b + 1), hf, :], A[:, kc, HP * b:HP * (b + 1)],
                                             XT4[:, n0:n0 + BT, kc, :], start=kc == 0, stop=kc == KC - 1)
                last.then_inc(s_sc, 1)
                after_scores()
                pe.wait_ge(s_ex, n + 1)
                for j in range(TPB):
                    last = t_.transpose(psT[0][:, j, :], PR[:, j * P:(j + 1) * P], identf[:, :])
                last.then_inc(s_pt, 1)
                pe.wait_ge(s_ptc, n + 1)
                for j in range(TPB):
                    for b in range(GB):
                        last = t_.matmul(psX[HP * b:HP * (b + 1), 0:D], PT[:, j, HP * b:HP * (b + 1)],
                                         XN[:, b * TPB + j, :], start=j == 0, stop=j == TPB - 1)
                last.then_inc(s_px, 1)
                after_sums()
                pe.wait_ge(s_pxn, n + 1)
                for kc in range(KC):
                    last = t_.transpose(psX[:, D + kc * P:D + (kc + 1) * P], pxn[:, kc * P:(kc + 1) * P],
                                        identf[:, :])
                last.then_inc(s_pxt, 1)
                pe.wait_ge(s_pxtc, n + 1)
                for hc in range(KC):
                    for kc in range(KC):
                        last = t_.matmul(psTf[1][:, hc * P:(hc + 1) * P], W[:, kc, hc * P:(hc + 1) * P],
                                         pxT[:, kc, :], start=kc == 0, stop=kc == KC - 1)
                last.then_inc(s_pv, 1)

            def transpose(n, q, first=False):
                pe.wait_ge(s_lo, n + 1)
                if not first:
                    pe.wait_ge(s_kept, n - 1)
                for u in range(BT):
                    for kc in range(KC):
                        for hl in range(2):
                            last = t_.matmul(psT[q][:, u * KC + kc, :], XS[q][:, u, hl, kc * P:(kc + 1) * P],
                                             identh[:, :], start=hl == 0, stop=hl == 1)
                last.then_inc(s_tr, 1)

            def norms(m, q, ws):
                for w in ws:
                    r = (3 * q + w) % 2
                    width, parts = (F, KC) if w < 2 else (D, FC)
                    pe.wait_ge(s_sq, m * 3 + (w + 1))
                    pe.wait_ge(s_nx, m * 3 + (w + 1))
                    for c in range(parts):
                        last = t_.matmul(psNorm[r][:, 0:width], onesb[:, :], SQ[r][:, c * width:(c + 1) * width],
                                         start=c == 0, stop=c == parts - 1)
                    last.then_inc(s_nm, 1)

            def router(n, q):
                pe.wait_ge(s_xtb, n + 1)
                for u in range(BT):
                    j = n * BT + u
                    dst = psL[:, j, :] if isinstance(j, int) else psL[:, ds(j, 1), :]
                    for kc in range(KC):
                        last = t_.matmul(dst, XTB[q][:, u, kc, :], rw[:, kc, :], start=kc == 0, stop=kc == KC - 1)
                last.then_inc(s_rt, 1)

            def ranks(part):
                chosen = route[part][4]
                pe.wait_ge(s_rank, 2 * part + 1)
                t_.matmul(psRank[part], before[:, :], chosen, start=True, stop=True)
                t_.matmul(psCnt[part], onesb[:, :], chosen, start=True, stop=True).then_inc(s_rank, 1)

            def blocks(grp):
                def step(i, q, first=False):
                    n = i * 2 + (q + grp * BPG)
                    if not grp:
                        norms(n, q, (0,))
                    transpose(n, q, first or (isinstance(n, int) and n < 2))
                    if not grp:
                        norms(n, q, (1,))
                    if not first:
                        router(n - 1, 1 - q)
                    if not grp:
                        norms(n, q, (2,))

                step(0, 0, True)
                if not grp:
                    pe.wait_ge(s_cl, 16 * LOADS)
                step(0, 1)
                if not grp:
                    transpose_projection(0)
                with pe.Fori(0, BPG // 2 - 2) as i:
                    for q in range(2):
                        step(i + 1, q)
                if not grp:
                    transpose_projection(1)
                if grp == NG - 1:
                    ranks(IN_BLOCKS)
                step(BPG // 2 - 1, 0)
                step(BPG // 2 - 1, 1)
                router((grp + 1) * BPG - 1, 1)


            def fold(b):
                pe.wait_ge(s_wtp, b + 1)
                if b >= 2:
                    pe.wait_ge(s_we, b - 1)
                for dc in range(KC):
                    for hc in range(KC):
                        last = t_.matmul(psEff[b % 2][:, dc, :], WqT[:, hc, dc * P:(dc + 1) * P],
                                         WTP[b % 2][:, hc, :], start=hc == 0, stop=hc == KC - 1)
                last.then_inc(s_eff, 1)

            blocks(0)
            pe.wait_ge(s_wTc, 2)
            attention(0, lambda: ranks(0))
            pe.wait_ge(s_pooled, 1)
            attention(1, lambda: ranks(1))
            pe.wait_ge(s_pooled, 2)
            blocks(1)
            attention(2, lambda: ranks(NR - 1))
            pe.wait_ge(s_pooled, 3)
            attention(3, after_sums=lambda: (fold(0), fold(1)))

            WMAX = (E - 1) * 3 * 2 * CH

            def offset(t):
                src = woff[0:1, t:t + 1] if isinstance(t, int) else woff[0:1, ds(t, 1)]
                return pe.value_load(src, min_val=0, max_val=WMAX)

            def transposes(t, q, nth):
                pe.wait_ge(s_g[q], nth * 16 + 16)
                for s in range(SUB):
                    for c in range(2 * KC):
                        last = t_.transpose(psXG[:, q, c, s * P:(s + 1) * P], GX[q][s][:, c // KC, c % KC, :],
                                            identh[:, :])
                last.then_inc(s_xgt, 1)

            def gate_up(t, q):
                w = offset(t)
                pe.wait_ge(s_xg, t + 1)
                for h in range(2):
                    if not (isinstance(t, int) and t == 0):
                        pe.wait_ge(s_h, t * 2 + (h - 1))
                    for f in range(2 * h, 2 * h + 2):
                        for m in range(2):
                            n = 0
                            for kc in range(KC):
                                for wl, xl in ((0, 0), (0, 1), (1, 0)):
                                    at = m * 2 * CH + wl * CH + kc * F + f * P
                                    last = t_.matmul(psGU[f][:, m, :], WR[:, ds(w + at, P)], XG[q][:, xl, kc, :],
                                                     start=n == 0, stop=n == 3 * KC - 1)
                                    n += 1
                    last.then_inc(s_gu, 1)

            def down(t, q):
                w = offset(t)
                pe.wait_ge(s_hl, t * 2 + 2)
                pe.wait_ge(s_yb, t + 1)
                for s in range(SUB):
                    n = 0
                    for f in range(FC):
                        for hl, wl in ((0, 0), (0, 1), (1, 0)):
                            at = 2 * 2 * CH + wl * CH + f * D
                            last = t_.matmul(psY[:, q, s, :], HH[q][:, hl, f, s * P:(s + 1) * P],
                                             WR[:, ds(w + at, D)], start=n == 0, stop=n == 3 * FC - 1)
                            n += 1
                last.then_inc(s_y, 1)

            for b in range(2, B - 2):
                fold(b)
            transposes(0, 0, 0)
            transposes(1, 1, 0)
            fold(B - 2)
            fold(B - 1)
            pe.wait_ge(s_bq, 1)
            for hc in range(KC):
                last = t_.matmul(psBe, bqk[:, hc, :], Wt[:, hc, :], start=hc == 0, stop=hc == KC - 1)
            last.then_inc(s_be, 1)
            pe.wait_ge(s_tables, 1)
            pe.wait_ge(s_wlo, 2 * NCH)
            pe.wait_ge(s_we, B)
            pe.wait_ge(s_be8, 1)
            gate_up(0, 0)
            with pe.Fori(0, (NS - 3) // 2) as i:
                for q in range(2):
                    t = i * 2 + 1 + q
                    transposes(t + 1, q, i + 1)
                    gate_up(t, 1 - q)
                    down(t - 1, q)
            t = NS - 2
            transposes(t + 1, 0, (NS - 1) // 2)
            gate_up(t, 1)
            down(t - 1, 0)
            gate_up(t + 1, 0)
            down(t, 1)
            down(t + 1, 0)

            with pe.Fori(0, B) as b:
                for u in range(TPB):
                    q = u % TQ
                    pe.wait_ge(s_tx[u // 2], b * 64 + 64)
                    pe.wait_ge(s_o, b * TPB + (u + 1))
                    for kc in range(KC):
                        last = t_.matmul(psAtt[q], XC[u // 2][:, u % 2, kc, :], WE[:, ds(b, 1), kc, :],
                                         start=kc == 0, stop=kc == KC - 1)
                    last.then_inc(s_s, 1)


_INS = ['L0_attn_hidden_states', 'L0_attn_Wq', 'L0_attn_bq', 'L0_attn_Wqa', 'L0_attn_bqa', 'L0_attn_Wk', 'L0_attn_bk',
        'L0_attn_Wka', 'L0_attn_bka', 'L0_attn_Wt', 'L0_attn_bt', 'L0_ffn_router_w', 'L0_ffn_w1', 'L0_ffn_w3',
        'L0_ffn_w2']


def kernel(**inputs):
    import numpy as _np
    import concourse.bacc as _bacc
    from concourse import mybir as _mybir
    from concourse.bass_utils import run_bass_kernel_spmd as _run

    nc = _bacc.Bacc("TRN2", target_bir_lowering=False, num_devices=1)
    arrays, args = {}, []
    for name in _INS:
        a = _np.ascontiguousarray(inputs[name])
        arrays[f"in_{name}_dram"] = a
        args.append(nc.dram_tensor(f"in_{name}_dram", a.shape, _mybir.dt.from_np(a.dtype), kind="ExternalInput").ap())
    shape = inputs[_INS[0]].shape
    args.append(nc.dram_tensor("out_0_dram", shape, _mybir.dt.float32, kind="ExternalOutput").ap())
    recurrent_attention_moe(nc, *args)
    r = _run(nc, [arrays], core_ids=[0])
    return r.results[0]["out_0_dram"]
```
